# Optimizing a Trainium2 kernel written in Bass

```python
import numpy as np
import jax
import jax.numpy as jnp

def _softmax(x, axis=-1):
    return jax.nn.softmax(x, axis=axis)

def _gelu(x):
    return jax.nn.gelu(x, approximate=True)

def _silu(x):
    return jax.nn.silu(x)

def _sigmoid(x):
    return jax.nn.sigmoid(x)

def _layernorm(x, axis=-1, eps=1e-05):
    m = jnp.mean(x, axis=axis, keepdims=True)
    v = jnp.var(x, axis=axis, keepdims=True)
    return (x - m) / jnp.sqrt(v + eps)

def _scatter_add(tgt, idx, src, axis=0):
    return tgt.at[idx].add(src)

def _segment_sum(src, seg, n):
    return jax.ops.segment_sum(src, seg, n)
kernel_name = 'mk_prb_d1_jaxref_r8_f050e0'

def setup_inputs(seed: int=0):
    np.random.seed(seed)
    _w = jnp.asarray

    def _L0_attn_setup():
        import jax, jax.numpy as jnp
        import numpy as np
        NUM_HEADS = 16
        EPS = 1e-12

        def _l2norm(t):
            n = jnp.sqrt(jnp.sum(t * t, axis=-1, keepdims=True))
            return t / jnp.maximum(n, EPS)
        key = jax.random.key(seed)
        kx, kq, kk, kv = jax.random.split(key, 4)
        B, S, E = (2, 256, 128)
        head_dim = E // NUM_HEADS
        bound = 1.0 / np.sqrt(E)
        x = jax.random.normal(kx, (B, S, E), dtype=jnp.float32)
        Wq = jax.random.uniform(kq, (E, E), dtype=jnp.float32, minval=-bound, maxval=bound)
        Wk = jax.random.uniform(kk, (E, E), dtype=jnp.float32, minval=-bound, maxval=bound)
        Wv = jax.random.uniform(kv, (E, E), dtype=jnp.float32, minval=-bound, maxval=bound)
        g_scale = jnp.asarray(np.sqrt(head_dim), dtype=jnp.float32)
        return {'x': x, 'Wq': Wq, 'Wk': Wk, 'Wv': Wv, 'g_scale': g_scale}
    _L0_attn_in = _L0_attn_setup()

    def _L0_ffn_setup():
        import jax, jax.numpy as jnp
        import numpy as np
        DIM = 128
        N_HEADS = 16
        N_KV_HEADS = 4
        HEAD_DIM = DIM // N_HEADS
        N_REP = N_HEADS // N_KV_HEADS
        N_EXPERTS = 4
        TOP_K = 2
        HIDDEN = 3 * DIM
        EPS = 1.1920928955078125e-07

        def _rmsnorm(x, g):
            var = jnp.mean(jnp.square(x), axis=-1, keepdims=True)
            return x * jax.lax.rsqrt(var + EPS) * g

        def _rotate_half(x):
            x1, x2 = jnp.split(x, 2, axis=-1)
            return jnp.concatenate([-x2, x1], axis=-1)

        def _rope_tables(S):
            inv_freq = 1.0 / 10000.0 ** (jnp.arange(0, HEAD_DIM, 2, dtype=jnp.float32) / HEAD_DIM)
            freqs = jnp.arange(S, dtype=jnp.float32)[:, None] * inv_freq[None, :]
            emb = jnp.concatenate([freqs, freqs], axis=-1)
            return (jnp.cos(emb), jnp.sin(emb))

        def _attention(x, wq, wk, wv, wo):
            B, S, D = x.shape
            q = (x @ wq).reshape(B, S, N_HEADS, HEAD_DIM).transpose(0, 2, 1, 3)
            k = (x @ wk).reshape(B, S, N_KV_HEADS, HEAD_DIM).transpose(0, 2, 1, 3)
            v = (x @ wv).reshape(B, S, N_KV_HEADS, HEAD_DIM).transpose(0, 2, 1, 3)
            cos, sin = _rope_tables(S)
            q = q * cos + _rotate_half(q) * sin
            k = k * cos + _rotate_half(k) * sin
            k = jnp.repeat(k, N_REP, axis=1)
            v = jnp.repeat(v, N_REP, axis=1)
            scores = jnp.einsum('bhqd,bhkd->bhqk', q, k) / jnp.sqrt(jnp.float32(HEAD_DIM))
            causal = jnp.tril(jnp.ones((S, S), dtype=bool))
            scores = jnp.where(causal, scores, -jnp.inf)
            attn = jax.nn.softmax(scores, axis=-1)
            out = jnp.einsum('bhqk,bhkd->bhqd', attn, v)
            return out.transpose(0, 2, 1, 3).reshape(B, S, D) @ wo

        def _moe(x, gate, w1, w2, w3):
            B, S, D = x.shape
            xf = x.reshape(-1, D)
            probs = jax.nn.softmax(xf @ gate, axis=-1)
            w, idx = jax.lax.top_k(probs, TOP_K)
            w = w / jnp.sum(w, axis=-1, keepdims=True)
            oh = jax.nn.one_hot(idx, N_EXPERTS, dtype=xf.dtype)
            comb = jnp.einsum('nk,nke->ne', w, oh)
            out = jnp.zeros_like(xf)
            for e in range(N_EXPERTS):
                h = jax.nn.silu(xf @ w1[e]) * (xf @ w3[e])
                out = out + comb[:, e:e + 1] * (h @ w2[e])
            return out.reshape(B, S, D)
        key = jax.random.key(seed)
        ks = jax.random.split(key, 12)
        s = 0.02
        B, S = (2, 256)
        return {'x': jax.random.normal(ks[0], (B, S, DIM), jnp.float32), 'g1': jnp.ones((DIM,), jnp.float32), 'g2': jnp.ones((DIM,), jnp.float32), 'wq': jax.random.normal(ks[1], (DIM, N_HEADS * HEAD_DIM), jnp.float32) * s, 'wk': jax.random.normal(ks[2], (DIM, N_KV_HEADS * HEAD_DIM), jnp.float32) * s, 'wv': jax.random.normal(ks[3], (DIM, N_KV_HEADS * HEAD_DIM), jnp.float32) * s, 'wo': jax.random.normal(ks[4], (N_HEADS * HEAD_DIM, DIM), jnp.float32) * s, 'gate': jax.random.normal(ks[5], (DIM, N_EXPERTS), jnp.float32) * s, 'w1': jax.random.normal(ks[6], (N_EXPERTS, DIM, HIDDEN), jnp.float32) * s, 'w2': jax.random.normal(ks[7], (N_EXPERTS, HIDDEN, DIM), jnp.float32) * s, 'w3': jax.random.normal(ks[8], (N_EXPERTS, DIM, HIDDEN), jnp.float32) * s}
    _L0_ffn_in = _L0_ffn_setup()
    _d = {'L0_attn_x': _L0_attn_in['x'], 'L0_attn_Wq': _L0_attn_in['Wq'], 'L0_attn_Wk': _L0_attn_in['Wk'], 'L0_attn_Wv': _L0_attn_in['Wv'], 'L0_attn_g_scale': _L0_attn_in['g_scale'], 'L0_ffn_g1': _L0_ffn_in['g1'], 'L0_ffn_g2': _L0_ffn_in['g2'], 'L0_ffn_wq': _L0_ffn_in['wq'], 'L0_ffn_wk': _L0_ffn_in['wk'], 'L0_ffn_wv': _L0_ffn_in['wv'], 'L0_ffn_wo': _L0_ffn_in['wo'], 'L0_ffn_gate': _L0_ffn_in['gate'], 'L0_ffn_w1': _L0_ffn_in['w1'], 'L0_ffn_w2': _L0_ffn_in['w2'], 'L0_ffn_w3': _L0_ffn_in['w3']}
    _x0 = _d['L0_attn_x']
    _d['L0_attn_x'] = jax.random.normal(jax.random.fold_in(jax.random.key(seed), 1), (2, 1024, 128), dtype=_x0.dtype)
    del _x0
    return _d

def reference(L0_attn_x, L0_attn_Wq, L0_attn_Wk, L0_attn_Wv, L0_attn_g_scale, L0_ffn_g1, L0_ffn_g2, L0_ffn_wq, L0_ffn_wk, L0_ffn_wv, L0_ffn_wo, L0_ffn_gate, L0_ffn_w1, L0_ffn_w2, L0_ffn_w3):

    def _L0_attn_ref(x, Wq, Wk, Wv, g_scale):
        import jax, jax.numpy as jnp
        import numpy as np
        NUM_HEADS = 16
        EPS = 1e-12

        def _l2norm(t):
            n = jnp.sqrt(jnp.sum(t * t, axis=-1, keepdims=True))
            return t / jnp.maximum(n, EPS)
        B, S, E = x.shape
        H = NUM_HEADS
        D = E // H
        q = (x @ Wq.T).reshape(B, S, H, D).transpose(0, 2, 1, 3)
        k = (x @ Wk.T).reshape(B, S, H, D).transpose(0, 2, 1, 3)
        v = (x @ Wv.T).reshape(B, S, H, D).transpose(0, 2, 1, 3)
        q = _l2norm(q)
        k = _l2norm(k)
        scores = g_scale * jnp.einsum('bhqd,bhkd->bhqk', q, k)
        attn = jax.nn.softmax(scores, axis=-1)
        out = jnp.einsum('bhqk,bhkd->bhqd', attn, v)
        out = out.transpose(0, 2, 1, 3).reshape(B, S, E)
        return out

    def _L0_ffn_ref(x, g1, g2, wq, wk, wv, wo, gate, w1, w2, w3):
        import jax, jax.numpy as jnp
        import numpy as np
        DIM = 128
        N_HEADS = 16
        N_KV_HEADS = 4
        HEAD_DIM = DIM // N_HEADS
        N_REP = N_HEADS // N_KV_HEADS
        N_EXPERTS = 4
        TOP_K = 2
        HIDDEN = 3 * DIM
        EPS = 1.1920928955078125e-07

        def _rmsnorm(x, g):
            var = jnp.mean(jnp.square(x), axis=-1, keepdims=True)
            return x * jax.lax.rsqrt(var + EPS) * g

        def _rotate_half(x):
            x1, x2 = jnp.split(x, 2, axis=-1)
            return jnp.concatenate([-x2, x1], axis=-1)

        def _rope_tables(S):
            inv_freq = 1.0 / 10000.0 ** (jnp.arange(0, HEAD_DIM, 2, dtype=jnp.float32) / HEAD_DIM)
            freqs = jnp.arange(S, dtype=jnp.float32)[:, None] * inv_freq[None, :]
            emb = jnp.concatenate([freqs, freqs], axis=-1)
            return (jnp.cos(emb), jnp.sin(emb))

        def _attention(x, wq, wk, wv, wo):
            B, S, D = x.shape
            q = (x @ wq).reshape(B, S, N_HEADS, HEAD_DIM).transpose(0, 2, 1, 3)
            k = (x @ wk).reshape(B, S, N_KV_HEADS, HEAD_DIM).transpose(0, 2, 1, 3)
            v = (x @ wv).reshape(B, S, N_KV_HEADS, HEAD_DIM).transpose(0, 2, 1, 3)
            cos, sin = _rope_tables(S)
            q = q * cos + _rotate_half(q) * sin
            k = k * cos + _rotate_half(k) * sin
            k = jnp.repeat(k, N_REP, axis=1)
            v = jnp.repeat(v, N_REP, axis=1)
            scores = jnp.einsum('bhqd,bhkd->bhqk', q, k) / jnp.sqrt(jnp.float32(HEAD_DIM))
            causal = jnp.tril(jnp.ones((S, S), dtype=bool))
            scores = jnp.where(causal, scores, -jnp.inf)
            attn = jax.nn.softmax(scores, axis=-1)
            out = jnp.einsum('bhqk,bhkd->bhqd', attn, v)
            return out.transpose(0, 2, 1, 3).reshape(B, S, D) @ wo

        def _moe(x, gate, w1, w2, w3):
            B, S, D = x.shape
            xf = x.reshape(-1, D)
            probs = jax.nn.softmax(xf @ gate, axis=-1)
            w, idx = jax.lax.top_k(probs, TOP_K)
            w = w / jnp.sum(w, axis=-1, keepdims=True)
            oh = jax.nn.one_hot(idx, N_EXPERTS, dtype=xf.dtype)
            comb = jnp.einsum('nk,nke->ne', w, oh)
            out = jnp.zeros_like(xf)
            for e in range(N_EXPERTS):
                h = jax.nn.silu(xf @ w1[e]) * (xf @ w3[e])
                out = out + comb[:, e:e + 1] * (h @ w2[e])
            return out.reshape(B, S, D)
        x = x + _attention(_rmsnorm(x, g1), wq, wk, wv, wo)
        x = x + _moe(_rmsnorm(x, g2), gate, w1, w2, w3)
        return x
    x = L0_attn_x
    xn = _layernorm(x, axis=-1)
    x = x + _L0_attn_ref(xn, L0_attn_Wq, L0_attn_Wk, L0_attn_Wv, L0_attn_g_scale) + _L0_ffn_ref(xn, L0_ffn_g1, L0_ffn_g2, L0_ffn_wq, L0_ffn_wk, L0_ffn_wv, L0_ffn_wo, L0_ffn_gate, L0_ffn_w1, L0_ffn_w2, L0_ffn_w3)
    return x

_drawn_inputs = setup_inputs


def setup_inputs(seed=0):
    import zlib

    import numpy as np

    out = dict(_drawn_inputs(seed))
    spreads = {'L0_ffn_g1': (1.0, 0.6), 'L0_ffn_g2': (1.0, 0.6)}
    factors = {'L0_ffn_wq': 8.0,
     'L0_ffn_wk': 8.0,
     'L0_ffn_wv': 8.0,
     'L0_ffn_wo': 8.0,
     'L0_ffn_gate': 8.0,
     'L0_ffn_w1': 8.0,
     'L0_ffn_w2': 8.0,
     'L0_ffn_w3': 8.0,
     'L0_attn_Wq': 8.0,
     'L0_attn_Wk': 8.0,
     'L0_attn_Wv': 8.0}
    for name, (base, spread) in spreads.items():
        noise = np.random.default_rng([zlib.crc32(name.encode()), seed]).standard_normal(out[name].shape)
        drawn = base * np.exp(spread * noise) if base else spread * noise
        out[name] = jnp.asarray(drawn.astype(out[name].dtype))
    for name, factor in factors.items():
        out[name] = (out[name] * factor).astype(out[name].dtype)
    return out
```

```python
from contextlib import ExitStack

import concourse.bass as bass
from concourse import mybir

F32 = mybir.dt.float32
BF16 = mybir.dt.bfloat16
ALU = mybir.AluOpType
ACT = mybir.ActivationFunctionType
AX = mybir.AxisListType
ds = bass.ds

P = 128
BATCH, SEQ, DIM = 2, 1024, 128
TILES = BATCH * SEQ // P
SEQ_TILES = SEQ // P
CT = 4
CHUNKS = TILES // CT
CHUNK = CT * P
HEADS, KV_HEADS, HD = 16, 4, 8
GROUP = 4
GROUPS = HEADS // GROUP
ITERS = BATCH * GROUPS
PARTS = 4
HEAD_COLS = PARTS * HD
WINDOW = 3 * HD
TERMS = 3 * WINDOW
BIAS_ROW = 96
Q_WINDOWS, K_WINDOWS = (0, 0, HD), (0, HD, 0)
QK_HEADS = 2 * HEADS
ROPE_HEADS = HEADS + KV_HEADS
QK_COLS, ROPE_COLS, V_COLS = 2 * DIM, ROPE_HEADS * HD, DIM + KV_HEADS * HD
EXPERTS, HIDDEN = 4, 384
HT = HIDDEN // P
LN_EPS, RMS_EPS, NORM_EPS = 1e-5, 1.1920928955078125e-07, 1e-12
MASKED = -1e30
BIG = 3e38
BANK = 512
SLOT = 2 * BANK

COS_STEPS = [(j, h, 1) for j in range(SEQ_TILES) for h in range(GROUP)]
CAUSAL_STEPS = ([(j, h, 1) for j in range(4) for h in range(GROUP)]
                + [(j, h, 2) for j in (4, 5) for h in (0, 2)] + [(6, 0, 4), (7, 0, 4)])
STEPS = len(COS_STEPS) + len(CAUSAL_STEPS)

MAX_PIECES = [(t, p) for t in range(SEQ_TILES) for p in range(1 + t // 4)]
COS_JOBS = ([("out_causal", 0, 0), ("out_causal", 1, 0)]
            + [("max", h, n) for h in (0, 1) for n in range(len(MAX_PIECES))] + [("neg_max", 0, 0)]
            + [("max", h, n) for h in (2, 3) for n in range(len(MAX_PIECES))] + [("neg_max", 1, 0)])
CAUSAL_JOBS = [("cos", 0, 0), ("cos", 1, 0), ("out_cos", 0, 0), ("out_cos", 1, 0), ("key", 0, 0), ("query", 0, 0)]
MAX_STEPS = 26
COS_ISSUED = ([0, 0, 0, 1, 2] + [2 + -(-(len(COS_JOBS) - 3) * (i + 1) // MAX_STEPS) for i in range(MAX_STEPS)]
              + [len(COS_JOBS)])
CAUSAL_ISSUED = [1, 2, 2, 2, 2, 2, 3, 4, 5] + [6] * (len(CAUSAL_STEPS) - 9)
JOBS = len(COS_JOBS) + len(CAUSAL_JOBS)
FIRST_JOBS = 4
assert STEPS % 2 == 0 and JOBS % 2 == 0 and FIRST_JOBS % 2 == 0

TILE_CREDIT = 2 * SEQ_TILES
RES_CREDIT = 3
LAID = {"q_cos": 48 * GROUP, "k_cos": 48 * GROUP, "query0": 96, "query1": 96, "key": 48, "neg_max0": 16, "neg_max1": 16}


def build(nc, x, wq_cos, wk_cos, wv_cos, g_scale, g1, g2, wq, wk, wv, wo, gate, w1, w2, w3,
          cos_table, sin_table, out):
    ctx = ExitStack()
    with ctx:
        def sb(name, shape, dt=F32):
            return ctx.enter_context(nc.sbuf_tensor(name, shape, dt))

        def sem(name):
            return ctx.enter_context(nc.semaphore(name))

        x_tok = sb("x_tok", [P, TILES * DIM])
        xn = sb("xn", [P, TILES * DIM])
        w_qk = sb("w_qk", [P, QK_COLS + ROPE_COLS])
        w_v = sb("w_v", [P, V_COLS])
        w_o = sb("w_o", [P, DIM])
        w_gate = sb("w_gate", [P, EXPERTS])
        w_1 = sb("w_1", [P, EXPERTS, HIDDEN])
        w_3 = sb("w_3", [P, EXPERTS, HIDDEN])
        w_2 = sb("w_2", [P, EXPERTS * HT, DIM])
        g1_col, g2_col, g_col = sb("g1_col", [P, 1]), sb("g2_col", [P, 1]), sb("g_col", [P, 1])
        cos_t = sb("cos_t", [P, SEQ_TILES * HD])
        sin_t = sb("sin_t", [P, SEQ_TILES * HD])
        ident = sb("ident", [P, P])
        ident_b = sb("ident_b", [P, P], BF16)
        mask_q = sb("mask_q", [P, P], BF16)
        mask_k = sb("mask_k", [P, P], BF16)
        stat = sb("stat", [P, TILES, 6])
        s_mean, s_diff, s_var = sb("s_mean", [P, TILES]), sb("s_diff", [P, TILES]), sb("s_var", [P, TILES])
        roots = sb("roots", [P, 2, TILES])
        scales = sb("scales", [P, 2, TILES])
        parts_cos = sb("parts_cos", [P, TILES * QK_HEADS * HEAD_COLS], BF16)
        parts_rope = sb("parts_rope", [P, TILES * ROPE_HEADS * HEAD_COLS + P - HEAD_COLS], BF16)
        v_cos = sb("v_cos", [P, TILES * DIM])
        v_causal = sb("v_causal", [P, TILES * KV_HEADS * HD])
        q_cos_t = sb("q_cos_t", [P, GROUP, SEQ], BF16)
        k_cos_t = sb("k_cos_t", [P, GROUP, SEQ], BF16)
        q_causal_t = sb("q_causal_t", [P, GROUP, SEQ], BF16)
        k_causal_t = sb("k_causal_t", [P, SEQ], BF16)
        parts_t = {n: sb(f"parts_t_{n}", [P, SEQ], BF16) for n in ("q_cos", "k_cos", "query", "key")}
        neg_max_t = sb("neg_max_t", [2 * SEQ_TILES, 2, P], BF16)
        v_cos_pad = sb("v_cos_pad", [P, SEQ_TILES, GROUP, 32])
        v_causal_pad = sb("v_causal_pad", [P, SEQ_TILES, 32])
        neg_piece = sb("neg_piece", [P, GROUP, SEQ_TILES, 2])
        neg_max = sb("neg_max", [P, GROUP, SEQ_TILES], BF16)
        out_t = sb("out_t", [P, 2, SEQ])
        recip = sb("recip", [P, 2, CT, GROUP])
        att_cos = sb("att_cos", [P, ITERS * SEQ_TILES * 32])
        att_causal = sb("att_causal", [P, (ITERS + 1) * SEQ_TILES * 32])
        probs = sb("probs", [P, 2, GROUP, SEQ])

        room = probs[:, :, :, :].rearrange("p a h s -> p (a h s)")

        def part(start, size):
            return room[:, start:start + size]

        xn_stage = part(0, CHUNK)
        xn_t = part(512, CHUNK)
        squares = part(1024, CT * QK_COLS)
        unit = part(2048, CT * QK_COLS)
        rope_in = part(3072, CT * ROPE_COLS)
        rope_a = part(3712, CT * ROPE_COLS)
        rope_b = part(4352, CT * ROPE_COLS)
        norms = part(4992, CT * QK_HEADS)
        inv_norms = part(5120, CT * QK_HEADS)
        xf_t = part(0, TILES * P)
        hidden = [part(2048 + 1536 * i, HT * CHUNK).rearrange("p (h n) -> p h n", h=HT) for i in range(2)]
        gated = [part(5120 + 512 * i, CHUNK) for i in range(2)]
        att_stage = part(6144, CHUNK)
        att_stage_t = part(6656, CHUNK)
        f_stage = part(7168, CHUNK)
        f_stage_t = part(7680, CHUNK)
        sum_sq = s_mean
        logits = sb("logits", [P, TILES, EXPERTS])
        g_exp, g_rank = sb("g_exp", [P, TILES, EXPERTS]), sb("g_rank", [P, TILES, EXPERTS])
        g_cmp = sb("g_cmp", [P, 6, TILES])
        comb = sb("comb", [P, TILES * EXPERTS])

        ps = ctx.enter_context(nc.psum_tensor("ps", [P, 8, BANK], F32))
        acc = ps[:, 4:6, :]
        aux = [ps[:, 6 + i, :] for i in range(2)]
        aux_b = [a.bitcast(BF16) for a in aux]

        def slot(n):
            return ps[:, 2 * (n % 2):2 * (n % 2) + 2, :].rearrange("p b n -> p (b n)")

        s_x = [sem(f"x_landed{i}") for i in range(CHUNKS)]
        s_wqkv, s_small, s_w_rest, s_rope_t = sem("wqkv_landed"), sem("small_landed"), sem("rest_landed"), sem("tables_landed")
        s_const, s_clear, s_rows = sem("constants_made"), sem("buffers_cleared"), sem("rows_cleared")
        s_wscaled = sem("weights_scaled")
        s_dve0, s_stats, s_root0 = sem("dve_steps_stats"), sem("stats_made"), sem("roots_made")
        s_xn, s_xn_saved = sem("xn_staged"), sem("xn_saved")
        s_xt_ps, s_xt, s_proj = sem("xt_in_psum"), sem("xt_ready"), sem("projected")
        s_sq, s_vc, s_nsq, s_nroot = sem("squares_ready"), sem("v_copied"), sem("norm_squares_ready"), sem("norms_ready")
        s_dve1, s_rin, s_rope = sem("dve_steps_proj"), sem("rope_input_ready"), sem("rope_steps")
        s_again = sem("high_parts_again")
        s_hi, s_mid, s_res, s_lo = sem("high_parts"), sem("middle_parts"), sem("residues"), sem("low_parts")
        s_sc, s_pr = sem("scores_ready"), sem("probs_ready")
        s_pv, s_accfree = sem("key_tiles_used"), sem("acc_copied")
        s_fill, s_free = sem("aux_filled"), sem("aux_read")
        s_negmax, s_norm = sem("neg_max_ready"), sem("recips_ready")
        s_laid = {n: sem(f"laid_{n}") for n in LAID}
        s_va, s_vb = sem("v_cos_padded"), sem("v_causal_padded")
        s_f1 = {n: sem("f1_" + n) for n in ("staged", "t_ps", "t", "wo", "x1", "sq", "ssq", "sum", "y")}
        s_f2 = {n: sem("f2_" + n) for n in ("ms", "root", "r2", "xs", "t_ps", "t_stage", "t", "gate", "logits", "dve", "exp", "comb")}
        s_f3 = {n: sem("f3_" + n) for n in ("up", "silu", "h", "y", "y_used", "stored")}

        block = ctx.enter_context(nc.Block())

        def step_view(n, j, heads, causal):
            s = slot(n)
            if not causal or j < 4:
                return s[:, (j * P if causal else 0):SEQ].unsqueeze(1)
            width = SEQ - j * P
            if heads == 2:
                return s.rearrange("p (h n) -> p h n", h=2)[:, :, 0:width]
            return s[:, 0:heads * width].rearrange("p (h n) -> p h n", h=heads)

        @block.sync
        def _(sp):
            for c in range(CHUNKS):
                b, t0 = divmod(c * CT, SEQ_TILES)
                src = x[b, t0 * P:(t0 + CT) * P, :].rearrange("(t p) d -> p t d", p=P)
                dst = x_tok[:, c * CHUNK:(c + 1) * CHUNK].rearrange("p (t d) -> p t d", t=CT)
                sp.dma_start(dst, src).then_inc(s_x[c], 16)
            sp.dma_start(w_1[:, :, :], w1.rearrange("e i h -> i e h")).then_inc(s_w_rest, 16)
            sp.dma_start(w_3[:, :, :], w3.rearrange("e i h -> i e h")).then_inc(s_w_rest, 16)
            sp.dma_start(w_2[:, :, :], w2.rearrange("e (h i) d -> i (e h) d", i=P)).then_inc(s_w_rest, 16)
            sp.dma_start(w_o[:, :], wo).then_inc(s_w_rest, 16)
            sp.dma_start(w_gate[:, :], gate).then_inc(s_w_rest, 16)

            def lay_out(signal, src, dst, windows, heads):
                for h in heads:
                    for w, row in enumerate(windows):
                        sp.dma_start(dst[w * WINDOW:(w + 1) * WINDOW, h, :],
                                     parts_t[src][h * HEAD_COLS + row:h * HEAD_COLS + row + WINDOW, :])\
                          .then_inc(s_laid[signal], 16)

            def lay_out_cos(base):
                sp.wait_ge(s_free, base + 3)
                lay_out("q_cos", "q_cos", q_cos_t, Q_WINDOWS, range(GROUP))
                sp.wait_ge(s_free, base + 4)
                lay_out("k_cos", "k_cos", k_cos_t, K_WINDOWS, range(GROUP))

            sp.wait_ge(s_rows, 4)
            lay_out_cos(0)
            with sp.Fori(0, ITERS) as it:
                base = it * JOBS + FIRST_JOBS
                sp.wait_ge(s_free, base + 2)
                sp.wait_ge(s_sc, it * STEPS + 1)
                lay_out("key", "key", k_causal_t[:, :].unsqueeze(1), K_WINDOWS, range(1))
                lay_out("query0", "query", q_causal_t, Q_WINDOWS, (0, 1))
                lay_out("query1", "query", q_causal_t, Q_WINDOWS, (2, 3))
                for a in range(2):
                    sp.wait_ge(s_free, base + (COS_JOBS.index(("neg_max", a, 0)) + 3))
                    sp.dma_start(q_causal_t[BIAS_ROW:BIAS_ROW + 1, 2 * a:2 * a + 2, :], neg_max_t[:, a, :])\
                      .then_inc(s_laid[f"neg_max{a}"], 16)
                lay_out_cos(base + len(COS_JOBS))
            for name in ("q_cos", "k_cos"):
                sp.wait_ge(s_laid[name], (ITERS + 2) * LAID[name])

            for c in range(CHUNKS):
                b, t0 = divmod(c * CT, SEQ_TILES)
                dst = out[b, t0 * P:(t0 + CT) * P, :].rearrange("(t p) d -> p t d", p=P)
                sp.wait_ge(s_f3["y_used"], (c + 1) * EXPERTS + 2)
                sp.dma_start(dst, x_tok[:, c * CHUNK:(c + 1) * CHUNK].rearrange("p (t d) -> p t d", t=CT))\
                  .then_inc(s_f3["stored"], 16)
            sp.wait_ge(s_f3["stored"], 16 * CHUNKS)

        @block.gpsimd
        def _(pool):
            pool.memset(ident[:, :], 0.0).then_inc(s_const, 1)
            pool.memset(ident_b[:, :], 0.0).then_inc(s_const, 1)
            pool.memset(mask_q[:, :], 0.0).then_inc(s_const, 1)
            pool.memset(mask_k[:, :], 0.0).then_inc(s_const, 1)
            pool.wait_ge(s_const, 4)
            for m in (ident, ident_b):
                pool.affine_select(out=m[:, :], in_=m[:, :], compare_op=ALU.not_equal, fill=1.0,
                                   base=0, pattern=[[-1, P]], channel_multiplier=1).then_inc(s_const, 1)
            pool.affine_select(out=mask_q[:, :], in_=mask_q[:, :], compare_op=ALU.is_ge, fill=MASKED,
                               base=0, pattern=[[-1, P]], channel_multiplier=1).then_inc(s_const, 1)
            pool.affine_select(out=mask_k[:, :], in_=mask_k[:, :], compare_op=ALU.is_ge, fill=MASKED,
                               base=0, pattern=[[1, P]], channel_multiplier=-1).then_inc(s_const, 1)
            pool.memset(v_cos_pad[:, :, :, HD:], 0.0).then_inc(s_clear, 1)
            pool.memset(v_causal_pad[:, :, HD:], 0.0).then_inc(s_clear, 1)
            pool.memset(neg_piece[:, :, :, :], BIG).then_inc(s_clear, 1)
            pool.memset(out_t[:, 1, :], 1.0).then_inc(s_clear, 1)
            pool.wait_ge(s_clear, 6)
            pool.memset(v_cos_pad[:, :, :, HD:HD + 1], 1.0).then_inc(s_clear, 1)
            pool.memset(v_causal_pad[:, :, HD:HD + 1], 1.0).then_inc(s_clear, 1)
            pool.wait_ge(s_rope_t, 32)

            with pool.Fori(0, CHUNKS) as c:
                pool.wait_ge(s_xn, CT * c + CT)
                pool.tensor_copy(xn[:, ds(c * CHUNK, CHUNK)], xn_stage).then_inc(s_xn_saved, 1)
                pool.wait_ge(s_rin, c + 1)
                pool.wait_ge(s_lo, 2 * c + 1)
                heads = CT * ROPE_HEADS
                table = ds((c % 2) * CT * HD, CT * HD)
                cos_c = cos_t[:, table].rearrange("p (t d) -> p t d", t=CT)
                sin_c = sin_t[:, table].rearrange("p (t d) -> p t d", t=CT)
                r_in = rope_in.rearrange("p (t h d) -> p t h d", t=CT, d=HD)
                r_a = rope_a.rearrange("p (t h d) -> p t h d", t=CT, d=HD)
                r_b = rope_b.rearrange("p (t h d) -> p t h d", t=CT, d=HD)
                half = HD // 2
                pool.tensor_tensor(r_a, r_in, cos_c.unsqueeze(2).to_broadcast([P, CT, ROPE_HEADS, HD]),
                                   ALU.mult).then_inc(s_rope, 1)
                for to, of in ((0, half), (half, 0)):
                    pool.tensor_tensor(r_b[:, :, :, to:to + half], r_in[:, :, :, of:of + half],
                                       sin_c[:, :, to:to + half].unsqueeze(2)
                                       .to_broadcast([P, CT, ROPE_HEADS, half]), ALU.mult).then_inc(s_rope, 1)
                pool.wait_ge(s_rope, 4 * c + 3)
                pool.tensor_tensor(rope_a, rope_a, rope_b, ALU.add).then_inc(s_rope, 1)
                for n, (flat, count) in enumerate(((parts_cos, CT * QK_HEADS), (parts_rope, CT * ROPE_HEADS))):
                    pool.wait_ge(s_hi, 2 * c + (n + 1))
                    words = flat[:, ds(c * (count * HEAD_COLS), count * HEAD_COLS)].bitcast(F32)\
                        .rearrange("p (h w) -> p h w", w=HEAD_COLS // 2)
                    pool.tensor_copy(words[:, :, 3 * HD // 2:], words[:, :, 0:HD // 2]).then_inc(s_again, 1)

            with pool.Fori(0, ITERS) as it:
                b, g = it // GROUPS, it % GROUPS
                pool.wait_ge(s_pv, it * (2 * SEQ_TILES) + (TILE_CREDIT - SEQ_TILES))
                src = v_cos[:, ds(b * (SEQ_TILES * DIM) + g * (GROUP * HD), SEQ_TILES * DIM - (GROUPS - 1) * GROUP * HD)]
                for t in range(SEQ_TILES):
                    one = src[:, t * DIM:t * DIM + GROUP * HD].rearrange("p (h d) -> p h d", h=GROUP)
                    ins = pool.tensor_copy(v_cos_pad[:, t, :, 0:HD], one)
                ins.then_inc(s_va, 1)
                pool.wait_ge(s_pv, it * (2 * SEQ_TILES) + TILE_CREDIT)
                width = KV_HEADS * HD
                src = v_causal[:, ds(b * (SEQ_TILES * width) + g * HD, SEQ_TILES * width - (KV_HEADS - 1) * HD)]
                for t in range(SEQ_TILES):
                    ins = pool.tensor_copy(v_causal_pad[:, t, 0:HD], src[:, t * width:t * width + HD])
                ins.then_inc(s_vb, 1)

            pool.wait_ge(s_free, 2 + FIRST_JOBS + ITERS * JOBS + 2)
            with pool.Fori(0, CHUNKS) as c:
                b, t0 = c // 2, (c % 2) * CT
                pool.wait_ge(s_f1["t_ps"], c + 1)
                stage = att_stage.rearrange("p (t g d) -> p t g d", t=CT, g=GROUPS)
                cols = SEQ_TILES * 32
                for g in range(GROUPS):
                    src = att_causal[:, ds((b * GROUPS + (g + 1)) * cols + t0 * 32, CT * 32)]
                    ins = pool.tensor_copy(stage[:, :, g, :], src.rearrange("p (t d) -> p t d", t=CT))
                ins.then_inc(s_f1["staged"], 1)
                x_c = x_tok[:, ds(c * CHUNK, CHUNK)].rearrange("p (t g d) -> p t g d", t=CT, g=GROUPS)
                for g in range(GROUPS):
                    src = att_cos[:, ds((b * GROUPS + g) * cols + t0 * 32, CT * 32)]
                    ins = pool.tensor_tensor(x_c[:, :, g, :], x_c[:, :, g, :],
                                             src.rearrange("p (t d) -> p t d", t=CT), ALU.add)
                ins.then_inc(s_f1["sum"], 1)

        @block.scalar
        def _(act):
            for n, (dst, src) in enumerate((
                    (w_qk[:, 0:128], wq_cos), (w_qk[:, 128:256], wk_cos), (w_qk[:, 256:384], wq),
                    (w_qk[:, 384:416], wk), (w_v[:, 0:128], wv_cos), (w_v[:, 128:160], wv))):
                act.dma_start(dst, src).then_inc(s_wqkv, 16)
            act.dma_start(g1_col[:, :], g1).then_inc(s_small, 16)
            act.dma_start(g2_col[:, :], g2).then_inc(s_small, 16)
            act.dma_start(g_col[:, :], g_scale).then_inc(s_small, 16)
            act.dma_start(cos_t[:, :], cos_table).then_inc(s_rope_t, 16)
            act.dma_start(sin_t[:, :], sin_table).then_inc(s_rope_t, 16)
            act.wait_ge(s_stats, 1)
            act.activation(roots[:, :, :], roots[:, :, :], ACT.Sqrt).then_inc(s_root0, 1)

            with act.Fori(0, CHUNKS) as c:
                act.wait_ge(s_xt_ps, c + 1)
                act.wait_ge(s_proj, c + 1)
                act.activation(xn_t, ps[:, 6, :], ACT.Copy).then_inc(s_xt, 1)
                act.wait_ge(s_proj, c + 2)
                act.wait_ge(s_nsq, c + 1)
                act.activation(squares.rearrange("p (t n) -> p t n", t=CT), ps[:, 0:CT, 0:QK_COLS],
                               ACT.Square).then_inc(s_sq, 1)
                v_ps = ps[:, 4:6, 0:2 * V_COLS].rearrange("p b (t n) -> p b t n", t=2)
                act.activation(v_cos[:, ds(c * CHUNK, CHUNK)].rearrange("p (b t n) -> p b t n", b=2, t=2),
                               v_ps[:, :, :, 0:DIM], ACT.Copy).then_inc(s_vc, 1)
                act.wait_ge(s_nsq, c + 2)
                act.activation(norms, norms, ACT.Sqrt).then_inc(s_nroot, 1)
                a_parts = parts_cos[:, ds(c * (CT * QK_HEADS * HEAD_COLS), CT * QK_HEADS * HEAD_COLS)]\
                    .rearrange("p (h s d) -> p h s d", s=PARTS, d=HD)
                r_parts = parts_rope[:, ds(c * (CT * ROPE_HEADS * HEAD_COLS), CT * ROPE_HEADS * HEAD_COLS)]\
                    .rearrange("p (h s d) -> p h s d", s=PARTS, d=HD)
                unit_h = unit.rearrange("p (h d) -> p h d", d=HD)
                rope_h = rope_a.rearrange("p (h d) -> p h d", d=HD)
                act.wait_ge(s_res, 3 * c + (RES_CREDIT + 1))
                act.activation(a_parts[:, :, 0, :], unit_h, ACT.Copy).then_inc(s_hi, 1)
                act.wait_ge(s_rope, 4 * c + 4)
                act.activation(r_parts[:, :, 0, :], rope_h, ACT.Copy).then_inc(s_hi, 1)
                act.wait_ge(s_res, 3 * c + (RES_CREDIT + 2))
                act.activation(a_parts[:, :, 1, :], unit_h, ACT.Copy).then_inc(s_mid, 1)
                act.wait_ge(s_res, 3 * c + (RES_CREDIT + 3))
                act.activation(r_parts[:, :, 1, :], rope_h, ACT.Copy).then_inc(s_mid, 1)

            with act.Fori(0, ITERS) as it:
                for n, (j, h, heads) in enumerate(COS_STEPS + CAUSAL_STEPS):
                    causal = n >= len(COS_STEPS)
                    tile = j + SEQ_TILES * causal
                    if h == 0:
                        act.wait_ge(s_pv, it * (2 * SEQ_TILES) + (tile - 1 + TILE_CREDIT))
                    act.wait_ge(s_sc, it * STEPS + (n + 2))
                    first = j * P if causal else 0
                    act.activation(probs[:, j % 2, h:h + heads, first:SEQ], step_view(n, j, heads, causal),
                                   ACT.Exp).then_inc(s_pr, 1)

            with act.Fori(0, CHUNKS) as c:
                act.wait_ge(s_f1["t_ps"], c + 2)
                act.wait_ge(s_f1["wo"], c + 1)
                act.activation(att_stage_t, ps[:, 0, :], ACT.Copy).then_inc(s_f1["t"], 1)
                act.wait_ge(s_f1["x1"], c + 2)
                act.wait_ge(s_f1["ssq"], c + 1)
                act.activation(f_stage, xn[:, ds(c * CHUNK, CHUNK)], ACT.Square).then_inc(s_f1["sq"], 1)
            act.wait_ge(s_f2["ms"], 1)
            act.activation(sum_sq[:, :], sum_sq[:, :], ACT.Sqrt).then_inc(s_f2["root"], 1)
            with act.Fori(0, CHUNKS) as c:
                act.wait_ge(s_f2["t_ps"], c + 1)
                act.wait_ge(s_f2["gate"], c + 1)
                act.activation(f_stage_t, ps[:, 0, :], ACT.Copy, scale=g2_col[:, :]).then_inc(s_f2["t_stage"], 1)
                act.activation(xf_t[:, ds(c * CHUNK, CHUNK)], ps[:, 0, :], ACT.Copy,
                               scale=g2_col[:, :]).then_inc(s_f2["t"], 1)
            act.wait_ge(s_f2["dve"], 2)
            act.activation(g_exp[:, :, :], logits[:, :, :], ACT.Exp).then_inc(s_f2["exp"], 1)
            with act.Fori(0, CHUNKS) as c:
                for k in range(EXPERTS * HT):
                    act.wait_ge(s_f3["up"], c * (EXPERTS * HT) + (k + 1))
                    act.wait_ge(s_f3["h"], c * (EXPERTS * HT) + (k + 1))
                    act.activation(gated[k % 2], ps[:, k % 2, :], ACT.Silu).then_inc(s_f3["silu"], 1)

        @block.vector
        def _(dve):
            step0 = [0]

            def link(ins):
                step0[0] += 1
                ins.then_inc(s_dve0, 1)
                dve.wait_ge(s_dve0, step0[0])

            for s, n in ((s_proj, 1), (s_nsq, 1), (s_lo, 1), (s_res, RES_CREDIT), (s_sc, 1), (s_pr, 2), (s_pv, TILE_CREDIT),
                         (s_free, 2), (s_accfree, 1), (s_f1["t_ps"], 1), (s_f1["wo"], 1), (s_f1["x1"], 1),
                         (s_f1["ssq"], 1), (s_f2["gate"], 1), (s_f2["t"], 1), (s_f2["logits"], 1),
                         (s_f3["h"], 2), (s_f3["y"], 2), (s_f3["y_used"], 2)):
                dve.sem_inc(s, n)
            for name, n in LAID.items():
                dve.sem_inc(s_laid[name], n)

            for t in (q_cos_t, k_cos_t, q_causal_t):
                dve.memset(t[64:P, :, :], 0.0).then_inc(s_rows, 1)
            dve.memset(k_causal_t[64:P, :], 0.0).then_inc(s_rows, 1)
            dve.wait_ge(s_rows, 4)
            dve.memset(k_causal_t[BIAS_ROW:BIAS_ROW + 1, :], 1.0).then_inc(s_clear, 1)
            dve.memset(parts_rope[:, TILES * ROPE_HEADS * HEAD_COLS:], 0.0).then_inc(s_clear, 1)

            for t in range(TILES):
                dve.wait_ge(s_x[t // CT], 16)
                ins = dve.bn_stats(stat[:, t, :], x_tok[:, t * DIM:(t + 1) * DIM])
            link(ins)
            dve.tensor_tensor(s_mean[:, :], stat[:, :, 1], stat[:, :, 4], ALU.add).then_inc(s_dve0, 1)
            dve.tensor_tensor(s_diff[:, :], stat[:, :, 1], stat[:, :, 4], ALU.subtract).then_inc(s_dve0, 1)
            step0[0] += 2
            link(dve.tensor_tensor(s_var[:, :], stat[:, :, 2], stat[:, :, 5], ALU.add))
            link(dve.tensor_tensor(s_diff[:, :], s_diff[:, :], s_diff[:, :], ALU.mult))
            link(dve.scalar_tensor_tensor(out=s_var[:, :], in0=s_diff[:, :], scalar=DIM / 4.0, in1=s_var[:, :],
                                          op0=ALU.mult, op1=ALU.add))
            dve.tensor_scalar(s_mean[:, :], s_mean[:, :], 0.5, None, ALU.mult).then_inc(s_dve0, 1)
            step0[0] += 1
            link(dve.tensor_scalar(roots[:, 0, :], s_var[:, :], 1.0 / DIM, LN_EPS, ALU.mult, ALU.add))
            link(dve.reciprocal(roots[:, 1, :], roots[:, 0, :]))
            link(dve.tensor_tensor(roots[:, 1, :], roots[:, 1, :], s_var[:, :], ALU.mult))
            dve.tensor_scalar(roots[:, 1, :], roots[:, 1, :], 1.0 / DIM, RMS_EPS, ALU.mult, ALU.add).then_inc(s_stats, 1)
            dve.wait_ge(s_wqkv, 96)
            dve.wait_ge(s_small, 48)
            dve.tensor_scalar(w_qk[:, 256:384], w_qk[:, 256:384], g1_col[:, :], float(HD) ** -0.5,
                              ALU.mult, ALU.mult).then_inc(s_wscaled, 1)
            dve.tensor_scalar(w_qk[:, 384:416], w_qk[:, 384:416], g1_col[:, :], None, ALU.mult).then_inc(s_wscaled, 1)
            dve.tensor_scalar(w_v[:, DIM:V_COLS], w_v[:, DIM:V_COLS], g1_col[:, :], None, ALU.mult)\
               .then_inc(s_wscaled, 1)
            dve.wait_ge(s_root0, 1)
            link(dve.reciprocal(scales[:, :, :], roots[:, :, :]))

            with dve.Fori(0, CHUNKS) as c:
                for t in range(CT):
                    dve.tensor_scalar(xn_stage[:, t * DIM:(t + 1) * DIM],
                                      x_tok[:, ds(c * CHUNK + t * DIM, DIM)],
                                      s_mean[:, ds(c * CT + t, 1)], scales[:, 0, ds(c * CT + t, 1)],
                                      ALU.subtract, ALU.mult).then_inc(s_xn, 1)
                r1 = scales[:, 1, ds(c * CT, CT)]
                dve.wait_ge(s_sq, c + 1)
                dve.tensor_reduce(norms, squares.rearrange("p (h d) -> p h d", d=HD), AX.X, ALU.add)\
                   .then_inc(s_nsq, 1)
                dve.tensor_tensor(rope_in.rearrange("p (t n) -> p t n", t=CT), ps[:, 0:CT, QK_COLS:QK_COLS + ROPE_COLS],
                                  r1.unsqueeze(2).to_broadcast([P, CT, ROPE_COLS]), ALU.mult).then_inc(s_rin, 1)
                v_ps = ps[:, 4:6, 0:2 * V_COLS].rearrange("p b (t n) -> p b t n", t=2)
                dve.wait_ge(s_vc, c + 1)
                dve.tensor_tensor(v_causal[:, ds(c * (CT * KV_HEADS * HD), CT * KV_HEADS * HD)]
                                  .rearrange("p (b t n) -> p b t n", b=2, t=2), v_ps[:, :, :, DIM:V_COLS],
                                  r1.rearrange("p (b t) -> p b t", b=2).unsqueeze(3)
                                  .to_broadcast([P, 2, 2, KV_HEADS * HD]), ALU.mult).then_inc(s_dve1, 1)
                dve.wait_ge(s_nroot, c + 1)
                dve.tensor_scalar(norms, norms, NORM_EPS, None, ALU.max).then_inc(s_dve1, 1)
                dve.wait_ge(s_dve1, 4 * c + 2)
                dve.reciprocal(inv_norms, norms).then_inc(s_dve1, 1)
                dve.wait_ge(s_dve1, 4 * c + 3)
                inv_q = inv_norms.rearrange("p (t h) -> p t h", t=CT)[:, :, 0:HEADS]
                dve.tensor_scalar(inv_q, inv_q, g_col[:, :], None, ALU.mult).then_inc(s_dve1, 1)
                dve.wait_ge(s_dve1, 4 * c + 4)
                dve.tensor_tensor(unit.rearrange("p (t h d) -> p t h d", t=CT, d=HD),
                                  ps[:, 0:CT, 0:QK_COLS].rearrange("p t (h d) -> p t h d", d=HD),
                                  inv_norms.rearrange("p (t h) -> p t h", t=CT).unsqueeze(3)
                                  .to_broadcast([P, CT, QK_HEADS, HD]), ALU.mult).then_inc(s_res, 1)
                a_parts = parts_cos[:, ds(c * (CT * QK_HEADS * HEAD_COLS), CT * QK_HEADS * HEAD_COLS)]\
                    .rearrange("p (h s d) -> p h s d", s=PARTS, d=HD)
                r_parts = parts_rope[:, ds(c * (CT * ROPE_HEADS * HEAD_COLS), CT * ROPE_HEADS * HEAD_COLS)]\
                    .rearrange("p (h s d) -> p h s d", s=PARTS, d=HD)
                unit_h = unit.rearrange("p (h d) -> p h d", d=HD)
                rope_h = rope_a.rearrange("p (h d) -> p h d", d=HD)
                dve.wait_ge(s_hi, 2 * c + 1)
                dve.tensor_tensor(unit_h, unit_h, a_parts[:, :, 0, :], ALU.subtract).then_inc(s_res, 1)
                dve.wait_ge(s_hi, 2 * c + 2)
                dve.tensor_tensor(rope_h, rope_h, r_parts[:, :, 0, :], ALU.subtract).then_inc(s_res, 1)
                dve.wait_ge(s_mid, 2 * c + 1)
                dve.tensor_tensor(a_parts[:, :, 2, :], unit_h, a_parts[:, :, 1, :], ALU.subtract).then_inc(s_lo, 1)
                dve.wait_ge(s_mid, 2 * c + 2)
                dve.tensor_tensor(r_parts[:, :, 2, :], rope_h, r_parts[:, :, 1, :], ALU.subtract).then_inc(s_lo, 1)
                dve.wait_ge(s_lo, 2 * c + 3)
                dve.wait_ge(s_xn_saved, c + 1)

            def empty_slot(base, index, kind, a, b, it):
                k = index % 2
                dve.wait_ge(s_fill, base + (index + 1))
                if kind in ("cos", "query", "key"):
                    name = ("q_cos", "k_cos")[a] if kind == "cos" else kind
                    rows = HEAD_COLS if kind == "key" else P
                    for signal in ("query0", "query1") if kind == "query" else (name,):
                        dve.wait_ge(s_laid[signal], (it + 1) * LAID[signal])
                    dve.tensor_copy(parts_t[name][0:rows, :], aux_b[k][0:rows, :]).then_inc(s_free, 1)
                elif kind == "neg_max":
                    dve.wait_ge(s_laid[f"neg_max{a}"], (it + 1) * LAID[f"neg_max{a}"])
                    dve.tensor_copy(neg_max_t[:, a, :], aux_b[k][0:2 * SEQ_TILES, 0:P]).then_inc(s_free, 1)
                elif kind == "max":
                    t, piece = MAX_PIECES[b]
                    width = min((t + 1) * P - piece * BANK, BANK)
                    dve.tensor_reduce(neg_piece[:, a, t, piece:piece + 1], aux[k][:, 0:width], AX.X, ALU.max,
                                      negate=True).then_inc(s_free, 1)

            def normalise(base, index, step, dst):
                k = index % 2
                o = aux[k].rearrange("p (t h d) -> p t h d", t=CT, h=GROUP)
                dve.wait_ge(s_fill, base + (index + 1))
                dve.reciprocal(recip[:, k, :, :], o[:, :, :, HD]).then_inc(s_norm, 1)
                dve.wait_ge(s_norm, step)
                dve.tensor_tensor(dst.rearrange("p (t h d) -> p t h d", t=CT, h=GROUP), o[:, :, :, 0:HD],
                                  recip[:, k, :, :].unsqueeze(3).to_broadcast([P, CT, GROUP, HD]),
                                  ALU.mult).then_inc(s_free, 1)

            def copy_acc(which, tiles_done):
                dve.wait_ge(s_pv, tiles_done)
                dve.tensor_copy(out_t[:, which, :], acc.rearrange("p b n -> p (b n)")).then_inc(s_accfree, 1)

            cols, half_cols = SEQ_TILES * 32, CT * 32
            for n, (kind, a) in enumerate((("cos", 0), ("cos", 1), ("key", 0), ("query", 0))):
                empty_slot(0, n, kind, a, 0, 0)
            with dve.Fori(0, ITERS) as it:
                base = it * JOBS
                tiles = it * (2 * SEQ_TILES)
                for n, (kind, a, b) in enumerate(COS_JOBS):
                    if kind == "out_causal":
                        normalise(base, FIRST_JOBS + n, it * 4 + (a + 1),
                                  att_causal[:, ds(it * cols + a * half_cols, half_cols)])
                    else:
                        empty_slot(base, FIRST_JOBS + n, kind, a, b, it)
                    if kind == "max" and b == len(MAX_PIECES) - 1:
                        dve.wait_ge(s_free, base + (FIRST_JOBS + n + 1 + 2))
                        dve.tensor_tensor(neg_max[:, a, :], neg_piece[:, a, :, 0], neg_piece[:, a, :, 1],
                                          ALU.min).then_inc(s_negmax, 1)
                for n, (kind, a, b) in enumerate(CAUSAL_JOBS):
                    if n == 2:
                        copy_acc(0, tiles + (SEQ_TILES + TILE_CREDIT))
                    index = FIRST_JOBS + len(COS_JOBS) + n
                    if kind == "out_cos":
                        normalise(base, index, it * 4 + (a + 3),
                                  att_cos[:, ds(it * cols + a * half_cols, half_cols)])
                    else:
                        empty_slot(base, index, kind, a, b, it + 1)
                copy_acc(1, tiles + (2 * SEQ_TILES + TILE_CREDIT))
            for a in range(2):
                normalise(ITERS * JOBS, FIRST_JOBS + a, ITERS * 4 + (a + 1),
                          att_causal[:, ITERS * cols + a * half_cols:ITERS * cols + (a + 1) * half_cols])

            with dve.Fori(0, CHUNKS) as c:
                chunk = ds(c * CHUNK, CHUNK)
                dve.wait_ge(s_f1["wo"], c + 2)
                dve.tensor_tensor(xn[:, chunk], xn[:, chunk], ps[:, 1, :], ALU.add).then_inc(s_f1["x1"], 1)
                dve.wait_ge(s_f1["sum"], c + 1)
                dve.wait_ge(s_f1["x1"], c + 2)
                dve.tensor_tensor(x_tok[:, chunk], x_tok[:, chunk], xn[:, chunk], ALU.add).then_inc(s_f1["y"], 1)
                dve.wait_ge(s_f1["sq"], c + 1)
                dve.tensor_reduce(sum_sq[:, ds(c * CT, CT)], f_stage.rearrange("p (t d) -> p t d", t=CT),
                                  AX.X, ALU.add).then_inc(s_f1["ssq"], 1)
            dve.wait_ge(s_f1["ssq"], CHUNKS + 1)
            dve.tensor_scalar(sum_sq[:, :], sum_sq[:, :], 1.0 / DIM, RMS_EPS, ALU.mult, ALU.add)\
               .then_inc(s_f2["ms"], 1)
            dve.wait_ge(s_f2["root"], 1)
            dve.reciprocal(s_var[:, :], sum_sq[:, :]).then_inc(s_f2["r2"], 1)
            dve.wait_ge(s_f2["r2"], 1)

            with dve.Fori(0, CHUNKS) as c:
                dve.wait_ge(s_f2["gate"], c + 1)
                dve.tensor_tensor(f_stage.rearrange("p (t d) -> p t d", t=CT),
                                  xn[:, ds(c * CHUNK, CHUNK)].rearrange("p (t d) -> p t d", t=CT),
                                  s_var[:, ds(c * CT, CT)].unsqueeze(2).to_broadcast([P, CT, DIM]), ALU.mult)\
                   .then_inc(s_f2["xs"], 1)
                dve.wait_ge(s_f2["gate"], c + 2)
                dve.tensor_copy(logits[:, ds(c * CT, CT), :],
                                ps[:, 1, 0:CT * EXPERTS].rearrange("p (t e) -> p t e", t=CT)).then_inc(s_f2["logits"], 1)
            dve.wait_ge(s_f2["logits"], CHUNKS + 1)

            steps2 = [0]

            def link2(ins):
                steps2[0] += 1
                ins.then_inc(s_f2["dve"], 1)
                dve.wait_ge(s_f2["dve"], steps2[0])

            g_max = g_cmp[:, 0, :]
            link2(dve.tensor_reduce(g_max, logits[:, :, :], AX.X, ALU.max))
            link2(dve.tensor_tensor(logits[:, :, :], logits[:, :, :],
                                    g_max.unsqueeze(2).to_broadcast([P, TILES, EXPERTS]), ALU.subtract))
            link2(dve.memset(g_rank[:, :, :], 0.0))
            dve.wait_ge(s_f2["exp"], 1)
            pairs = [(i, j) for i in range(EXPERTS) for j in range(i + 1, EXPERTS)]
            for n, (i, j) in enumerate(pairs):
                ins = dve.tensor_tensor(g_cmp[:, n, :], g_exp[:, :, i], g_exp[:, :, j], ALU.is_ge)
            link2(ins)
            for n, (i, j) in enumerate(pairs):
                link2(dve.tensor_tensor(g_rank[:, :, j], g_rank[:, :, j], g_cmp[:, n, :], ALU.add))
                link2(dve.tensor_tensor(g_rank[:, :, i], g_rank[:, :, i], g_cmp[:, n, :], ALU.subtract))
            for i in range(EXPERTS):
                link2(dve.tensor_scalar(g_rank[:, :, i], g_rank[:, :, i], float(EXPERTS - 1 - i), 2.0,
                                        ALU.add, ALU.is_lt))
            link2(dve.tensor_tensor(g_exp[:, :, :], g_exp[:, :, :], g_rank[:, :, :], ALU.mult))
            link2(dve.tensor_reduce(g_max, g_exp[:, :, :], AX.X, ALU.add))
            link2(dve.reciprocal(g_max, g_max))
            link2(dve.tensor_tensor(comb[:, :].rearrange("p (t e) -> p t e", t=TILES), g_exp[:, :, :],
                                    g_max.unsqueeze(2).to_broadcast([P, TILES, EXPERTS]), ALU.mult))

            dve.wait_ge(s_f1["y"], CHUNKS)
            with dve.Fori(0, CHUNKS) as c:
                def add_expert(e):
                    dve.wait_ge(s_f3["y"], c * EXPERTS + (e + 3))
                    if e:
                        dve.wait_ge(s_f3["y_used"], c * EXPERTS + (e + 2))
                    for t in range(CT):
                        acc_t = x_tok[:, ds(c * CHUNK + t * DIM, DIM)]
                        ins = dve.scalar_tensor_tensor(
                            out=acc_t, in0=ps[:, 4 + e % 2, t * DIM:(t + 1) * DIM],
                            scalar=comb[:, ds(c * (CT * EXPERTS) + (t * EXPERTS + e), 1)], in1=acc_t,
                            op0=ALU.mult, op1=ALU.add)
                    ins.then_inc(s_f3["y_used"], 1)

                for e in range(EXPERTS):
                    for h in range(HT):
                        k = e * HT + h
                        dve.wait_ge(s_f3["silu"], c * (EXPERTS * HT) + (k + 1))
                        if h == 0:
                            dve.wait_ge(s_f3["y"], c * EXPERTS + (e + 1))
                        dve.tensor_tensor(hidden[e % 2][:, h, :], gated[k % 2], ps[:, 2 + k % 2, :], ALU.mult)\
                           .then_inc(s_f3["h"], 1)
                    if e:
                        add_expert(e - 1)
                add_expert(EXPERTS - 1)

        @block.tensor
        def _(pe):
            pe.wait_ge(s_const, 8)
            pe.wait_ge(s_wscaled, 3)
            with pe.Fori(0, CHUNKS) as c:
                pe.wait_ge(s_xn, CT * c + CT)
                for t in range(CT):
                    ins = pe.transpose(ps[:, 6, t * P:(t + 1) * P], xn_stage[:, t * DIM:(t + 1) * DIM], ident[:, :])
                ins.then_inc(s_xt_ps, 1)
                pe.wait_ge(s_xt, c + 1)
                pe.wait_ge(s_res, 3 * c + (RES_CREDIT - 2))
                for t in range(CT):
                    pe.matmul(ps[:, t, 0:QK_COLS + ROPE_COLS], xn_t[:, t * P:(t + 1) * P], w_qk[:, :],
                              start=True, stop=True)
                for t in range(CT):
                    v_out = ps[:, 4 + t // 2, (t % 2) * V_COLS:(t % 2 + 1) * V_COLS]
                    ins = pe.matmul(v_out, xn_t[:, t * P:(t + 1) * P], w_v[:, :], start=True, stop=True)
                ins.then_inc(s_proj, 1)

            pe.wait_ge(s_clear, 8)
            pe.wait_ge(s_again, 2 * CHUNKS)
            pe.wait_ge(s_lo, 2 * CHUNKS + 1)

            def aux_job(base, index, kind, a, b, batch, group):
                k = index % 2
                pe.wait_ge(s_free, base + (index + 1))
                if kind in ("cos", "query", "key"):
                    if kind == "cos":
                        flat, heads, first, step = parts_cos, QK_HEADS, a * HEADS, GROUP
                    elif kind == "query":
                        flat, heads, first, step = parts_rope, ROPE_HEADS, 0, GROUP
                    else:
                        flat, heads, first, step = parts_rope, ROPE_HEADS, HEADS, 1
                    for t in range(SEQ_TILES):
                        src = flat[:, ds(batch * (SEQ_TILES * heads * HEAD_COLS) + group * (step * HEAD_COLS)
                                         + (t * heads + first) * HEAD_COLS, P)]
                        ins = pe.transpose(aux_b[k][:, t * P:(t + 1) * P], src, ident_b[:, :])
                elif kind == "neg_max":
                    ins = pe.transpose(aux_b[k][0:2 * SEQ_TILES, 0:P],
                                       neg_max[:, 2 * a:2 * a + 2, :].rearrange("p h t -> p (h t)"), ident_b[:, :])
                elif kind == "max":
                    t, piece = MAX_PIECES[b]
                    width = min((t + 1) * P - piece * BANK, BANK)
                    last = piece == t // 4
                    ins = pe.matmul(aux[k][:, 0:width], q_causal_t[0:BIAS_ROW, a, t * P:(t + 1) * P],
                                    k_causal_t[0:BIAS_ROW, piece * BANK:piece * BANK + width], start=True, stop=True)
                    if last:
                        ins = pe.matmul(aux[k][:, width - P:width], ident_b[:, :], mask_q[:, :], start=False, stop=True,
                                        skip_group_check=True)
                else:
                    which = int(kind == "out_causal")
                    for t in range(CT):
                        lo = (a * CT + t) * P
                        ins = pe.transpose(aux[k][:, t * P:(t + 1) * P], out_t[:, which, lo:lo + P], ident[:, :])
                ins.then_inc(s_fill, 1)

            def scores(n, j, h, heads, causal):
                s = slot(n)
                for i in range(heads):
                    if causal:
                        width = SEQ - j * P
                        keys, queries = k_causal_t[:, j * P:(j + 1) * P], q_causal_t[:, h + i, :]
                        place = j * P if heads == 1 else (i * BANK if heads == 2 else i * width)
                    else:
                        width, place = SEQ, 0
                        keys, queries = k_cos_t[:, h, j * P:(j + 1) * P], q_cos_t[:, h, :]
                    done = 0
                    while done < width:
                        at = place + done
                        n_cols = min(width - done, BANK - at % BANK)
                        q0 = SEQ - width + done
                        first = at % BANK == 0 or i == 0 or heads == 2
                        ins = pe.matmul(s[:, at:at + n_cols], keys, queries[:, q0:q0 + n_cols], start=first,
                                        stop=True, skip_group_check=True)
                        if causal and done == 0:
                            ins = pe.matmul(s[:, at:at + P], ident_b[:, :], mask_k[:, :], start=False, stop=True,
                                            skip_group_check=True)
                        done += n_cols
                ins.then_inc(s_sc, 1)

            def values(j, quarter, causal):
                lo, hi = max(quarter * 256, j * P if causal else 0), (quarter + 1) * 256
                bank, at = divmod(lo, BANK)
                for h in range(GROUP):
                    v = v_causal_pad[:, j, :] if causal else v_cos_pad[:, j, h, :]
                    ins = pe.matmul(acc[32 * h:32 * h + 32, bank, at:at + hi - lo], v, probs[:, j % 2, h, lo:hi],
                                    start=(j == 0 and at == 0), stop=True, skip_group_check=True)
                return ins

            def score_step(n, it_first, exps, cos_laid):
                causal = len(COS_STEPS) <= n < STEPS
                j, h, heads = (COS_STEPS + CAUSAL_STEPS)[n % STEPS]
                if j == h == 0 and not causal:
                    pe.wait_ge(s_laid["q_cos"], it_first * LAID["q_cos"] + cos_laid * LAID["q_cos"])
                    pe.wait_ge(s_laid["k_cos"], it_first * LAID["k_cos"] + cos_laid * LAID["k_cos"])
                if j == 0 and causal and h in (0, 2):
                    name = f"neg_max{h // 2}"
                    pe.wait_ge(s_laid[name], it_first * LAID[name] + 2 * LAID[name])
                pe.wait_ge(s_pr, exps)
                scores(n, j, h, heads, causal)

            for n, (kind, a) in enumerate((("cos", 0), ("cos", 1), ("key", 0), ("query", 0))):
                aux_job(0, n, kind, a, 0, 0, 0)
            for n in range(2):
                score_step(n, 0, n + 1, 2)
            with pe.Fori(0, ITERS) as it:
                batch, group = it // GROUPS, it % GROUPS
                next_batch, next_group = ((it + 1) % ITERS) // GROUPS, ((it + 1) % ITERS) % GROUPS
                base = it * JOBS

                def next_job(n):
                    kind, a, b = (COS_JOBS + CAUSAL_JOBS)[n]
                    if kind == "out_causal":
                        pe.wait_ge(s_accfree, it * 2 + 1)
                    elif kind == "out_cos":
                        pe.wait_ge(s_accfree, it * 2 + 2)
                    elif kind == "max" and b == 0 and a % 2 == 0:
                        if a == 0:
                            pe.wait_ge(s_laid["key"], (it + 2) * LAID["key"])
                        pe.wait_ge(s_laid[f"query{a // 2}"], (it + 2) * LAID[f"query{a // 2}"])
                    elif kind == "neg_max":
                        pe.wait_ge(s_negmax, it * GROUP + (2 * a + 2))
                    of_next = kind in ("cos", "key", "query")
                    aux_job(base, FIRST_JOBS + n, kind, a, b,
                            next_batch if of_next else batch, next_group if of_next else group)

                def value_quarter(j, quarter, causal, steps_done):
                    first = quarter == (j // 2 if causal else 0)
                    if first:
                        pe.wait_ge(s_pr, it * STEPS + (steps_done + 2))
                    if first and j == 0:
                        pe.wait_ge(s_vb if causal else s_va, it + 1)
                        pe.wait_ge(s_accfree, it * 2 + (1 + causal))
                    ins = values(j, quarter, causal)
                    if quarter == 3:
                        ins.then_inc(s_pv, 1)

                plan = COS_ISSUED + [len(COS_JOBS) + i for i in CAUSAL_ISSUED] + [JOBS, JOBS]
                tile_of = [step[0] + SEQ_TILES * (n >= len(COS_STEPS)) for n, step in enumerate(COS_STEPS + CAUSAL_STEPS)]
                tile_of += [2 * SEQ_TILES] * 2
                pending, issued = [], 0
                for n in range(2, STEPS + 2):
                    score_step(n, it, it * STEPS + (n + 1), 3)
                    jobs = plan[n] - issued
                    left = tile_of[n:].count(tile_of[n])
                    quarters = -(-len(pending) // left) if n != STEPS else 0
                    for i in range(max(jobs, quarters)):
                        if i < jobs:
                            next_job(issued)
                            issued += 1
                        if i < quarters:
                            value_quarter(*pending.pop(0))
                    if left == 1:
                        causal = n >= len(COS_STEPS)
                        j = tile_of[n] % SEQ_TILES
                        pending = [(j, q, causal, n + 1) for q in range(j // 2 if causal else 0, 4)]
            pe.wait_ge(s_accfree, ITERS * 2 + 1)
            for a in range(2):
                aux_job(ITERS * JOBS, FIRST_JOBS + a, "out_causal", a, 0, 0, 0)

            pe.wait_ge(s_w_rest, 80)
            with pe.Fori(0, CHUNKS) as c:
                pe.wait_ge(s_f1["staged"], c + 1)
                for t in range(CT):
                    ins = pe.transpose(ps[:, 0, t * P:(t + 1) * P], att_stage[:, t * DIM:(t + 1) * DIM], ident[:, :])
                ins.then_inc(s_f1["t_ps"], 1)
                pe.wait_ge(s_f1["t"], c + 1)
                pe.wait_ge(s_f1["x1"], c + 1)
                for t in range(CT):
                    ins = pe.matmul(ps[:, 1, t * DIM:(t + 1) * DIM], att_stage_t[:, t * P:(t + 1) * P], w_o[:, :],
                                    start=True, stop=True)
                ins.then_inc(s_f1["wo"], 1)
            with pe.Fori(0, CHUNKS) as c:
                pe.wait_ge(s_f2["xs"], c + 1)
                pe.wait_ge(s_f2["t"], c + 1)
                for t in range(CT):
                    ins = pe.transpose(ps[:, 0, t * P:(t + 1) * P], f_stage[:, t * DIM:(t + 1) * DIM], ident[:, :])
                ins.then_inc(s_f2["t_ps"], 1)
                pe.wait_ge(s_f2["t_stage"], c + 1)
                pe.wait_ge(s_f2["logits"], c + 1)
                for t in range(CT):
                    ins = pe.matmul(ps[:, 1, t * EXPERTS:(t + 1) * EXPERTS], f_stage_t[:, t * P:(t + 1) * P],
                                    w_gate[:, :], start=True, stop=True)
                ins.then_inc(s_f2["gate"], 1)
            pe.wait_ge(s_f2["t"], CHUNKS + 1)
            pe.wait_ge(s_f2["logits"], CHUNKS + 1)
            with pe.Fori(0, CHUNKS) as c:
                def down(e):
                    pe.wait_ge(s_f3["h"], c * (EXPERTS * HT) + ((e + 1) * HT + 2))
                    pe.wait_ge(s_f3["y_used"], c * EXPERTS + (e + 1))
                    for t in range(CT):
                        for h in range(HT):
                            ins = pe.matmul(ps[:, 4 + e % 2, t * DIM:(t + 1) * DIM],
                                            hidden[e % 2][:, h, t * P:(t + 1) * P], w_2[:, e * HT + h, :],
                                            start=h == 0, stop=h == HT - 1)
                    ins.then_inc(s_f3["y"], 1)

                tokens = xf_t[:, ds(c * CHUNK, CHUNK)]
                for e in range(EXPERTS):
                    for h in range(HT):
                        k = e * HT + h
                        pe.wait_ge(s_f3["h"], c * (EXPERTS * HT) + (k + 1))
                        pe.matmul(ps[:, k % 2, :], w_1[:, e, h * P:(h + 1) * P], tokens, start=True, stop=True)
                        pe.matmul(ps[:, 2 + k % 2, :], w_3[:, e, h * P:(h + 1) * P], tokens, start=True, stop=True)\
                          .then_inc(s_f3["up"], 1)
                        if h == 0 and e:
                            down(e - 1)
                down(EXPERTS - 1)


def kernel(**inputs):
    import numpy as _np
    import concourse.bacc as _bacc
    from concourse import mybir as _mybir
    from concourse.bass_utils import run_bass_kernel_spmd as _run

    inv_freq = _np.float32(1.0) / _np.float32(10000.0) ** (_np.arange(0, HD, 2, dtype=_np.float32) / _np.float32(HD))
    freqs = _np.arange(SEQ, dtype=_np.float32)[:, None] * inv_freq.astype(_np.float32)[None, :]
    angles = _np.concatenate([freqs, freqs], axis=-1)
    sign = _np.where(_np.arange(HD) < HD // 2, -1.0, 1.0)
    def tiled(table):
        table = table.astype(_np.float32).reshape(SEQ_TILES, P, HD)
        return _np.ascontiguousarray(table.transpose(1, 0, 2).reshape(P, SEQ_TILES * HD))

    given = {name.replace("L0_", ""): _np.asarray(a) for name, a in inputs.items()}
    arrays = {
        "x": given["attn_x"], "wq_cos": given["attn_Wq"].T, "wk_cos": given["attn_Wk"].T, "wv_cos": given["attn_Wv"].T,
        "g_scale": _np.broadcast_to(given["attn_g_scale"].reshape(1, 1), (P, 1)),
        "g1": given["ffn_g1"].reshape(P, 1), "g2": given["ffn_g2"].reshape(P, 1),
        "wq": given["ffn_wq"], "wk": given["ffn_wk"], "wv": given["ffn_wv"], "wo": given["ffn_wo"],
        "gate": given["ffn_gate"], "w1": given["ffn_w1"], "w2": given["ffn_w2"], "w3": given["ffn_w3"],
        "cos_table": tiled(_np.cos(angles)), "sin_table": tiled(_np.sin(angles) * sign),
    }
    nc = _bacc.Bacc("TRN2", target_bir_lowering=False, num_devices=1)
    feeds, aps = {}, {}
    for name, a in arrays.items():
        feeds[f"in_{name}"] = _np.ascontiguousarray(a)
        aps[name] = nc.dram_tensor(f"in_{name}", a.shape, _mybir.dt.float32, kind="ExternalInput").ap()
    result = nc.dram_tensor("out_dram", (BATCH, SEQ, DIM), _mybir.dt.float32, kind="ExternalOutput").ap()
    build(nc, out=result, **aps)
    return _run(nc, [feeds], core_ids=[0]).results[0]["out_dram"]
```

```python
from contextlib import ExitStack

import concourse.bass as bass
from concourse import mybir

F32 = mybir.dt.float32
BF16 = mybir.dt.bfloat16
ALU = mybir.AluOpType
ACT = mybir.ActivationFunctionType
AX = mybir.AxisListType
ds = bass.ds

P = 128
BATCH, SEQ, DIM = 2, 1024, 128
TILES = BATCH * SEQ // P
SEQ_TILES = SEQ // P
CT = 4
CHUNKS = TILES // CT
CHUNK = CT * P
HEADS, KV_HEADS, HD = 16, 4, 8
GROUP = 4
GROUPS = HEADS // GROUP
ITERS = BATCH * GROUPS
PARTS = 4
HEAD_COLS = PARTS * HD
WINDOW = 3 * HD
TERMS = 3 * WINDOW
BIAS_ROW = 96
Q_WINDOWS, K_WINDOWS = (0, 0, HD), (0, HD, 0)
QK_HEADS = 2 * HEADS
ROPE_HEADS = HEADS + KV_HEADS
QK_COLS, ROPE_COLS, V_COLS = 2 * DIM, ROPE_HEADS * HD, DIM + KV_HEADS * HD
EXPERTS, HIDDEN = 4, 384
HT = HIDDEN // P
LN_EPS, RMS_EPS, NORM_EPS = 1e-5, 1.1920928955078125e-07, 1e-12
MASKED = -1e30
BIG = 3e38
BANK = 512
SLOT = 2 * BANK

COS_STEPS = [(j, h, 1) for j in range(SEQ_TILES) for h in range(GROUP)]
CAUSAL_STEPS = ([(j, h, 1) for j in range(4) for h in range(GROUP)]
                + [(j, h, 2) for j in (4, 5) for h in (0, 2)] + [(6, 0, 4), (7, 0, 4)])
STEPS = len(COS_STEPS) + len(CAUSAL_STEPS)
ZEROED_STEPS = sum(j < 6 for j, h, heads in CAUSAL_STEPS)
ROWS_CLEARED = 6
TURN = 3 * GROUP

PIECES = [(t, p, min((t + 1) * P - p * BANK, BANK)) for t in range(SEQ_TILES) for p in range(1 + t // 4)]
PACKED = {P: 4, 2 * P: 2, 3 * P: 1, 4 * P: 1}
MAXIMA = [[(t, p, w, h, PACKED[w]) for t, p, w in PIECES for h in range(pair, pair + 2, PACKED[w]) if PACKED[w] < 4]
          for pair in (0, 2)]
ALL_HEADS = [(t, p, w, 0, GROUP) for t, p, w in PIECES if PACKED[w] == GROUP]
FIRST_PAIR = [("max", 0, piece) for piece in ALL_HEADS + MAXIMA[0]]
EARLY = 4
COS_JOBS = FIRST_PAIR[EARLY:]
COS_JOBS.insert(1, ("out_causal", 1, 0))
COS_JOBS[7:7] = [("key", 0, 0), ("query", 0, 0)]
COS_JOBS += [("max", 1, piece) for piece in MAXIMA[1][:2]] + [("neg_max", 0, 0)]
COS_JOBS += [("max", 1, piece) for piece in MAXIMA[1][2:]] + [("cos", 0, 0), ("neg_max", 1, 0)]
CAUSAL_JOBS = [("cos", 1, 0), ("out_cos", 0, 0), ("out_cos", 1, 0)] + FIRST_PAIR[:EARLY] + [("out_causal", 0, 0)]
MAX_STEPS = 29
COS_ISSUED = ([0, 0] + [-(-(len(COS_JOBS) - 1) * (i + 1) // MAX_STEPS) for i in range(MAX_STEPS)]
              + [len(COS_JOBS)])
CAUSAL_JOB_STEPS = (0, 5, 6, 9, 11, 14, 16, 20)
CAUSAL_ISSUED = [sum(step <= i for step in CAUSAL_JOB_STEPS) for i in range(len(CAUSAL_STEPS))]
assert ITERS % 2 == 0
ALL_JOBS = COS_JOBS + CAUSAL_JOBS
JOBS = len(ALL_JOBS)
OF_NEXT = ("cos", "key", "query")
FIRST = [("cos", 0, 0), ("cos", 1, 0), ("key", 0, 0), ("query", 0, 0)] + FIRST_PAIR[:EARLY]
FIRST_JOBS = len(FIRST)
assert STEPS % 2 == 0 and JOBS % 2 == 0 and FIRST_JOBS % 2 == 0

TILE_CREDIT = 2 * SEQ_TILES
RES_CREDIT = 3
LO_CREDIT = 2
LAID = {"q_cos": 48 * GROUP, "k_cos": 48 * GROUP, "query": 48 * GROUP, "key": 48, "neg_max0": 16, "neg_max1": 16}


def build(nc, x, wq_cos, wk_cos, wv_cos, g_scale, g1, g2, wq, wk, wv, wo, gate, w1, w2, w3,
          cos_table, sin_table, out):
    ctx = ExitStack()
    with ctx:
        def sb(name, shape, dt=F32):
            return ctx.enter_context(nc.sbuf_tensor(name, shape, dt))

        def sem(name):
            return ctx.enter_context(nc.semaphore(name))

        x_tok = sb("x_tok", [P, TILES * DIM])
        xn = sb("xn", [P, TILES * DIM])
        w_qk = sb("w_qk", [P, QK_COLS + ROPE_COLS])
        w_v = sb("w_v", [P, V_COLS])
        w_o = sb("w_o", [P, DIM])
        w_gate = sb("w_gate", [P, 32])
        w_1 = sb("w_1", [P, EXPERTS, HIDDEN])
        w_3 = sb("w_3", [P, EXPERTS, HIDDEN])
        w_2 = sb("w_2", [P, EXPERTS * HT, DIM])
        g1_col, g2_col, g_col = sb("g1_col", [P, 1]), sb("g2_col", [P, 1]), sb("g_col", [P, 1])
        cos_t = sb("cos_t", [P, SEQ_TILES * HD])
        sin_t = sb("sin_t", [P, SEQ_TILES * HD])
        ident = sb("ident", [P, P])
        ident_b = sb("ident_b", [P, P], BF16)
        mask_q = sb("mask_q", [P, P], BF16)
        mask_k = sb("mask_k", [P, P], BF16)
        keep = sb("keep", [P, P])
        stat = sb("stat", [P, TILES, 6])
        s_mean, s_diff, s_var = sb("s_mean", [P, TILES]), sb("s_diff", [P, TILES]), sb("s_var", [P, TILES])
        roots = sb("roots", [P, 2, TILES])
        scales = sb("scales", [P, 2, TILES])
        parts_cos = sb("parts_cos", [P, TILES * QK_HEADS * HEAD_COLS], BF16)
        parts_rope = sb("parts_rope", [P, TILES * ROPE_HEADS * HEAD_COLS + P - HEAD_COLS], BF16)
        v_cos = sb("v_cos", [P, TILES * DIM])
        v_causal = sb("v_causal", [P, TILES * KV_HEADS * HD])
        q_cos_t = sb("q_cos_t", [P, GROUP, SEQ], BF16)
        k_cos_t = sb("k_cos_t", [P, GROUP, SEQ], BF16)
        q_causal_t = [sb(f"q_causal_t{i}", [P, GROUP, SEQ], BF16) for i in range(2)]
        k_causal_t = [sb(f"k_causal_t{i}", [P, SEQ], BF16) for i in range(2)]
        parts_t = {n: sb(f"parts_t_{n}", [P, SEQ], BF16) for n in ("q_cos", "k_cos", "query", "key")}
        neg_max_t = sb("neg_max_t", [2 * SEQ_TILES, 2, P], BF16)
        v_cos_pad = sb("v_cos_pad", [P, SEQ_TILES, GROUP, 32])
        v_causal_pad = sb("v_causal_pad", [P, SEQ_TILES, 32])
        neg_piece = sb("neg_piece", [P, GROUP, SEQ_TILES, 2])
        neg_max = sb("neg_max", [P, GROUP, SEQ_TILES], BF16)
        out_t = sb("out_t", [P, 2, SEQ])
        recip = sb("recip", [P, 2, CT, GROUP])
        att_cos = sb("att_cos", [P, SEQ_TILES, GROUP * HD])
        att_causal = sb("att_causal", [P, TILES, DIM])
        probs = sb("probs", [P, 2, GROUP, SEQ])

        room = probs[:, :, :, :].rearrange("p a h s -> p (a h s)")

        def part(start, size):
            return room[:, start:start + size]

        xn_stage = part(0, CHUNK)
        xn_t = part(512, CHUNK)
        squares = part(1024, CT * QK_COLS)
        rope_in = part(3072, CT * ROPE_COLS)
        rope_a = part(3712, CT * ROPE_COLS)
        rope_b = part(4352, CT * ROPE_COLS)
        norms = part(4992, CT * QK_HEADS)
        inv_norms = part(5120, CT * QK_HEADS)
        unit = part(2048, CT * QK_COLS)
        xf_t = part(0, TILES * P)
        hidden = [part(2048 + 1536 * i, HT * CHUNK).rearrange("p (h n) -> p h n", h=HT) for i in range(2)]
        gated = [part(5120 + 512 * i, CHUNK) for i in range(2)]
        att_t = [part(6144 + 512 * i, CHUNK) for i in range(2)]
        f_stage = [part(7168 + 512 * i, CHUNK) for i in range(2)]
        sum_sq = s_mean
        logits = sb("logits", [P, TILES, EXPERTS])
        g_exp, g_rank = sb("g_exp", [P, TILES, EXPERTS]), sb("g_rank", [P, TILES, EXPERTS])
        g_cmp = sb("g_cmp", [P, 6, TILES])
        comb = sb("comb", [P, TILES * EXPERTS])
        unused = sb("unused", [P, 3])

        ps = ctx.enter_context(nc.psum_tensor("ps", [P, 8, BANK], F32))
        acc = ps[:, 4:6, :]
        aux = [ps[:, 6 + i, :] for i in range(2)]
        aux_b = [a.bitcast(BF16) for a in aux]

        def slot(n):
            return ps[:, 2 * (n % 2):2 * (n % 2) + 2, :].rearrange("p b n -> p (b n)")

        s_x = [sem(f"x_landed{i}") for i in range(CHUNKS)]
        s_wqkv, s_small, s_w_rest, s_rope_t = sem("wqkv_landed"), sem("small_landed"), sem("rest_landed"), sem("tables_landed")
        s_const, s_clear, s_rows = sem("constants_made"), sem("buffers_cleared"), sem("rows_cleared")
        s_wscaled = sem("weights_scaled")
        s_dve0, s_stats, s_root0 = sem("dve_steps_stats"), sem("stats_made"), sem("roots_made")
        s_xn, s_xn_saved = sem("xn_staged"), sem("xn_saved")
        s_xt_ps, s_xt, s_proj = sem("xt_in_psum"), sem("xt_ready"), sem("projected")
        s_qk, s_read = sem("q_and_k_copied"), sem("projections_read")
        s_sq, s_vc, s_nsq, s_nroot = sem("squares_ready"), sem("v_copied"), sem("norm_squares_ready"), sem("norms_ready")
        s_dve1, s_rin, s_rope = sem("dve_steps_proj"), sem("rope_input_ready"), sem("rope_steps")
        s_again = sem("high_parts_again")
        s_hi, s_mid, s_res, s_lo = sem("high_parts"), sem("middle_parts"), sem("residues"), sem("low_parts")
        s_sc, s_pr, s_zeroed = sem("scores_ready"), sem("probs_ready"), sem("masked_probs_zeroed")
        s_pv, s_accdone, s_accfree = sem("key_tiles_used"), sem("first_half_done"), sem("acc_halves_copied")
        s_fill, s_free = sem("aux_filled"), sem("aux_read")
        s_negmax, s_norm = sem("neg_max_ready"), sem("recips_ready")
        s_laid = {n: sem(f"laid_{n}") for n in LAID}
        s_va, s_vb = sem("v_cos_padded"), sem("v_causal_padded")
        s_f1 = {n: sem("f1_" + n) for n in ("t_ps", "t", "wo", "x1", "sq", "ssq", "sum", "y")}
        s_f2 = {n: sem("f2_" + n) for n in ("ms", "root", "r2", "xs", "t_ps", "t", "gate", "logits", "logits_ps", "dve", "exp")}
        s_f3 = {n: sem("f3_" + n) for n in ("up", "silu", "h", "y", "y_used", "stored")}

        block = ctx.enter_context(nc.Block())

        def step_view(n, j, heads, causal):
            s = slot(n)
            if not causal or j < 4:
                return s[:, (j * P if causal else 0):SEQ].unsqueeze(1)
            width = SEQ - j * P
            if heads == 2:
                return s.rearrange("p (h n) -> p h n", h=2)[:, :, 0:width]
            return s[:, 0:heads * width].rearrange("p (h n) -> p h n", h=heads)

        @block.sync
        def _(sp):
            for c in range(CHUNKS):
                b, t0 = divmod(c * CT, SEQ_TILES)
                src = x[b, t0 * P:(t0 + CT) * P, :].rearrange("(t p) d -> p t d", p=P)
                dst = x_tok[:, c * CHUNK:(c + 1) * CHUNK].rearrange("p (t d) -> p t d", t=CT)
                sp.dma_start(dst, src).then_inc(s_x[c], 16)
            sp.dma_start(g1_col[:, :], g1).then_inc(s_small, 16)
            sp.dma_start(g2_col[:, :], g2).then_inc(s_small, 16)
            sp.dma_start(g_col[:, :], g_scale).then_inc(s_small, 16)
            sp.dma_start(cos_t[:, :], cos_table).then_inc(s_rope_t, 16)
            sp.dma_start(sin_t[:, :], sin_table).then_inc(s_rope_t, 16)
            sp.dma_start(w_1[:, :, :], w1.rearrange("e i h -> i e h")).then_inc(s_w_rest, 16)
            sp.dma_start(w_3[:, :, :], w3.rearrange("e i h -> i e h")).then_inc(s_w_rest, 16)
            sp.dma_start(w_2[:, :, :], w2.rearrange("e (h i) d -> i (e h) d", i=P)).then_inc(s_w_rest, 16)
            sp.dma_start(w_o[:, :], wo).then_inc(s_w_rest, 16)
            sp.dma_start(w_gate[:, 0:EXPERTS], gate).then_inc(s_w_rest, 16)

            def lay_out(signal, src, dst, windows, heads):
                for h in heads:
                    for w, row in enumerate(windows):
                        sp.dma_start(dst[w * WINDOW:(w + 1) * WINDOW, h, :],
                                     parts_t[src][h * HEAD_COLS + row:h * HEAD_COLS + row + WINDOW, :])\
                          .then_inc(s_laid[signal], 16)

            def lay_out_cos(base, base_k, scores_made):
                sp.wait_ge(s_free, base + 3)
                sp.wait_ge(s_sc, scores_made)
                lay_out("q_cos", "q_cos", q_cos_t, Q_WINDOWS, range(GROUP))
                sp.wait_ge(s_free, base_k + 3)
                lay_out("k_cos", "k_cos", k_cos_t, K_WINDOWS, range(GROUP))

            def lay_out_causal(base, parity):
                sp.wait_ge(s_free, base + 3)
                lay_out("key", "key", k_causal_t[parity][:, :].unsqueeze(1), K_WINDOWS, range(1))
                sp.wait_ge(s_free, base + 4)
                lay_out("query", "query", q_causal_t[parity], Q_WINDOWS, range(GROUP))

            sp.wait_ge(s_rows, ROWS_CLEARED)
            lay_out_cos(0, 1, 1)
            lay_out_causal(2, 0)
            with sp.Fori(0, ITERS // 2) as pair:
                for parity in range(2):
                    base = (pair * 2 + parity) * JOBS + FIRST_JOBS
                    lay_out_causal(base + COS_JOBS.index(("key", 0, 0)), 1 - parity)
                    for a in range(2):
                        sp.wait_ge(s_free, base + (COS_JOBS.index(("neg_max", a, 0)) + 3))
                        sp.dma_start(q_causal_t[parity][BIAS_ROW:BIAS_ROW + 1, 2 * a:2 * a + 2, :], neg_max_t[:, a, :])\
                          .then_inc(s_laid[f"neg_max{a}"], 16)
                    lay_out_cos(base + ALL_JOBS.index(("cos", 0, 0)), base + ALL_JOBS.index(("cos", 1, 0)),
                                (pair * 2 + parity) * STEPS + (len(COS_STEPS) + 1))
            for name in ("q_cos", "k_cos", "key", "query"):
                sp.wait_ge(s_laid[name], (ITERS + 2) * LAID[name])

            for c in range(CHUNKS):
                b, t0 = divmod(c * CT, SEQ_TILES)
                dst = out[b, t0 * P:(t0 + CT) * P, :].rearrange("(t p) d -> p t d", p=P)
                sp.wait_ge(s_f3["y_used"], (c + 1) * EXPERTS + 2)
                sp.dma_start(dst, x_tok[:, c * CHUNK:(c + 1) * CHUNK].rearrange("p (t d) -> p t d", t=CT))\
                  .then_inc(s_f3["stored"], 16)
            sp.wait_ge(s_f3["stored"], 16 * CHUNKS)

        @block.gpsimd
        def _(pool):
            pool.memset(ident[:, :], 0.0).then_inc(s_const, 1)
            pool.memset(ident_b[:, :], 0.0).then_inc(s_const, 1)
            pool.memset(mask_q[:, :], 0.0).then_inc(s_const, 1)
            pool.memset(mask_k[:, :], 0.0).then_inc(s_const, 1)
            pool.memset(keep[:, :], BIG).then_inc(s_const, 1)
            pool.wait_ge(s_const, 5)
            for m in (ident, ident_b):
                pool.affine_select(out=m[:, :], in_=m[:, :], compare_op=ALU.not_equal, fill=1.0,
                                   base=0, pattern=[[-1, P]], channel_multiplier=1).then_inc(s_const, 1)
            pool.affine_select(out=mask_q[:, :], in_=mask_q[:, :], compare_op=ALU.is_ge, fill=MASKED,
                               base=0, pattern=[[-1, P]], channel_multiplier=1).then_inc(s_const, 1)
            pool.affine_select(out=mask_k[:, :], in_=mask_k[:, :], compare_op=ALU.is_ge, fill=MASKED,
                               base=0, pattern=[[1, P]], channel_multiplier=-1).then_inc(s_const, 1)
            pool.affine_select(out=keep[:, :], in_=keep[:, :], compare_op=ALU.is_ge, fill=0.0,
                               base=0, pattern=[[1, P]], channel_multiplier=-1).then_inc(s_const, 1)
            pool.memset(v_cos_pad[:, :, :, HD:], 0.0).then_inc(s_clear, 1)
            pool.memset(v_causal_pad[:, :, HD:], 0.0).then_inc(s_clear, 1)
            pool.memset(neg_piece[:, :, :, :], BIG).then_inc(s_clear, 1)
            pool.memset(w_gate[:, EXPERTS:], 0.0).then_inc(s_clear, 1)
            pool.memset(out_t[:, 1, :], 1.0).then_inc(s_clear, 1)
            pool.wait_ge(s_clear, 6)
            pool.memset(v_cos_pad[:, :, :, HD:HD + 1], 1.0).then_inc(s_clear, 1)
            pool.memset(v_causal_pad[:, :, HD:HD + 1], 1.0).then_inc(s_clear, 1)
            pool.wait_ge(s_clear, 8)
            for n, t in enumerate((q_cos_t, k_cos_t, *q_causal_t)):
                pool.memset(t[64:P, :, :], 0.0).then_inc(s_rows, 1)
                pool.wait_ge(s_rows, n + 1)
            for n, t in enumerate(k_causal_t):
                pool.memset(t[64:P, :], 0.0).then_inc(s_rows, 1)
                pool.wait_ge(s_rows, n + 5)
            for n, t in enumerate(k_causal_t):
                pool.memset(t[BIAS_ROW:BIAS_ROW + 1, :], 1.0).then_inc(s_clear, 1)
                pool.wait_ge(s_clear, n + 9)
            pool.wait_ge(s_rope_t, 32)

            with pool.Fori(0, CHUNKS) as c:
                pool.wait_ge(s_rin, c + 1)
                pool.wait_ge(s_lo, 2 * c + LO_CREDIT)
                heads = CT * ROPE_HEADS
                table = ds((c % 2) * CT * HD, CT * HD)
                cos_c = cos_t[:, table].rearrange("p (t d) -> p t d", t=CT)
                sin_c = sin_t[:, table].rearrange("p (t d) -> p t d", t=CT)
                r_in = rope_in.rearrange("p (t h d) -> p t h d", t=CT, d=HD)
                r_a = rope_a.rearrange("p (t h d) -> p t h d", t=CT, d=HD)
                r_b = rope_b.rearrange("p (t h d) -> p t h d", t=CT, d=HD)
                half = HD // 2
                pool.tensor_tensor(r_a, r_in, cos_c.unsqueeze(2).to_broadcast([P, CT, ROPE_HEADS, HD]),
                                   ALU.mult).then_inc(s_rope, 1)
                for to, of in ((0, half), (half, 0)):
                    pool.tensor_tensor(r_b[:, :, :, to:to + half], r_in[:, :, :, of:of + half],
                                       sin_c[:, :, to:to + half].unsqueeze(2)
                                       .to_broadcast([P, CT, ROPE_HEADS, half]), ALU.mult).then_inc(s_rope, 1)
                pool.wait_ge(s_rope, 4 * c + 3)
                pool.tensor_tensor(rope_a, rope_a, rope_b, ALU.add).then_inc(s_rope, 1)
                for n, (flat, count) in enumerate(((parts_cos, CT * QK_HEADS), (parts_rope, CT * ROPE_HEADS))):
                    pool.wait_ge(s_hi, 2 * c + (n + 1))
                    words = flat[:, ds(c * (count * HEAD_COLS), count * HEAD_COLS)].bitcast(F32)\
                        .rearrange("p (h w) -> p h w", w=HEAD_COLS // 2)
                    pool.tensor_copy(words[:, :, 3 * HD // 2:], words[:, :, 0:HD // 2]).then_inc(s_again, 1)

            with pool.Fori(0, ITERS) as it:
                b, g = it // GROUPS, it % GROUPS
                pool.wait_ge(s_pv, it * (2 * SEQ_TILES) + (TILE_CREDIT - SEQ_TILES))
                src = v_cos[:, ds(b * (SEQ_TILES * DIM) + g * (GROUP * HD), SEQ_TILES * DIM - (GROUPS - 1) * GROUP * HD)]
                for t in range(SEQ_TILES):
                    one = src[:, t * DIM:t * DIM + GROUP * HD].rearrange("p (h d) -> p h d", h=GROUP)
                    ins = pool.tensor_copy(v_cos_pad[:, t, :, 0:HD], one)
                ins.then_inc(s_va, 1)
                pool.wait_ge(s_pv, it * (2 * SEQ_TILES) + TILE_CREDIT)
                width = KV_HEADS * HD
                src = v_causal[:, ds(b * (SEQ_TILES * width) + g * HD, SEQ_TILES * width - (KV_HEADS - 1) * HD)]
                for t in range(SEQ_TILES):
                    ins = pool.tensor_copy(v_causal_pad[:, t, 0:HD], src[:, t * width:t * width + HD])
                ins.then_inc(s_vb, 1)
                pool.wait_ge(s_free, it * JOBS + (FIRST_JOBS + len(COS_JOBS) + CAUSAL_JOBS.index(("out_cos", 1, 0)) + 3))
                tokens, heads = ds(b * SEQ_TILES, SEQ_TILES), ds(g * (GROUP * HD), GROUP * HD)
                x_heads = x_tok[:, :].rearrange("p (t d) -> p t d", d=DIM)[:, tokens, heads]
                pool.tensor_tensor(x_heads, x_heads, att_cos[:, :, :], ALU.add).then_inc(s_f1["sum"], 1)

            pool.wait_ge(s_f1["sum"], ITERS + 1)
            for c in range(CHUNKS):
                chunk = slice(c * CHUNK, (c + 1) * CHUNK)
                pool.wait_ge(s_f1["x1"], c + 1)
                pool.tensor_tensor(x_tok[:, chunk], x_tok[:, chunk], xn[:, chunk], ALU.add).then_inc(s_f1["y"], 1)

        @block.scalar
        def _(act):
            for n, (dst, src) in enumerate((
                    (w_qk[:, 0:128], wq_cos), (w_qk[:, 128:256], wk_cos), (w_qk[:, 256:384], wq),
                    (w_qk[:, 384:416], wk), (w_v[:, 0:128], wv_cos), (w_v[:, 128:160], wv))):
                act.dma_start(dst, src).then_inc(s_wqkv, 16)
            act.wait_ge(s_stats, 1)
            act.wait_ge(s_const, 10)
            act.activation(roots[:, :, :], roots[:, :, :], ACT.Sqrt).then_inc(s_root0, 1)

            def load_table(n, func):
                act.activation(unused[:, n:n + 1], ident[:, 0:1], func)

            def copy_xt(c):
                act.wait_ge(s_xt_ps, c + 1)
                act.wait_ge(s_proj, c + 1)
                act.activation(xn_t, ps[:, 6, :], ACT.Copy).then_inc(s_xt, 1)

            def save_xn(c):
                act.wait_ge(s_xn, CT * c + CT)
                act.activation(xn[:, ds(c * CHUNK, CHUNK)], xn_stage, ACT.Copy).then_inc(s_xn_saved, 1)

            def project_chunk(c, more):
                act.wait_ge(s_proj, c + 2)
                act.wait_ge(s_lo, 2 * c + LO_CREDIT)
                act.activation(unit.rearrange("p (t n) -> p t n", t=CT), ps[:, 0:CT, 0:QK_COLS], ACT.Copy).then_inc(s_qk, 1)
                if more:
                    copy_xt(c + 1)
                v_ps = ps[:, 4:6, 0:2 * V_COLS].rearrange("p b (t n) -> p b t n", t=2)
                act.activation(v_cos[:, ds(c * CHUNK, CHUNK)].rearrange("p (b t n) -> p b t n", b=2, t=2),
                               v_ps[:, :, :, 0:DIM], ACT.Copy).then_inc(s_vc, 1)
                act.wait_ge(s_qk, c + 1)
                act.wait_ge(s_nsq, c + 1)
                act.activation(squares, unit, ACT.Square).then_inc(s_sq, 1)
                if more:
                    save_xn(c + 1)
                act.wait_ge(s_nsq, c + 2)
                act.activation(norms, norms, ACT.Sqrt).then_inc(s_nroot, 1)
                a_parts = parts_cos[:, ds(c * (CT * QK_HEADS * HEAD_COLS), CT * QK_HEADS * HEAD_COLS)]\
                    .rearrange("p (h s d) -> p h s d", s=PARTS, d=HD)
                r_parts = parts_rope[:, ds(c * (CT * ROPE_HEADS * HEAD_COLS), CT * ROPE_HEADS * HEAD_COLS)]\
                    .rearrange("p (h s d) -> p h s d", s=PARTS, d=HD)
                unit_h = unit.rearrange("p (h d) -> p h d", d=HD)
                rope_h = rope_a.rearrange("p (h d) -> p h d", d=HD)
                act.wait_ge(s_res, 3 * c + (RES_CREDIT + 1))
                act.activation(a_parts[:, :, 0, :], unit_h, ACT.Copy).then_inc(s_hi, 1)
                act.wait_ge(s_rope, 4 * c + 4)
                act.activation(r_parts[:, :, 0, :], rope_h, ACT.Copy).then_inc(s_hi, 1)
                act.wait_ge(s_res, 3 * c + (RES_CREDIT + 2))
                act.activation(a_parts[:, :, 1, :], unit_h, ACT.Copy).then_inc(s_mid, 1)
                act.wait_ge(s_res, 3 * c + (RES_CREDIT + 3))
                act.activation(r_parts[:, :, 1, :], rope_h, ACT.Copy).then_inc(s_mid, 1)

            copy_xt(0)
            save_xn(0)
            with act.Fori(0, CHUNKS // 2) as c:
                project_chunk(c, more=True)
            for c in range(CHUNKS // 2, CHUNKS):
                project_chunk(c, more=c < CHUNKS - 1)

            def exp_steps(it, first, last):
                for n, (j, h, heads) in list(enumerate(COS_STEPS + CAUSAL_STEPS))[first:last]:
                    causal = n >= len(COS_STEPS)
                    tile = j + SEQ_TILES * causal
                    if h == 0:
                        act.wait_ge(s_pv, it * (2 * SEQ_TILES) + (tile - 1 + TILE_CREDIT))
                    act.wait_ge(s_sc, it * STEPS + (n + 2))
                    start = j * P if causal else 0
                    act.activation(probs[:, j % 2, h:h + heads, start:SEQ], step_view(n, j, heads, causal),
                                   ACT.Exp).then_inc(s_pr, 1)

            load_table(0, ACT.Exp)
            exp_steps(0, 0, TURN)
            with act.Fori(0, ITERS - 1) as it:
                exp_steps(it, TURN, STEPS)
                exp_steps(it + 1, 0, TURN)
            exp_steps(ITERS - 1, TURN, STEPS)
            load_table(1, ACT.Sqrt)

            def copy_attention(c):
                act.wait_ge(s_f1["t_ps"], c + 1)
                if c >= 2:
                    act.wait_ge(s_f1["wo"], c - 1)
                act.activation(att_t[c % 2], ps[:, c % 2, :], ACT.Copy).then_inc(s_f1["t"], 1)

            def square(c):
                act.wait_ge(s_f1["x1"], c + 1)
                if c >= 2:
                    act.wait_ge(s_f1["ssq"], c - 1)
                act.activation(f_stage[c % 2], xn[:, c * CHUNK:(c + 1) * CHUNK], ACT.Square).then_inc(s_f1["sq"], 1)

            for c in range(CHUNKS):
                copy_attention(c)
                if c:
                    square(c - 1)
            square(CHUNKS - 1)
            act.wait_ge(s_f2["ms"], 1)
            act.activation(sum_sq[:, :], sum_sq[:, :], ACT.Sqrt).then_inc(s_f2["root"], 1)
            for c in range(CHUNKS):
                act.wait_ge(s_f2["t_ps"], c + 1)
                act.activation(xf_t[:, c * CHUNK:(c + 1) * CHUNK], ps[:, 4 + c % 2, :], ACT.Copy,
                               scale=g2_col[:, :]).then_inc(s_f2["t"], 1)
            load_table(2, ACT.Exp)
            act.wait_ge(s_f2["gate"], CHUNKS)
            act.activation(att_t[0], ps[:, 7, :], ACT.Copy).then_inc(s_f2["logits"], 1)
            act.wait_ge(s_f2["dve"], 2)
            act.activation(g_exp[:, :, :], logits[:, :, :], ACT.Exp).then_inc(s_f2["exp"], 1)
            with act.Fori(0, CHUNKS) as c:
                for k in range(EXPERTS * HT):
                    act.wait_ge(s_f3["up"], c * (EXPERTS * HT) + (k + 1))
                    act.wait_ge(s_f3["h"], c * (EXPERTS * HT) + (k + 1))
                    act.activation(gated[k % 2], ps[:, k % 2, :], ACT.Silu).then_inc(s_f3["silu"], 1)

        @block.vector
        def _(dve):
            step0 = [0]

            def link(ins):
                step0[0] += 1
                ins.then_inc(s_dve0, 1)
                dve.wait_ge(s_dve0, step0[0])

            for s, n in ((s_proj, 1), (s_read, 1), (s_nsq, 1), (s_lo, LO_CREDIT), (s_res, RES_CREDIT), (s_sc, 1), (s_pr, 2), (s_pv, TILE_CREDIT),
                         (s_free, 2), (s_accfree, 2), (s_f1["sum"], 1), (s_f3["h"], 2), (s_f3["y"], 2), (s_f3["y_used"], 2)):
                dve.sem_inc(s, n)
            for name, n in LAID.items():
                dve.sem_inc(s_laid[name], n)

            dve.memset(parts_rope[:, TILES * ROPE_HEADS * HEAD_COLS:], 0.0).then_inc(s_clear, 1)

            for t in range(TILES):
                dve.wait_ge(s_x[t // CT], 16)
                ins = dve.bn_stats(stat[:, t, :], x_tok[:, t * DIM:(t + 1) * DIM])
            link(ins)
            dve.tensor_tensor(s_mean[:, :], stat[:, :, 1], stat[:, :, 4], ALU.add).then_inc(s_dve0, 1)
            dve.tensor_tensor(s_diff[:, :], stat[:, :, 1], stat[:, :, 4], ALU.subtract).then_inc(s_dve0, 1)
            step0[0] += 2
            link(dve.tensor_tensor(s_var[:, :], stat[:, :, 2], stat[:, :, 5], ALU.add))
            link(dve.tensor_tensor(s_diff[:, :], s_diff[:, :], s_diff[:, :], ALU.mult))
            link(dve.scalar_tensor_tensor(out=s_var[:, :], in0=s_diff[:, :], scalar=DIM / 4.0, in1=s_var[:, :],
                                          op0=ALU.mult, op1=ALU.add))
            dve.tensor_scalar(s_mean[:, :], s_mean[:, :], 0.5, None, ALU.mult).then_inc(s_dve0, 1)
            step0[0] += 1
            link(dve.tensor_scalar(roots[:, 0, :], s_var[:, :], 1.0 / DIM, LN_EPS, ALU.mult, ALU.add))
            link(dve.reciprocal(roots[:, 1, :], roots[:, 0, :]))
            link(dve.tensor_tensor(roots[:, 1, :], roots[:, 1, :], s_var[:, :], ALU.mult))
            dve.tensor_scalar(roots[:, 1, :], roots[:, 1, :], 1.0 / DIM, RMS_EPS, ALU.mult, ALU.add).then_inc(s_stats, 1)
            dve.wait_ge(s_root0, 1)
            link(dve.reciprocal(scales[:, :, :], roots[:, :, :]))

            def stage_xn(c):
                for t in range(CT):
                    dve.tensor_scalar(xn_stage[:, t * DIM:(t + 1) * DIM],
                                      x_tok[:, ds(c * CHUNK + t * DIM, DIM)],
                                      s_mean[:, ds(c * CT + t, 1)], scales[:, 0, ds(c * CT + t, 1)],
                                      ALU.subtract, ALU.mult).then_inc(s_xn, 1)

            def project_chunk(c, ahead):
                r1 = scales[:, 1, ds(c * CT, CT)]
                dve.wait_ge(s_qk, c + 1)
                dve.tensor_tensor(rope_in.rearrange("p (t n) -> p t n", t=CT), ps[:, 0:CT, QK_COLS:QK_COLS + ROPE_COLS],
                                  r1.unsqueeze(2).to_broadcast([P, CT, ROPE_COLS]), ALU.mult).then_inc(s_rin, 1)
                v_ps = ps[:, 4:6, 0:2 * V_COLS].rearrange("p b (t n) -> p b t n", t=2)
                dve.wait_ge(s_vc, c + 1)
                dve.tensor_tensor(v_causal[:, ds(c * (CT * KV_HEADS * HD), CT * KV_HEADS * HD)]
                                  .rearrange("p (b t n) -> p b t n", b=2, t=2), v_ps[:, :, :, DIM:V_COLS],
                                  r1.rearrange("p (b t) -> p b t", b=2).unsqueeze(3)
                                  .to_broadcast([P, 2, 2, KV_HEADS * HD]), ALU.mult).then_inc(s_read, 1)
                dve.wait_ge(s_sq, c + 1)
                dve.tensor_reduce(norms, squares.rearrange("p (h d) -> p h d", d=HD), AX.X, ALU.add)\
                   .then_inc(s_nsq, 1)
                dve.wait_ge(s_nroot, c + 1)
                dve.tensor_scalar(norms, norms, NORM_EPS, None, ALU.max).then_inc(s_dve1, 1)
                dve.wait_ge(s_dve1, 3 * c + 1)
                dve.reciprocal(inv_norms, norms).then_inc(s_dve1, 1)
                dve.wait_ge(s_dve1, 3 * c + 2)
                inv_q = inv_norms.rearrange("p (t h) -> p t h", t=CT)[:, :, 0:HEADS]
                dve.tensor_scalar(inv_q, inv_q, g_col[:, :], None, ALU.mult).then_inc(s_dve1, 1)
                dve.wait_ge(s_dve1, 3 * c + 3)
                dve.tensor_tensor(unit.rearrange("p (t h d) -> p t h d", t=CT, d=HD),
                                  unit.rearrange("p (t h d) -> p t h d", t=CT, d=HD),
                                  inv_norms.rearrange("p (t h) -> p t h", t=CT).unsqueeze(3)
                                  .to_broadcast([P, CT, QK_HEADS, HD]), ALU.mult).then_inc(s_res, 1)
                if ahead:
                    dve.wait_ge(s_xn_saved, c + 2)
                    dve.wait_ge(s_xt_ps, c + 2)
                    stage_xn(c + 2)
                a_parts = parts_cos[:, ds(c * (CT * QK_HEADS * HEAD_COLS), CT * QK_HEADS * HEAD_COLS)]\
                    .rearrange("p (h s d) -> p h s d", s=PARTS, d=HD)
                r_parts = parts_rope[:, ds(c * (CT * ROPE_HEADS * HEAD_COLS), CT * ROPE_HEADS * HEAD_COLS)]\
                    .rearrange("p (h s d) -> p h s d", s=PARTS, d=HD)
                unit_h = unit.rearrange("p (h d) -> p h d", d=HD)
                rope_h = rope_a.rearrange("p (h d) -> p h d", d=HD)
                dve.wait_ge(s_hi, 2 * c + 1)
                dve.tensor_tensor(unit_h, unit_h, a_parts[:, :, 0, :], ALU.subtract).then_inc(s_res, 1)
                dve.wait_ge(s_hi, 2 * c + 2)
                dve.tensor_tensor(rope_h, rope_h, r_parts[:, :, 0, :], ALU.subtract).then_inc(s_res, 1)
                dve.wait_ge(s_mid, 2 * c + 1)
                dve.tensor_tensor(a_parts[:, :, 2, :], unit_h, a_parts[:, :, 1, :], ALU.subtract).then_inc(s_lo, 1)
                dve.wait_ge(s_mid, 2 * c + 2)
                dve.tensor_tensor(r_parts[:, :, 2, :], rope_h, r_parts[:, :, 1, :], ALU.subtract).then_inc(s_lo, 1)
                dve.wait_ge(s_lo, 2 * c + (LO_CREDIT + 2))

            def empty_slot(base, index, kind, a, b, it):
                k = index % 2
                dve.wait_ge(s_fill, base + (index + 1))
                if kind in ("cos", "query", "key"):
                    name = ("q_cos", "k_cos")[a] if kind == "cos" else kind
                    rows = HEAD_COLS if kind == "key" else P
                    dve.wait_ge(s_laid[name], (it + 1) * LAID[name])
                    dve.tensor_copy(parts_t[name][0:rows, :], aux_b[k][0:rows, :]).then_inc(s_free, 1)
                elif kind == "neg_max":
                    dve.wait_ge(s_laid[f"neg_max{a}"], (it + 1) * LAID[f"neg_max{a}"])
                    dve.tensor_copy(neg_max_t[:, a, :], aux_b[k][0:2 * SEQ_TILES, 0:P]).then_inc(s_free, 1)
                elif kind == "max":
                    t, piece, width, h, heads = b
                    dve.tensor_reduce(neg_piece[:, h:h + heads, t, piece],
                                      aux[k][:, 0:heads * width].rearrange("p (h n) -> p h n", h=heads), AX.X, ALU.max,
                                      negate=True).then_inc(s_free, 1)

            def normalise(base, index, step, att, tile, g):
                dst = att[:, ds(tile, CT), ds(g * (GROUP * HD), GROUP * HD)].rearrange("p t (h d) -> p t h d", h=GROUP)
                k = index % 2
                o = aux[k].rearrange("p (t h d) -> p t h d", t=CT, h=GROUP)
                dve.wait_ge(s_fill, base + (index + 1))
                dve.reciprocal(recip[:, k, :, :], o[:, :, :, HD]).then_inc(s_norm, 1)
                dve.wait_ge(s_norm, step)
                dve.tensor_tensor(dst, o[:, :, :, 0:HD],
                                  recip[:, k, :, :].unsqueeze(3).to_broadcast([P, CT, GROUP, HD]),
                                  ALU.mult).then_inc(s_free, 1)

            def zero_masked(it, i):
                j, h, heads = CAUSAL_STEPS[i]
                diagonal = probs[:, j % 2, h:h + heads, j * P:(j + 1) * P]
                dve.wait_ge(s_pr, it * STEPS + (len(COS_STEPS) + i + 3))
                dve.tensor_tensor(diagonal, diagonal, keep[:, :].unsqueeze(1).to_broadcast([P, heads, P]),
                                  ALU.min).then_inc(s_zeroed, 1)

            def copy_acc(which, half, it):
                if half == 0:
                    dve.wait_ge(s_accdone, it * 2 + (which + 1))
                else:
                    dve.wait_ge(s_pv, it * (2 * SEQ_TILES) + ((which + 1) * SEQ_TILES + TILE_CREDIT))
                dve.tensor_copy(out_t[:, which, half * BANK:(half + 1) * BANK], acc[:, half, :]).then_inc(s_accfree, 1)

            stage_xn(0)
            dve.wait_ge(s_wqkv, 96)
            dve.wait_ge(s_small, 48)
            dve.tensor_scalar(w_qk[:, 256:384], w_qk[:, 256:384], g1_col[:, :], float(HD) ** -0.5,
                              ALU.mult, ALU.mult).then_inc(s_wscaled, 1)
            dve.tensor_scalar(w_qk[:, 384:416], w_qk[:, 384:416], g1_col[:, :], None, ALU.mult).then_inc(s_wscaled, 1)
            dve.tensor_scalar(w_v[:, DIM:V_COLS], w_v[:, DIM:V_COLS], g1_col[:, :], None, ALU.mult)\
               .then_inc(s_wscaled, 1)
            dve.wait_ge(s_xn_saved, 1)
            dve.wait_ge(s_xt_ps, 1)
            stage_xn(1)
            with dve.Fori(0, CHUNKS // 2) as c:
                project_chunk(c, ahead=True)
            for n, (kind, a, piece) in enumerate(FIRST[:4]):
                if n == 2:
                    project_chunk(CHUNKS - 2, ahead=False)
                empty_slot(0, n, kind, a, piece, 0)
            project_chunk(CHUNKS - 1, ahead=False)
            for n, (kind, a, piece) in list(enumerate(FIRST))[4:]:
                empty_slot(0, n, kind, a, piece, 0)
            with dve.Fori(0, ITERS) as it:
                base = it * JOBS
                b, g = it // GROUPS, it % GROUPS
                last_b, last_g = ((it + (ITERS - 1)) % ITERS) // GROUPS, ((it + (ITERS - 1)) % ITERS) % GROUPS
                for n, (kind, a, piece) in enumerate(COS_JOBS):
                    if kind == "out_causal":
                        normalise(base, FIRST_JOBS + n, it * 4 + 1, att_causal,
                                  last_b * SEQ_TILES + a * CT, last_g)
                    else:
                        empty_slot(base, FIRST_JOBS + n, kind, a, piece, it + 1 if kind in OF_NEXT else it)
                    if kind == "max" and piece == MAXIMA[a][-1]:
                        dve.wait_ge(s_free, base + (FIRST_JOBS + n + 1 + 2))
                        dve.tensor_tensor(neg_max[:, 2 * a:2 * a + 2, :], neg_piece[:, 2 * a:2 * a + 2, :, 0],
                                          neg_piece[:, 2 * a:2 * a + 2, :, 1], ALU.min).then_inc(s_negmax, 1)
                done = 0
                for i in range(len(CAUSAL_STEPS)):
                    if i in (2, 4):
                        copy_acc(0, i // 2 - 1, it)
                    elif i == 18:
                        copy_acc(1, 0, it)
                    for n in range(done, CAUSAL_ISSUED[i]):
                        kind, a, piece = CAUSAL_JOBS[n]
                        index = FIRST_JOBS + len(COS_JOBS) + n
                        if kind == "out_cos":
                            dve.wait_ge(s_f1["sum"], it + 1)
                            normalise(base, index, it * 4 + (a + 2), att_cos, a * CT, 0)
                        elif kind == "out_causal":
                            normalise(base, index, it * 4 + 4, att_causal, b * SEQ_TILES, g)
                        else:
                            empty_slot(base, index, kind, a, piece, it + 1)
                    done = CAUSAL_ISSUED[i]
                    if i < ZEROED_STEPS:
                        zero_masked(it, i)
                copy_acc(1, 1, it)

            def add_attention(c):
                chunk = slice(c * CHUNK, (c + 1) * CHUNK)
                dve.wait_ge(s_f1["wo"], c + 1)
                dve.tensor_tensor(xn[:, chunk], xn[:, chunk], ps[:, 2 + c % 2, :], ALU.add).then_inc(s_f1["x1"], 1)

            def sum_squares(c):
                dve.wait_ge(s_f1["sq"], c + 1)
                dve.tensor_reduce(sum_sq[:, c * CT:(c + 1) * CT], f_stage[c % 2].rearrange("p (t d) -> p t d", t=CT),
                                  AX.X, ALU.add).then_inc(s_f1["ssq"], 1)

            add_attention(0)
            add_attention(1)
            normalise(ITERS * JOBS, FIRST_JOBS, ITERS * 4 + 1, att_causal, (BATCH - 1) * SEQ_TILES + CT, GROUPS - 1)
            sum_squares(0)
            add_attention(2)
            sum_squares(1)
            add_attention(3)
            sum_squares(2)
            sum_squares(3)
            dve.wait_ge(s_f1["ssq"], CHUNKS)
            dve.tensor_scalar(sum_sq[:, :], sum_sq[:, :], 1.0 / DIM, RMS_EPS, ALU.mult, ALU.add)\
               .then_inc(s_f2["ms"], 1)
            dve.wait_ge(s_f2["root"], 1)
            dve.reciprocal(s_var[:, :], sum_sq[:, :]).then_inc(s_f2["r2"], 1)
            dve.wait_ge(s_f2["r2"], 1)

            for c in range(CHUNKS):
                if c >= 2:
                    dve.wait_ge(s_f2["t_ps"], c - 1)
                dve.tensor_tensor(f_stage[c % 2].rearrange("p (t d) -> p t d", t=CT),
                                  xn[:, c * CHUNK:(c + 1) * CHUNK].rearrange("p (t d) -> p t d", t=CT),
                                  s_var[:, c * CT:(c + 1) * CT].unsqueeze(2).to_broadcast([P, CT, DIM]), ALU.mult)\
                   .then_inc(s_f2["xs"], 1)
            dve.wait_ge(s_f2["logits_ps"], 1)
            logits_ps = ps[:, 6, :].rearrange("p (t c n) -> p c t n", t=CT, c=CHUNKS)[:, :, :, 0:EXPERTS]

            steps2 = [0]

            def link2(ins):
                steps2[0] += 1
                ins.then_inc(s_f2["dve"], 1)
                dve.wait_ge(s_f2["dve"], steps2[0])

            g_max = g_cmp[:, 0, :]
            by_chunk = "p (c t) -> p c t"
            link2(dve.tensor_reduce(g_max.rearrange(by_chunk, c=CHUNKS), logits_ps, AX.X, ALU.max))
            link2(dve.tensor_tensor(logits[:, :, :].rearrange("p (c t) e -> p c t e", c=CHUNKS), logits_ps,
                                    g_max.rearrange(by_chunk, c=CHUNKS).unsqueeze(3)
                                    .to_broadcast([P, CHUNKS, CT, EXPERTS]), ALU.subtract))
            link2(dve.memset(g_rank[:, :, :], 0.0))

            pairs = [(i, j) for i in range(EXPERTS) for j in range(i + 1, EXPERTS)]

            def compare():
                dve.wait_ge(s_f2["exp"], 1)
                for n, (i, j) in enumerate(pairs):
                    ins = dve.tensor_tensor(g_cmp[:, n, :], g_exp[:, :, i], g_exp[:, :, j], ALU.is_ge)
                link2(ins)

            def rank(first, last):
                for n, (i, j) in list(enumerate(pairs))[first:last]:
                    link2(dve.tensor_tensor(g_rank[:, :, j], g_rank[:, :, j], g_cmp[:, n, :], ALU.add))
                    link2(dve.tensor_tensor(g_rank[:, :, i], g_rank[:, :, i], g_cmp[:, n, :], ALU.subtract))

            def weigh():
                for i in range(EXPERTS):
                    ins = dve.tensor_scalar(g_rank[:, :, i], g_rank[:, :, i], float(EXPERTS - 1 - i), 2.0,
                                            ALU.add, ALU.is_lt)
                link2(ins)
                link2(dve.tensor_tensor(g_exp[:, :, :], g_exp[:, :, :], g_rank[:, :, :], ALU.mult))
                link2(dve.tensor_reduce(g_max, g_exp[:, :, :], AX.X, ALU.add))
                link2(dve.reciprocal(g_max, g_max))
                link2(dve.tensor_tensor(comb[:, :].rearrange("p (t e) -> p t e", t=TILES), g_exp[:, :, :],
                                        g_max.unsqueeze(2).to_broadcast([P, TILES, EXPERTS]), ALU.mult))

            def weight_part(k):
                if k == 0:
                    compare()
                elif k <= 3:
                    rank(2 * k - 2, 2 * k)
                elif k == 4:
                    weigh()

            dve.wait_ge(s_f1["y"], CHUNKS)

            def chunk_experts(c, first):
                def add_expert(e):
                    dve.wait_ge(s_f3["y"], c * EXPERTS + (e + 3))
                    if e:
                        dve.wait_ge(s_f3["y_used"], c * EXPERTS + (e + 2))
                    for t in range(CT):
                        acc_t = x_tok[:, ds(c * CHUNK + t * DIM, DIM)]
                        ins = dve.scalar_tensor_tensor(
                            out=acc_t, in0=ps[:, 4 + e % 2, t * DIM:(t + 1) * DIM],
                            scalar=comb[:, ds(c * (CT * EXPERTS) + (t * EXPERTS + e), 1)], in1=acc_t,
                            op0=ALU.mult, op1=ALU.add)
                    ins.then_inc(s_f3["y_used"], 1)

                for e in range(EXPERTS):
                    for h in range(HT):
                        k = e * HT + h
                        dve.wait_ge(s_f3["silu"], c * (EXPERTS * HT) + (k + 1))
                        if h == 0:
                            dve.wait_ge(s_f3["y"], c * EXPERTS + (e + 1))
                        dve.tensor_tensor(hidden[e % 2][:, h, :], gated[k % 2], ps[:, 2 + k % 2, :], ALU.mult)\
                           .then_inc(s_f3["h"], 1)
                        if first:
                            weight_part(k)
                    if e:
                        add_expert(e - 1)
                add_expert(EXPERTS - 1)

            chunk_experts(0, first=True)
            with dve.Fori(1, CHUNKS) as c:
                chunk_experts(c, first=False)

        @block.tensor
        def _(pe):
            pe.wait_ge(s_const, 10)
            def transpose_xn(c):
                pe.wait_ge(s_xn, CT * c + CT)
                for t in range(CT):
                    ins = pe.transpose(ps[:, 6, t * P:(t + 1) * P], xn_stage[:, t * DIM:(t + 1) * DIM], ident[:, :])
                ins.then_inc(s_xt_ps, 1)

            def project_chunk(c):
                pe.wait_ge(s_xt, c + 1)
                pe.wait_ge(s_read, c + 1)
                for t in range(CT):
                    pe.matmul(ps[:, t, 0:QK_COLS + ROPE_COLS], xn_t[:, t * P:(t + 1) * P], w_qk[:, :],
                              start=True, stop=True)
                for t in range(CT):
                    v_out = ps[:, 4 + t // 2, (t % 2) * V_COLS:(t % 2 + 1) * V_COLS]
                    ins = pe.matmul(v_out, xn_t[:, t * P:(t + 1) * P], w_v[:, :], start=True, stop=True)
                ins.then_inc(s_proj, 1)

            def aux_job(base, index, kind, a, b, batch, group, parity=0):
                k = index % 2
                pe.wait_ge(s_free, base + (index + 1))
                if kind in ("cos", "query", "key"):
                    if kind == "cos":
                        flat, heads, first, step = parts_cos, QK_HEADS, a * HEADS, GROUP
                    elif kind == "query":
                        flat, heads, first, step = parts_rope, ROPE_HEADS, 0, GROUP
                    else:
                        flat, heads, first, step = parts_rope, ROPE_HEADS, HEADS, 1
                    for t in range(SEQ_TILES):
                        src = flat[:, ds(batch * (SEQ_TILES * heads * HEAD_COLS) + group * (step * HEAD_COLS)
                                         + (t * heads + first) * HEAD_COLS, P)]
                        ins = pe.transpose(aux_b[k][:, t * P:(t + 1) * P], src, ident_b[:, :])
                elif kind == "neg_max":
                    ins = pe.transpose(aux_b[k][0:2 * SEQ_TILES, 0:P],
                                       neg_max[:, 2 * a:2 * a + 2, :].rearrange("p h t -> p (h t)"), ident_b[:, :])
                elif kind == "max":
                    t, piece, width, h, heads = b
                    for i in range(heads):
                        ins = pe.matmul(aux[k][:, i * width:(i + 1) * width],
                                        q_causal_t[parity][0:BIAS_ROW, h + i, t * P:(t + 1) * P],
                                        k_causal_t[parity][0:BIAS_ROW, piece * BANK:piece * BANK + width],
                                        start=i == 0, stop=True, skip_group_check=True)
                        if piece == t // 4:
                            ins = pe.matmul(aux[k][:, (i + 1) * width - P:(i + 1) * width], ident_b[:, :], mask_q[:, :],
                                            start=False, stop=True, skip_group_check=True)
                else:
                    which = int(kind == "out_causal")
                    for t in range(CT):
                        lo = (a * CT + t) * P
                        ins = pe.transpose(aux[k][:, t * P:(t + 1) * P], out_t[:, which, lo:lo + P], ident[:, :])
                ins.then_inc(s_fill, 1)

            def scores(n, j, h, heads, causal, parity):
                s = slot(n)
                for i in range(heads):
                    if causal:
                        width = SEQ - j * P
                        keys, queries = k_causal_t[parity][:, j * P:(j + 1) * P], q_causal_t[parity][:, h + i, :]
                        place = j * P if heads == 1 else (i * BANK if heads == 2 else i * width)
                    else:
                        width, place = SEQ, 0
                        keys, queries = k_cos_t[:, h, j * P:(j + 1) * P], q_cos_t[:, h, :]
                    done = 0
                    while done < width:
                        at = place + done
                        n_cols = min(width - done, BANK - at % BANK)
                        q0 = SEQ - width + done
                        first = at % BANK == 0 or i == 0 or heads == 2
                        ins = pe.matmul(s[:, at:at + n_cols], keys, queries[:, q0:q0 + n_cols], start=first,
                                        stop=True, skip_group_check=True)
                        if causal and done == 0 and j >= 6:
                            ins = pe.matmul(s[:, at:at + P], ident_b[:, :], mask_k[:, :], start=False, stop=True,
                                            skip_group_check=True)
                        done += n_cols
                ins.then_inc(s_sc, 1)

            def values(j, half, causal):
                lo, hi = max(half * BANK, j * P if causal else 0), (half + 1) * BANK
                at = lo - half * BANK
                for h in range(GROUP):
                    v = v_causal_pad[:, j, :] if causal else v_cos_pad[:, j, h, :]
                    ins = pe.matmul(acc[32 * h:32 * h + 32, half, at:at + hi - lo], v, probs[:, j % 2, h, lo:hi],
                                    start=(j == 0 and at == 0), stop=True, skip_group_check=True)
                return ins

            def score_step(n, it_first, exps, cos_laid, parity):
                causal = len(COS_STEPS) <= n < STEPS
                j, h, heads = (COS_STEPS + CAUSAL_STEPS)[n % STEPS]
                if j == h == 0 and not causal:
                    pe.wait_ge(s_laid["q_cos"], it_first * LAID["q_cos"] + cos_laid * LAID["q_cos"])
                    pe.wait_ge(s_laid["k_cos"], it_first * LAID["k_cos"] + cos_laid * LAID["k_cos"])
                if j == 0 and causal and h in (0, 2):
                    name = f"neg_max{h // 2}"
                    pe.wait_ge(s_laid[name], it_first * LAID[name] + 2 * LAID[name])
                pe.wait_ge(s_pr, exps)
                scores(n, j, h, heads, causal, parity)

            def wait_causal_laid(count):
                for name in ("key", "query"):
                    pe.wait_ge(s_laid[name], count * LAID[name])

            transpose_xn(0)
            pe.wait_ge(s_wscaled, 3)
            with pe.Fori(0, CHUNKS // 2) as c:
                project_chunk(c)
                transpose_xn(c + 1)
            for c in range(CHUNKS // 2, CHUNKS):
                project_chunk(c)
                if c == CHUNKS // 2:
                    pe.wait_ge(s_again, 2 * c)
                    pe.wait_ge(s_lo, 2 * c + LO_CREDIT)
                    aux_job(0, 0, *FIRST[0], 0, 0)
                    aux_job(0, 1, *FIRST[1], 0, 0)
                    pe.wait_ge(s_free, 3)
                    transpose_xn(c + 1)
            aux_job(0, 2, *FIRST[2], 0, 0)
            aux_job(0, 3, *FIRST[3], 0, 0)
            pe.wait_ge(s_clear, 10)
            pe.wait_ge(s_again, 2 * CHUNKS)
            pe.wait_ge(s_lo, 2 * CHUNKS + LO_CREDIT)
            for n in range(2):
                score_step(n, 0, n + 1, 2, 0)
            wait_causal_laid(2)
            for n, (kind, a, piece) in list(enumerate(FIRST))[4:]:
                aux_job(0, n, kind, a, piece, 0, 0)
            def iteration(it, parity):
                batch, group = it // GROUPS, it % GROUPS
                next_batch, next_group = ((it + 1) % ITERS) // GROUPS, ((it + 1) % ITERS) % GROUPS
                base = it * JOBS

                def next_job(n):
                    kind, a, b = (COS_JOBS + CAUSAL_JOBS)[n]
                    if kind == "out_causal":
                        pe.wait_ge(s_accfree, it * 4 + (2 if a else 5))
                    elif kind == "out_cos":
                        pe.wait_ge(s_accfree, it * 4 + (a + 3))
                    elif kind == "max" and b == FIRST_PAIR[0][2]:
                        wait_causal_laid(it + 3)
                    elif kind == "neg_max":
                        pe.wait_ge(s_negmax, it * 2 + (a + 1))
                    of_next = kind in OF_NEXT or n >= len(COS_JOBS) and kind == "max"
                    aux_job(base, FIRST_JOBS + n, kind, a, b,
                            next_batch if of_next else batch, next_group if of_next else group, 1 - parity if of_next else parity)

                def value_half(j, half, causal, steps_done):
                    first = half == (j // CT if causal else 0)
                    if first:
                        pe.wait_ge(s_pr, it * STEPS + (steps_done + 2))
                    if first and j == 0:
                        pe.wait_ge(s_vb if causal else s_va, it + 1)
                    if first and causal and j < 6:
                        pe.wait_ge(s_zeroed, it * ZEROED_STEPS + (steps_done - len(COS_STEPS)))
                    if j == 0:
                        pe.wait_ge(s_accfree, it * 4 + (1 + 2 * causal + half))
                    ins = values(j, half, causal)
                    if half == 1:
                        ins.then_inc(s_pv, 1)
                    if (j, half) == (SEQ_TILES // 2 - 1 if causal else SEQ_TILES - 1, 0):
                        ins.then_inc(s_accdone, 1)

                plan = COS_ISSUED + [len(COS_JOBS) + i for i in CAUSAL_ISSUED] + [JOBS, JOBS]
                tile_of = [step[0] + SEQ_TILES * (n >= len(COS_STEPS)) for n, step in enumerate(COS_STEPS + CAUSAL_STEPS)]
                tile_of += [2 * SEQ_TILES] * 2
                pending, issued = [], 0
                for n in range(2, STEPS + 2):
                    jobs = plan[n] - issued
                    left = tile_of[n:].count(tile_of[n])
                    halves = len(pending) if left == 1 else int(left % 2 == 1 or tile_of.count(tile_of[n]) == len(pending))
                    if jobs >= 2 and not halves:
                        next_job(issued)
                        issued, jobs = issued + 1, jobs - 1
                    score_step(n, it, it * STEPS + (n + 1), 3, parity)
                    for i in range(max(jobs, halves)):
                        if i < jobs:
                            next_job(issued)
                            issued += 1
                        if i < halves:
                            value_half(*pending.pop(0))
                    if left == 1:
                        causal = n >= len(COS_STEPS)
                        j = tile_of[n] % SEQ_TILES
                        pending = [(j, half, causal, n + 1) for half in range(j // CT if causal else 0, 2)]

            def transpose_attention(c):
                if c >= 2:
                    pe.wait_ge(s_f1["t"], c - 1)
                for t in range(CT):
                    ins = pe.transpose(ps[:, c % 2, t * P:(t + 1) * P], att_causal[:, c * CT + t, :], ident[:, :])
                ins.then_inc(s_f1["t_ps"], 1)

            def project_out(c):
                pe.wait_ge(s_f1["t"], c + 1)
                if c >= 2:
                    pe.wait_ge(s_f1["x1"], c - 1)
                for t in range(CT):
                    ins = pe.matmul(ps[:, 2 + c % 2, t * DIM:(t + 1) * DIM], att_t[c % 2][:, t * P:(t + 1) * P],
                                    w_o[:, :], start=True, stop=True)
                ins.then_inc(s_f1["wo"], 1)

            with pe.Fori(0, ITERS // 2) as pair:
                for parity in range(2):
                    iteration(pair * 2 + parity, parity)

            pe.wait_ge(s_w_rest, 80)
            pe.wait_ge(s_pr, ITERS * STEPS + 2)
            transpose_attention(0)
            transpose_attention(1)
            project_out(0)
            project_out(1)
            pe.wait_ge(s_free, ITERS * JOBS + (FIRST_JOBS + 2))
            transpose_attention(2)
            pe.wait_ge(s_accfree, ITERS * 4 + 2)
            aux_job(ITERS * JOBS, FIRST_JOBS, "out_causal", 1, 0, 0, 0)
            project_out(2)
            pe.wait_ge(s_free, ITERS * JOBS + (FIRST_JOBS + 1 + 2))
            transpose_attention(3)
            project_out(3)

            def up(k, count, tokens):
                e, h = divmod(k, HT)
                pe.wait_ge(s_f3["h"], count + 1)
                pe.matmul(ps[:, k % 2, :], w_1[:, e, h * P:(h + 1) * P], tokens, start=True, stop=True)
                pe.matmul(ps[:, 2 + k % 2, :], w_3[:, e, h * P:(h + 1) * P], tokens, start=True, stop=True)\
                  .then_inc(s_f3["up"], 1)

            def gate(c):
                pe.wait_ge(s_f2["t"], c + 1)
                pe.matmul(ps[32 * c:32 * c + 32, 7, :], w_gate[:, :], xf_t[:, c * CHUNK:(c + 1) * CHUNK],
                          start=True, stop=True, skip_group_check=True).then_inc(s_f2["gate"], 1)

            pe.wait_ge(s_f1["x1"], CHUNKS)
            for c in range(CHUNKS):
                pe.wait_ge(s_f2["xs"], c + 1)
                if c >= 2:
                    pe.wait_ge(s_f2["t"], c - 1)
                for t in range(CT):
                    ins = pe.transpose(ps[:, 4 + c % 2, t * P:(t + 1) * P], f_stage[c % 2][:, t * DIM:(t + 1) * DIM],
                                       ident[:, :])
                ins.then_inc(s_f2["t_ps"], 1)
                if c:
                    gate(c - 1)
            gate(CHUNKS - 1)
            up(0, 0, xf_t[:, 0:CHUNK])
            pe.wait_ge(s_f2["logits"], 1)
            for t in range(CT):
                ins = pe.transpose(ps[:, 6, t * P:(t + 1) * P], att_t[0][:, t * P:(t + 1) * P], ident[:, :])
            ins.then_inc(s_f2["logits_ps"], 1)

            with pe.Fori(0, CHUNKS) as c:
                def down(e):
                    pe.wait_ge(s_f3["h"], c * (EXPERTS * HT) + ((e + 1) * HT + 2))
                    pe.wait_ge(s_f3["y_used"], c * EXPERTS + (e + 1))
                    for t in range(CT):
                        for h in range(HT):
                            ins = pe.matmul(ps[:, 4 + e % 2, t * DIM:(t + 1) * DIM],
                                            hidden[e % 2][:, h, t * P:(t + 1) * P], w_2[:, e * HT + h, :],
                                            start=h == 0, stop=h == HT - 1)
                    ins.then_inc(s_f3["y"], 1)

                tokens = xf_t[:, ds(c * CHUNK, CHUNK)]
                for k in range(1, EXPERTS * HT):
                    up(k, c * (EXPERTS * HT) + k, tokens)
                    if k % HT == 0:
                        down(k // HT - 1)
                up(0, c * (EXPERTS * HT) + EXPERTS * HT, xf_t[:, ds(((c + 1) % CHUNKS) * CHUNK, CHUNK)])
                down(EXPERTS - 1)


def kernel(**inputs):
    import numpy as _np
    import concourse.bacc as _bacc
    from concourse import mybir as _mybir
    from concourse.bass_utils import run_bass_kernel_spmd as _run

    inv_freq = _np.float32(1.0) / _np.float32(10000.0) ** (_np.arange(0, HD, 2, dtype=_np.float32) / _np.float32(HD))
    freqs = _np.arange(SEQ, dtype=_np.float32)[:, None] * inv_freq.astype(_np.float32)[None, :]
    angles = _np.concatenate([freqs, freqs], axis=-1)
    sign = _np.where(_np.arange(HD) < HD // 2, -1.0, 1.0)
    def tiled(table):
        table = table.astype(_np.float32).reshape(SEQ_TILES, P, HD)
        return _np.ascontiguousarray(table.transpose(1, 0, 2).reshape(P, SEQ_TILES * HD))

    given = {name.replace("L0_", ""): _np.asarray(a) for name, a in inputs.items()}
    arrays = {
        "x": given["attn_x"], "wq_cos": given["attn_Wq"].T, "wk_cos": given["attn_Wk"].T, "wv_cos": given["attn_Wv"].T,
        "g_scale": _np.broadcast_to(given["attn_g_scale"].reshape(1, 1), (P, 1)),
        "g1": given["ffn_g1"].reshape(P, 1), "g2": given["ffn_g2"].reshape(P, 1),
        "wq": given["ffn_wq"], "wk": given["ffn_wk"], "wv": given["ffn_wv"], "wo": given["ffn_wo"],
        "gate": given["ffn_gate"], "w1": given["ffn_w1"], "w2": given["ffn_w2"], "w3": given["ffn_w3"],
        "cos_table": tiled(_np.cos(angles)), "sin_table": tiled(_np.sin(angles) * sign),
    }
    nc = _bacc.Bacc("TRN2", target_bir_lowering=False, num_devices=1)
    feeds, aps = {}, {}
    for name, a in arrays.items():
        feeds[f"in_{name}"] = _np.ascontiguousarray(a)
        aps[name] = nc.dram_tensor(f"in_{name}", a.shape, _mybir.dt.float32, kind="ExternalInput").ap()
    result = nc.dram_tensor("out_dram", (BATCH, SEQ, DIM), _mybir.dt.float32, kind="ExternalOutput").ap()
    build(nc, out=result, **aps)
    return _run(nc, [feeds], core_ids=[0]).results[0]["out_dram"]
```

```python
from contextlib import ExitStack

import concourse.bass as bass
from concourse import mybir

F32 = mybir.dt.float32
BF16 = mybir.dt.bfloat16
ALU = mybir.AluOpType
ACT = mybir.ActivationFunctionType
AX = mybir.AxisListType
ds = bass.ds

P = 128
BATCH, SEQ, DIM = 2, 1024, 128
TILES = BATCH * SEQ // P
SEQ_TILES = SEQ // P
CT = 4
CHUNKS = TILES // CT
CHUNK = CT * P
HEADS, KV_HEADS, HD = 16, 4, 8
GROUP = 4
GROUPS = HEADS // GROUP
ITERS = BATCH * GROUPS
PARTS = 4
HEAD_COLS = PARTS * HD
WINDOW = 3 * HD
TERMS = 3 * WINDOW
BIAS_ROW = 96
Q_WINDOWS, K_WINDOWS = (0, 0, HD), (0, HD, 0)
QK_HEADS = 2 * HEADS
ROPE_HEADS = HEADS + KV_HEADS
QK_COLS, ROPE_COLS, V_COLS = 2 * DIM, ROPE_HEADS * HD, DIM + KV_HEADS * HD
EXPERTS, HIDDEN = 4, 384
HT = HIDDEN // P
LN_EPS, RMS_EPS, NORM_EPS = 1e-5, 1.1920928955078125e-07, 1e-12
COS_BOUND = 64.0
MASKED = -1e30
BIG = 3e38
BANK = 512

COS_STEPS = [(j, h, 1) for j in range(SEQ_TILES) for h in range(GROUP)]
CAUSAL_STEPS = ([(j, h, 1) for j in range(4) for h in range(GROUP)]
                + [(j, h, 2) for j in (4, 5) for h in (0, 2)] + [(6, 0, 4), (7, 0, 4)])
STEPS = len(COS_STEPS) + len(CAUSAL_STEPS)
ZEROED_TILES = 6
ZEROED_STEPS = sum(j < ZEROED_TILES for j, h, heads in CAUSAL_STEPS)
ROWS_CLEARED = 6
TURN = 3 * GROUP

PIECES = [(t, p, min((t + 1) * P - p * BANK, BANK)) for t in range(SEQ_TILES) for p in range(1 + t // 4)]
PACKED = {P: 4, 2 * P: 2, 3 * P: 1, 4 * P: 1}
MAXIMA = [[(t, p, w, h, PACKED[w]) for t, p, w in PIECES for h in range(pair, pair + 2, PACKED[w]) if PACKED[w] < 4]
          for pair in (0, 2)]
ALL_HEADS = [(t, p, w, 0, GROUP) for t, p, w in PIECES if PACKED[w] == GROUP]
FIRST_PAIR = [("max", 0, piece) for piece in ALL_HEADS + MAXIMA[0]]
EARLY = 4
COS_JOBS = FIRST_PAIR[EARLY:]
COS_JOBS.insert(1, ("out_causal", 1, 0))
COS_JOBS[7:7] = [("key", 0, 0), ("query", 0, 0)]
COS_JOBS += [("max", 1, piece) for piece in MAXIMA[1][:2]] + [("neg_max", 0, 0)]
COS_JOBS += [("max", 1, piece) for piece in MAXIMA[1][2:]] + [("cos", 0, 0), ("neg_max", 1, 0)]
CAUSAL_JOBS = [("cos", 1, 0), ("out_cos", 0, 0), ("out_cos", 1, 0)] + FIRST_PAIR[:EARLY] + [("out_causal", 0, 0)]
MAX_STEPS = 29
COS_ISSUED = ([0, 0] + [-(-(len(COS_JOBS) - 1) * (i + 1) // MAX_STEPS) for i in range(MAX_STEPS)]
              + [len(COS_JOBS)])
CAUSAL_JOB_STEPS = (0, 5, 6, 9, 11, 14, 16, 20)
CAUSAL_ISSUED = [sum(step <= i for step in CAUSAL_JOB_STEPS) for i in range(len(CAUSAL_STEPS))]
assert ITERS % 2 == 0
ALL_JOBS = COS_JOBS + CAUSAL_JOBS
JOBS = len(ALL_JOBS)
OF_NEXT = ("cos", "key", "query")
FIRST = [("cos", 0, 0), ("cos", 1, 0), ("key", 0, 0), ("query", 0, 0)] + FIRST_PAIR[:EARLY]
FIRST_JOBS = len(FIRST)
assert STEPS % 2 == 0 and JOBS % 2 == 0 and FIRST_JOBS % 2 == 0

TILE_CREDIT = 2 * SEQ_TILES
RES_CREDIT = 3
LO_CREDIT = 2
LAID = {"q_cos": 48 * GROUP, "k_cos": 48 * GROUP, "query": 48 * GROUP, "key": 48, "neg_max0": 16, "neg_max1": 16}


def build(nc, x, wq_cos, wk_cos, wv_cos, g_scale, g1, g2, wq, wk, wv, wo, gate, w1, w2, w3,
          cos_table, sin_table, out):
    ctx = ExitStack()
    with ctx:
        def sb(name, shape, dt=F32):
            return ctx.enter_context(nc.sbuf_tensor(name, shape, dt))

        def sem(name):
            return ctx.enter_context(nc.semaphore(name))

        x_tok = sb("x_tok", [P, TILES * DIM])
        xn = sb("xn", [P, TILES * DIM])
        w_qk = sb("w_qk", [P, QK_COLS + ROPE_COLS])
        w_v = sb("w_v", [P, V_COLS])
        w_o = sb("w_o", [P, DIM])
        w_gate = sb("w_gate", [P, 32])
        w_1 = sb("w_1", [P, EXPERTS, HIDDEN])
        w_3 = sb("w_3", [P, EXPERTS, HIDDEN])
        w_2 = sb("w_2", [P, EXPERTS * HT, DIM])
        g1_col, g2_col, g_col = sb("g1_col", [P, 1]), sb("g2_col", [P, 1]), sb("g_col", [P, 1])
        cos_t = sb("cos_t", [P, SEQ_TILES * HD])
        sin_t = sb("sin_t", [P, SEQ_TILES * HD])
        ident = sb("ident", [P, P])
        ident_b = sb("ident_b", [P, P], BF16)
        mask_q = sb("mask_q", [P, P], BF16)
        mask_k = sb("mask_k", [P, P], BF16)
        keep = sb("keep", [P, P])
        stat = sb("stat", [P, TILES, 6])
        s_mean, s_diff, s_var = sb("s_mean", [P, TILES]), sb("s_diff", [P, TILES]), sb("s_var", [P, TILES])
        roots = sb("roots", [P, 2, TILES])
        scales = sb("scales", [P, 2, TILES])
        parts_cos = sb("parts_cos", [P, TILES * QK_HEADS * HEAD_COLS], BF16)
        parts_rope = sb("parts_rope", [P, TILES * ROPE_HEADS * HEAD_COLS + P - HEAD_COLS], BF16)
        v_cos = sb("v_cos", [P, TILES * DIM])
        v_causal = sb("v_causal", [P, TILES * KV_HEADS * HD])
        q_cos_t = sb("q_cos_t", [P, GROUP, SEQ], BF16)
        k_cos_t = sb("k_cos_t", [P, GROUP, SEQ], BF16)
        q_causal_t = [sb(f"q_causal_t{i}", [P, GROUP, SEQ], BF16) for i in range(2)]
        k_causal_t = [sb(f"k_causal_t{i}", [P, SEQ], BF16) for i in range(2)]
        parts_t = {n: sb(f"parts_t_{n}", [P, SEQ], BF16) for n in ("q_cos", "k_cos", "query", "key")}
        neg_max_t = sb("neg_max_t", [2 * 2 * SEQ_TILES, 2, P], BF16)
        v_cos_pad = sb("v_cos_pad", [P, SEQ_TILES, GROUP, 32])
        v_causal_pad = sb("v_causal_pad", [P, SEQ_TILES, 32])
        neg_piece = sb("neg_piece", [P, GROUP, SEQ_TILES, 2])
        neg_max = sb("neg_max", [P, GROUP, SEQ_TILES])
        neg_max_parts = sb("neg_max_parts", [P, 2, 2, 2 * SEQ_TILES], BF16)
        out_t = sb("out_t", [P, 2, SEQ])
        recip = sb("recip", [P, 2, CT, GROUP])
        att_cos = sb("att_cos", [P, SEQ_TILES, GROUP * HD])
        att_causal = sb("att_causal", [P, TILES, DIM])
        probs = sb("probs", [P, 2, GROUP, SEQ])

        room = probs[:, :, :, :].rearrange("p a h s -> p (a h s)")

        def part(start, size):
            return room[:, start:start + size]

        xn_stage = part(0, CHUNK)
        xn_t = part(512, CHUNK)
        squares = part(1024, CT * QK_COLS)
        rope_in = part(3072, CT * ROPE_COLS)
        rope_a = part(3712, CT * ROPE_COLS)
        rope_b = part(4352, CT * ROPE_COLS)
        norms = part(4992, CT * QK_HEADS)
        inv_norms = part(5120, CT * QK_HEADS)
        unit = part(2048, CT * QK_COLS)
        xf_t = part(0, TILES * P)
        hidden = [part(2048 + 1536 * i, HT * CHUNK).rearrange("p (h n) -> p h n", h=HT) for i in range(2)]
        gated = [part(5120 + 512 * i, CHUNK) for i in range(2)]
        att_t = [part(6144 + 512 * i, CHUNK) for i in range(2)]
        f_stage = [part(7168 + 512 * i, CHUNK) for i in range(2)]
        sum_sq = s_mean
        logits = sb("logits", [P, TILES, EXPERTS])
        g_exp, g_rank = sb("g_exp", [P, TILES, EXPERTS]), sb("g_rank", [P, TILES, EXPERTS])
        g_cmp = sb("g_cmp", [P, 6, TILES])
        comb = sb("comb", [P, TILES * EXPERTS])
        neg_abs_g = sb("neg_abs_g", [P, 1])
        cos_shift = sb("cos_shift", [P, SEQ * GROUP // P], BF16)
        ones = sb("ones", [P, SEQ * GROUP // P], BF16)
        unused = sb("unused", [P, 3])

        ps = ctx.enter_context(nc.psum_tensor("ps", [P, 8, BANK], F32))
        acc = ps[:, 4:6, :]
        aux = [ps[:, 6 + i, :] for i in range(2)]
        aux_b = [a.bitcast(BF16) for a in aux]

        def slot(n):
            return ps[:, 2 * (n % 2):2 * (n % 2) + 2, :].rearrange("p b n -> p (b n)")

        x_landed = [sem(f"x_landed{i}") for i in range(CHUNKS)]
        wqkv_landed = sem("wqkv_landed")
        small_landed = sem("small_landed")
        rest_landed = sem("rest_landed")
        tables_landed = sem("tables_landed")
        constants_made = sem("constants_made")
        buffers_cleared = sem("buffers_cleared")
        rows_cleared = sem("rows_cleared")
        weights_scaled = sem("weights_scaled")
        cos_shift_steps = sem("cos_shift_steps")
        cos_bias_rows_laid = sem("cos_bias_rows_laid")
        dve_steps_stats = sem("dve_steps_stats")
        stats_made = sem("stats_made")
        roots_made = sem("roots_made")
        xn_staged = sem("xn_staged")
        xn_saved = sem("xn_saved")
        xt_in_psum = sem("xt_in_psum")
        xt_ready = sem("xt_ready")
        projected = sem("projected")
        q_and_k_copied = sem("q_and_k_copied")
        projections_read = sem("projections_read")
        squares_ready = sem("squares_ready")
        v_copied = sem("v_copied")
        norm_squares_ready = sem("norm_squares_ready")
        norms_ready = sem("norms_ready")
        dve_steps_proj = sem("dve_steps_proj")
        rope_input_ready = sem("rope_input_ready")
        rope_steps = sem("rope_steps")
        high_parts_again = sem("high_parts_again")
        high_parts = sem("high_parts")
        middle_parts = sem("middle_parts")
        residues = sem("residues")
        low_parts = sem("low_parts")
        scores_ready = sem("scores_ready")
        probs_ready = sem("probs_ready")
        masked_probs_zeroed = sem("masked_probs_zeroed")
        key_tiles_used = sem("key_tiles_used")
        first_half_done = sem("first_half_done")
        acc_halves_copied = sem("acc_halves_copied")
        aux_filled = sem("aux_filled")
        aux_read = sem("aux_read")
        neg_max_ready = sem("neg_max_ready")
        recips_ready = sem("recips_ready")
        laid = {n: sem(f"laid_{n}") for n in LAID}
        v_cos_padded = sem("v_cos_padded")
        v_causal_padded = sem("v_causal_padded")
        ffn_in_done = {n: sem("ffn_in_" + n) for n in (
            "transposed", "copied", "projected", "residual", "squares", "squares_summed", "cos_added", "all_added")}
        gating_done = {n: sem("gating_" + n) for n in (
            "mean_squares", "rms", "rms_inverse", "normalised", "transposed", "copied", "products", "logits_copied",
            "logits_transposed", "weight_steps", "logit_exps")}
        experts_done = {n: sem("experts_" + n) for n in (
            "up_products", "silus", "hidden", "down_products", "outputs_summed", "stored")}

        block = ctx.enter_context(nc.Block())

        def step_view(n, j, heads, causal):
            s = slot(n)
            if not causal or j < 4:
                return s[:, (j * P if causal else 0):SEQ].unsqueeze(1)
            width = SEQ - j * P
            if heads == 2:
                return s.rearrange("p (h n) -> p h n", h=2)[:, :, 0:width]
            return s[:, 0:heads * width].rearrange("p (h n) -> p h n", h=heads)

        @block.sync
        def _(sp):
            for c in range(CHUNKS):
                b, t0 = divmod(c * CT, SEQ_TILES)
                src = x[b, t0 * P:(t0 + CT) * P, :].rearrange("(t p) d -> p t d", p=P)
                dst = x_tok[:, c * CHUNK:(c + 1) * CHUNK].rearrange("p (t d) -> p t d", t=CT)
                sp.dma_start(dst, src).then_inc(x_landed[c], 16)
            sp.dma_start(g1_col[:, :], g1).then_inc(small_landed, 16)
            sp.dma_start(g2_col[:, :], g2).then_inc(small_landed, 16)
            sp.dma_start(g_col[:, :], g_scale).then_inc(small_landed, 16)
            sp.dma_start(cos_t[:, :], cos_table).then_inc(tables_landed, 16)
            sp.dma_start(sin_t[:, :], sin_table).then_inc(tables_landed, 16)
            sp.dma_start(w_1[:, :, :], w1.rearrange("e i h -> i e h")).then_inc(rest_landed, 16)
            sp.dma_start(w_3[:, :, :], w3.rearrange("e i h -> i e h")).then_inc(rest_landed, 16)
            sp.dma_start(w_2[:, :, :], w2.rearrange("e (h i) d -> i (e h) d", i=P)).then_inc(rest_landed, 16)
            sp.dma_start(w_o[:, :], wo).then_inc(rest_landed, 16)
            sp.dma_start(w_gate[:, 0:EXPERTS], gate).then_inc(rest_landed, 16)

            def lay_out(signal, src, dst, windows, heads):
                for h in heads:
                    for w, row in enumerate(windows):
                        sp.dma_start(dst[w * WINDOW:(w + 1) * WINDOW, h, :],
                                     parts_t[src][h * HEAD_COLS + row:h * HEAD_COLS + row + WINDOW, :])\
                          .then_inc(laid[signal], 16)

            def lay_out_cos(base, base_k, scores_made):
                sp.wait_ge(aux_read, base + 3)
                sp.wait_ge(scores_ready, scores_made)
                lay_out("q_cos", "q_cos", q_cos_t, Q_WINDOWS, range(GROUP))
                sp.wait_ge(aux_read, base_k + 3)
                lay_out("k_cos", "k_cos", k_cos_t, K_WINDOWS, range(GROUP))

            def lay_out_causal(base, parity):
                sp.wait_ge(aux_read, base + 3)
                lay_out("key", "key", k_causal_t[parity][:, :].unsqueeze(1), K_WINDOWS, range(1))
                sp.wait_ge(aux_read, base + 4)
                lay_out("query", "query", q_causal_t[parity], Q_WINDOWS, range(GROUP))

            sp.wait_ge(rows_cleared, ROWS_CLEARED)
            sp.wait_ge(cos_shift_steps, 3)
            sp.dma_start(q_cos_t[BIAS_ROW:BIAS_ROW + 1, :, :], cos_shift[:, :]).then_inc(cos_bias_rows_laid, 16)
            sp.dma_start(k_cos_t[BIAS_ROW:BIAS_ROW + 1, :, :], ones[:, :]).then_inc(cos_bias_rows_laid, 16)
            lay_out_cos(0, 1, 1)
            lay_out_causal(2, 0)
            with sp.Fori(0, ITERS // 2) as pair:
                for parity in range(2):
                    base = (pair * 2 + parity) * JOBS + FIRST_JOBS
                    lay_out_causal(base + COS_JOBS.index(("key", 0, 0)), 1 - parity)
                    for a in range(2):
                        sp.wait_ge(aux_read, base + (COS_JOBS.index(("neg_max", a, 0)) + 3))
                        sp.dma_start(q_causal_t[parity][BIAS_ROW:BIAS_ROW + 2, 2 * a:2 * a + 2, :], neg_max_t[:, a, :])\
                          .then_inc(laid[f"neg_max{a}"], 16)
                    lay_out_cos(base + ALL_JOBS.index(("cos", 0, 0)), base + ALL_JOBS.index(("cos", 1, 0)),
                                (pair * 2 + parity) * STEPS + (len(COS_STEPS) + 1))
            for name in ("q_cos", "k_cos", "key", "query"):
                sp.wait_ge(laid[name], (ITERS + 2) * LAID[name])

            for c in range(CHUNKS):
                b, t0 = divmod(c * CT, SEQ_TILES)
                dst = out[b, t0 * P:(t0 + CT) * P, :].rearrange("(t p) d -> p t d", p=P)
                sp.wait_ge(experts_done["outputs_summed"], (c + 1) * EXPERTS + 2)
                sp.dma_start(dst, x_tok[:, c * CHUNK:(c + 1) * CHUNK].rearrange("p (t d) -> p t d", t=CT))\
                  .then_inc(experts_done["stored"], 16)
            sp.wait_ge(experts_done["stored"], 16 * CHUNKS)

        @block.gpsimd
        def _(pool):
            pool.memset(ident[:, :], 0.0).then_inc(constants_made, 1)
            pool.memset(ident_b[:, :], 0.0).then_inc(constants_made, 1)
            pool.memset(mask_q[:, :], 0.0).then_inc(constants_made, 1)
            pool.memset(mask_k[:, :], 0.0).then_inc(constants_made, 1)
            pool.memset(keep[:, :], BIG).then_inc(constants_made, 1)
            pool.wait_ge(constants_made, 5)
            for m in (ident, ident_b):
                pool.affine_select(out=m[:, :], in_=m[:, :], compare_op=ALU.not_equal, fill=1.0,
                                   base=0, pattern=[[-1, P]], channel_multiplier=1).then_inc(constants_made, 1)
            pool.affine_select(out=mask_q[:, :], in_=mask_q[:, :], compare_op=ALU.is_ge, fill=MASKED,
                               base=0, pattern=[[-1, P]], channel_multiplier=1).then_inc(constants_made, 1)
            pool.affine_select(out=mask_k[:, :], in_=mask_k[:, :], compare_op=ALU.is_ge, fill=MASKED,
                               base=0, pattern=[[1, P]], channel_multiplier=-1).then_inc(constants_made, 1)
            pool.affine_select(out=keep[:, :], in_=keep[:, :], compare_op=ALU.is_ge, fill=0.0,
                               base=0, pattern=[[1, P]], channel_multiplier=-1).then_inc(constants_made, 1)
            pool.memset(v_cos_pad[:, :, :, HD:], 0.0).then_inc(buffers_cleared, 1)
            pool.memset(v_causal_pad[:, :, HD:], 0.0).then_inc(buffers_cleared, 1)
            pool.memset(neg_piece[:, :, :, :], BIG).then_inc(buffers_cleared, 1)
            pool.memset(w_gate[:, EXPERTS:], 0.0).then_inc(buffers_cleared, 1)
            pool.memset(ones[:, :], 1.0).then_inc(buffers_cleared, 1)
            pool.memset(out_t[:, 1, :], 1.0).then_inc(buffers_cleared, 1)
            pool.wait_ge(buffers_cleared, 7)
            pool.memset(v_cos_pad[:, :, :, HD:HD + 1], 1.0).then_inc(buffers_cleared, 1)
            pool.memset(v_causal_pad[:, :, HD:HD + 1], 1.0).then_inc(buffers_cleared, 1)
            pool.wait_ge(buffers_cleared, 9)
            for n, t in enumerate((q_cos_t, k_cos_t, *q_causal_t)):
                pool.memset(t[64:P, :, :], 0.0).then_inc(rows_cleared, 1)
                pool.wait_ge(rows_cleared, n + 1)
            for n, t in enumerate(k_causal_t):
                pool.memset(t[64:P, :], 0.0).then_inc(rows_cleared, 1)
                pool.wait_ge(rows_cleared, n + 5)
            for n, t in enumerate(k_causal_t):
                pool.memset(t[BIAS_ROW:BIAS_ROW + 2, :], 1.0).then_inc(buffers_cleared, 1)
                pool.wait_ge(buffers_cleared, n + 10)
            pool.wait_ge(tables_landed, 32)

            with pool.Fori(0, CHUNKS) as c:
                pool.wait_ge(rope_input_ready, c + 1)
                pool.wait_ge(low_parts, 2 * c + LO_CREDIT)
                heads = CT * ROPE_HEADS
                table = ds((c % 2) * CT * HD, CT * HD)
                cos_c = cos_t[:, table].rearrange("p (t d) -> p t d", t=CT)
                sin_c = sin_t[:, table].rearrange("p (t d) -> p t d", t=CT)
                r_in = rope_in.rearrange("p (t h d) -> p t h d", t=CT, d=HD)
                r_a = rope_a.rearrange("p (t h d) -> p t h d", t=CT, d=HD)
                r_b = rope_b.rearrange("p (t h d) -> p t h d", t=CT, d=HD)
                half = HD // 2
                pool.tensor_tensor(r_a, r_in, cos_c.unsqueeze(2).to_broadcast([P, CT, ROPE_HEADS, HD]),
                                   ALU.mult).then_inc(rope_steps, 1)
                for to, of in ((0, half), (half, 0)):
                    pool.tensor_tensor(r_b[:, :, :, to:to + half], r_in[:, :, :, of:of + half],
                                       sin_c[:, :, to:to + half].unsqueeze(2)
                                       .to_broadcast([P, CT, ROPE_HEADS, half]), ALU.mult).then_inc(rope_steps, 1)
                pool.wait_ge(rope_steps, 4 * c + 3)
                pool.tensor_tensor(rope_a, rope_a, rope_b, ALU.add).then_inc(rope_steps, 1)
                for n, (flat, count) in enumerate(((parts_cos, CT * QK_HEADS), (parts_rope, CT * ROPE_HEADS))):
                    pool.wait_ge(high_parts, 2 * c + (n + 1))
                    words = flat[:, ds(c * (count * HEAD_COLS), count * HEAD_COLS)].bitcast(F32)\
                        .rearrange("p (h w) -> p h w", w=HEAD_COLS // 2)
                    pool.tensor_copy(words[:, :, 3 * HD // 2:], words[:, :, 0:HD // 2]).then_inc(high_parts_again, 1)

            with pool.Fori(0, ITERS) as it:
                b, g = it // GROUPS, it % GROUPS
                pool.wait_ge(key_tiles_used, it * (2 * SEQ_TILES) + (TILE_CREDIT - SEQ_TILES))
                src = v_cos[:, ds(b * (SEQ_TILES * DIM) + g * (GROUP * HD), SEQ_TILES * DIM - (GROUPS - 1) * GROUP * HD)]
                for t in range(SEQ_TILES):
                    one = src[:, t * DIM:t * DIM + GROUP * HD].rearrange("p (h d) -> p h d", h=GROUP)
                    ins = pool.tensor_copy(v_cos_pad[:, t, :, 0:HD], one)
                ins.then_inc(v_cos_padded, 1)
                pool.wait_ge(key_tiles_used, it * (2 * SEQ_TILES) + TILE_CREDIT)
                width = KV_HEADS * HD
                src = v_causal[:, ds(b * (SEQ_TILES * width) + g * HD, SEQ_TILES * width - (KV_HEADS - 1) * HD)]
                for t in range(SEQ_TILES):
                    ins = pool.tensor_copy(v_causal_pad[:, t, 0:HD], src[:, t * width:t * width + HD])
                ins.then_inc(v_causal_padded, 1)
                pool.wait_ge(aux_read, it * JOBS + (FIRST_JOBS + ALL_JOBS.index(("out_cos", 1, 0)) + 3))
                tokens, heads = ds(b * SEQ_TILES, SEQ_TILES), ds(g * (GROUP * HD), GROUP * HD)
                x_heads = x_tok[:, :].rearrange("p (t d) -> p t d", d=DIM)[:, tokens, heads]
                pool.tensor_tensor(x_heads, x_heads, att_cos[:, :, :], ALU.add).then_inc(ffn_in_done["cos_added"], 1)

            pool.wait_ge(ffn_in_done["cos_added"], ITERS + 1)
            for c in range(CHUNKS):
                chunk = slice(c * CHUNK, (c + 1) * CHUNK)
                pool.wait_ge(ffn_in_done["residual"], c + 1)
                pool.tensor_tensor(x_tok[:, chunk], x_tok[:, chunk], xn[:, chunk], ALU.add)\
                   .then_inc(ffn_in_done["all_added"], 1)

        @block.scalar
        def _(act):
            for n, (dst, src) in enumerate((
                    (w_qk[:, 0:128], wq_cos), (w_qk[:, 128:256], wk_cos), (w_qk[:, 256:384], wq),
                    (w_qk[:, 384:416], wk), (w_v[:, 0:128], wv_cos), (w_v[:, 128:160], wv))):
                act.dma_start(dst, src).then_inc(wqkv_landed, 16)
            act.wait_ge(stats_made, 1)
            act.wait_ge(constants_made, 10)
            act.activation(roots[:, :, :], roots[:, :, :], ACT.Sqrt).then_inc(roots_made, 1)

            def load_table(n, func):
                act.activation(unused[:, n:n + 1], ident[:, 0:1], func)

            def copy_xt(c):
                act.wait_ge(xt_in_psum, c + 1)
                act.wait_ge(projected, c + 1)
                act.activation(xn_t, ps[:, 6, :], ACT.Copy).then_inc(xt_ready, 1)

            def save_xn(c):
                act.wait_ge(xn_staged, CT * c + CT)
                act.activation(xn[:, ds(c * CHUNK, CHUNK)], xn_stage, ACT.Copy).then_inc(xn_saved, 1)

            def project_chunk(c, more):
                act.wait_ge(projected, c + 2)
                act.wait_ge(low_parts, 2 * c + LO_CREDIT)
                act.activation(unit.rearrange("p (t n) -> p t n", t=CT), ps[:, 0:CT, 0:QK_COLS], ACT.Copy)\
                   .then_inc(q_and_k_copied, 1)
                if more:
                    copy_xt(c + 1)
                v_ps = ps[:, 4:6, 0:2 * V_COLS].rearrange("p b (t n) -> p b t n", t=2)
                act.activation(v_cos[:, ds(c * CHUNK, CHUNK)].rearrange("p (b t n) -> p b t n", b=2, t=2),
                               v_ps[:, :, :, 0:DIM], ACT.Copy).then_inc(v_copied, 1)
                act.wait_ge(q_and_k_copied, c + 1)
                act.wait_ge(norm_squares_ready, c + 1)
                act.activation(squares, unit, ACT.Square).then_inc(squares_ready, 1)
                if more:
                    save_xn(c + 1)
                act.wait_ge(norm_squares_ready, c + 2)
                act.activation(norms, norms, ACT.Sqrt).then_inc(norms_ready, 1)
                a_parts = parts_cos[:, ds(c * (CT * QK_HEADS * HEAD_COLS), CT * QK_HEADS * HEAD_COLS)]\
                    .rearrange("p (h s d) -> p h s d", s=PARTS, d=HD)
                r_parts = parts_rope[:, ds(c * (CT * ROPE_HEADS * HEAD_COLS), CT * ROPE_HEADS * HEAD_COLS)]\
                    .rearrange("p (h s d) -> p h s d", s=PARTS, d=HD)
                unit_h = unit.rearrange("p (h d) -> p h d", d=HD)
                rope_h = rope_a.rearrange("p (h d) -> p h d", d=HD)
                act.wait_ge(residues, 3 * c + (RES_CREDIT + 1))
                act.activation(a_parts[:, :, 0, :], unit_h, ACT.Copy).then_inc(high_parts, 1)
                act.wait_ge(rope_steps, 4 * c + 4)
                act.activation(r_parts[:, :, 0, :], rope_h, ACT.Copy).then_inc(high_parts, 1)
                act.wait_ge(residues, 3 * c + (RES_CREDIT + 2))
                act.activation(a_parts[:, :, 1, :], unit_h, ACT.Copy).then_inc(middle_parts, 1)
                act.wait_ge(residues, 3 * c + (RES_CREDIT + 3))
                act.activation(r_parts[:, :, 1, :], rope_h, ACT.Copy).then_inc(middle_parts, 1)

            copy_xt(0)
            save_xn(0)
            with act.Fori(0, CHUNKS // 2) as c:
                project_chunk(c, more=True)
            for c in range(CHUNKS // 2, CHUNKS):
                project_chunk(c, more=c < CHUNKS - 1)

            def exp_steps(it, first, last):
                for n, (j, h, heads) in list(enumerate(COS_STEPS + CAUSAL_STEPS))[first:last]:
                    causal = n >= len(COS_STEPS)
                    tile = j + SEQ_TILES * causal
                    if h == 0:
                        act.wait_ge(key_tiles_used, it * (2 * SEQ_TILES) + (tile - 1 + TILE_CREDIT))
                    act.wait_ge(scores_ready, it * STEPS + (n + 2))
                    start = j * P if causal else 0
                    act.activation(probs[:, j % 2, h:h + heads, start:SEQ], step_view(n, j, heads, causal),
                                   ACT.Exp).then_inc(probs_ready, 1)

            load_table(0, ACT.Exp)
            exp_steps(0, 0, TURN)
            with act.Fori(0, ITERS - 1) as it:
                exp_steps(it, TURN, STEPS)
                exp_steps(it + 1, 0, TURN)
            exp_steps(ITERS - 1, TURN, STEPS)
            load_table(1, ACT.Sqrt)

            def copy_attention(c):
                act.wait_ge(ffn_in_done["transposed"], c + 1)
                if c >= 2:
                    act.wait_ge(ffn_in_done["projected"], c - 1)
                act.activation(att_t[c % 2], ps[:, c % 2, :], ACT.Copy).then_inc(ffn_in_done["copied"], 1)

            def square(c):
                act.wait_ge(ffn_in_done["residual"], c + 1)
                if c >= 2:
                    act.wait_ge(ffn_in_done["squares_summed"], c - 1)
                act.activation(f_stage[c % 2], xn[:, c * CHUNK:(c + 1) * CHUNK], ACT.Square)\
                   .then_inc(ffn_in_done["squares"], 1)

            for c in range(CHUNKS):
                copy_attention(c)
                if c:
                    square(c - 1)
            square(CHUNKS - 1)
            act.wait_ge(gating_done["mean_squares"], 1)
            act.activation(sum_sq[:, :], sum_sq[:, :], ACT.Sqrt).then_inc(gating_done["rms"], 1)
            for c in range(CHUNKS):
                act.wait_ge(gating_done["transposed"], c + 1)
                act.activation(xf_t[:, c * CHUNK:(c + 1) * CHUNK], ps[:, 4 + c % 2, :], ACT.Copy,
                               scale=g2_col[:, :]).then_inc(gating_done["copied"], 1)
            load_table(2, ACT.Exp)
            act.wait_ge(gating_done["products"], CHUNKS)
            act.activation(att_t[0], ps[:, 7, :], ACT.Copy).then_inc(gating_done["logits_copied"], 1)
            act.wait_ge(gating_done["weight_steps"], 2)
            act.activation(g_exp[:, :, :], logits[:, :, :], ACT.Exp).then_inc(gating_done["logit_exps"], 1)
            with act.Fori(0, CHUNKS) as c:
                for k in range(EXPERTS * HT):
                    act.wait_ge(experts_done["up_products"], c * (EXPERTS * HT) + (k + 1))
                    act.wait_ge(experts_done["hidden"], c * (EXPERTS * HT) + (k + 1))
                    act.activation(gated[k % 2], ps[:, k % 2, :], ACT.Silu).then_inc(experts_done["silus"], 1)

        @block.vector
        def _(dve):
            step0 = [0]

            def link(ins):
                step0[0] += 1
                ins.then_inc(dve_steps_stats, 1)
                dve.wait_ge(dve_steps_stats, step0[0])

            for s, n in ((projected, 1), (projections_read, 1), (norm_squares_ready, 1), (low_parts, LO_CREDIT),
                         (residues, RES_CREDIT), (scores_ready, 1), (probs_ready, 2), (key_tiles_used, TILE_CREDIT),
                         (aux_read, 2), (acc_halves_copied, 2), (ffn_in_done["cos_added"], 1),
                         (experts_done["hidden"], 2), (experts_done["down_products"], 2),
                         (experts_done["outputs_summed"], 2)):
                dve.sem_inc(s, n)
            for name, n in LAID.items():
                dve.sem_inc(laid[name], n)

            dve.memset(parts_rope[:, TILES * ROPE_HEADS * HEAD_COLS:], 0.0).then_inc(buffers_cleared, 1)

            for t in range(TILES):
                dve.wait_ge(x_landed[t // CT], 16)
                ins = dve.bn_stats(stat[:, t, :], x_tok[:, t * DIM:(t + 1) * DIM])
            link(ins)
            dve.tensor_tensor(s_mean[:, :], stat[:, :, 1], stat[:, :, 4], ALU.add).then_inc(dve_steps_stats, 1)
            dve.tensor_tensor(s_diff[:, :], stat[:, :, 1], stat[:, :, 4], ALU.subtract).then_inc(dve_steps_stats, 1)
            step0[0] += 2
            link(dve.tensor_tensor(s_var[:, :], stat[:, :, 2], stat[:, :, 5], ALU.add))
            link(dve.tensor_tensor(s_diff[:, :], s_diff[:, :], s_diff[:, :], ALU.mult))
            link(dve.scalar_tensor_tensor(out=s_var[:, :], in0=s_diff[:, :], scalar=DIM / 4.0, in1=s_var[:, :],
                                          op0=ALU.mult, op1=ALU.add))
            dve.tensor_scalar(s_mean[:, :], s_mean[:, :], 0.5, None, ALU.mult).then_inc(dve_steps_stats, 1)
            step0[0] += 1
            link(dve.tensor_scalar(roots[:, 0, :], s_var[:, :], 1.0 / DIM, LN_EPS, ALU.mult, ALU.add))
            link(dve.reciprocal(roots[:, 1, :], roots[:, 0, :]))
            link(dve.tensor_tensor(roots[:, 1, :], roots[:, 1, :], s_var[:, :], ALU.mult))
            dve.tensor_scalar(roots[:, 1, :], roots[:, 1, :], 1.0 / DIM, RMS_EPS, ALU.mult, ALU.add)\
               .then_inc(stats_made, 1)
            dve.wait_ge(roots_made, 1)
            link(dve.reciprocal(scales[:, :, :], roots[:, :, :]))

            def stage_xn(c):
                for t in range(CT):
                    dve.tensor_scalar(xn_stage[:, t * DIM:(t + 1) * DIM],
                                      x_tok[:, ds(c * CHUNK + t * DIM, DIM)],
                                      s_mean[:, ds(c * CT + t, 1)], scales[:, 0, ds(c * CT + t, 1)],
                                      ALU.subtract, ALU.mult).then_inc(xn_staged, 1)

            def project_chunk(c, ahead):
                r1 = scales[:, 1, ds(c * CT, CT)]
                dve.wait_ge(q_and_k_copied, c + 1)
                dve.tensor_tensor(rope_in.rearrange("p (t n) -> p t n", t=CT), ps[:, 0:CT, QK_COLS:QK_COLS + ROPE_COLS],
                                  r1.unsqueeze(2).to_broadcast([P, CT, ROPE_COLS]), ALU.mult)\
                                     .then_inc(rope_input_ready, 1)
                v_ps = ps[:, 4:6, 0:2 * V_COLS].rearrange("p b (t n) -> p b t n", t=2)
                dve.wait_ge(v_copied, c + 1)
                dve.tensor_tensor(v_causal[:, ds(c * (CT * KV_HEADS * HD), CT * KV_HEADS * HD)]
                                  .rearrange("p (b t n) -> p b t n", b=2, t=2), v_ps[:, :, :, DIM:V_COLS],
                                  r1.rearrange("p (b t) -> p b t", b=2).unsqueeze(3)
                                  .to_broadcast([P, 2, 2, KV_HEADS * HD]), ALU.mult).then_inc(projections_read, 1)
                dve.wait_ge(squares_ready, c + 1)
                dve.tensor_reduce(norms, squares.rearrange("p (h d) -> p h d", d=HD), AX.X, ALU.add)\
                   .then_inc(norm_squares_ready, 1)
                dve.wait_ge(norms_ready, c + 1)
                dve.tensor_scalar(norms, norms, NORM_EPS, None, ALU.max).then_inc(dve_steps_proj, 1)
                dve.wait_ge(dve_steps_proj, 3 * c + 1)
                dve.reciprocal(inv_norms, norms).then_inc(dve_steps_proj, 1)
                dve.wait_ge(dve_steps_proj, 3 * c + 2)
                inv_q = inv_norms.rearrange("p (t h) -> p t h", t=CT)[:, :, 0:HEADS]
                dve.tensor_scalar(inv_q, inv_q, g_col[:, :], None, ALU.mult).then_inc(dve_steps_proj, 1)
                dve.wait_ge(dve_steps_proj, 3 * c + 3)
                dve.tensor_tensor(unit.rearrange("p (t h d) -> p t h d", t=CT, d=HD),
                                  unit.rearrange("p (t h d) -> p t h d", t=CT, d=HD),
                                  inv_norms.rearrange("p (t h) -> p t h", t=CT).unsqueeze(3)
                                  .to_broadcast([P, CT, QK_HEADS, HD]), ALU.mult).then_inc(residues, 1)
                if ahead:
                    dve.wait_ge(xn_saved, c + 2)
                    dve.wait_ge(xt_in_psum, c + 2)
                    stage_xn(c + 2)
                a_parts = parts_cos[:, ds(c * (CT * QK_HEADS * HEAD_COLS), CT * QK_HEADS * HEAD_COLS)]\
                    .rearrange("p (h s d) -> p h s d", s=PARTS, d=HD)
                r_parts = parts_rope[:, ds(c * (CT * ROPE_HEADS * HEAD_COLS), CT * ROPE_HEADS * HEAD_COLS)]\
                    .rearrange("p (h s d) -> p h s d", s=PARTS, d=HD)
                unit_h = unit.rearrange("p (h d) -> p h d", d=HD)
                rope_h = rope_a.rearrange("p (h d) -> p h d", d=HD)
                dve.wait_ge(high_parts, 2 * c + 1)
                dve.tensor_tensor(unit_h, unit_h, a_parts[:, :, 0, :], ALU.subtract).then_inc(residues, 1)
                dve.wait_ge(high_parts, 2 * c + 2)
                dve.tensor_tensor(rope_h, rope_h, r_parts[:, :, 0, :], ALU.subtract).then_inc(residues, 1)
                dve.wait_ge(middle_parts, 2 * c + 1)
                dve.tensor_tensor(a_parts[:, :, 2, :], unit_h, a_parts[:, :, 1, :], ALU.subtract).then_inc(low_parts, 1)
                dve.wait_ge(middle_parts, 2 * c + 2)
                dve.tensor_tensor(r_parts[:, :, 2, :], rope_h, r_parts[:, :, 1, :], ALU.subtract).then_inc(low_parts, 1)
                dve.wait_ge(low_parts, 2 * c + (LO_CREDIT + 2))

            def empty_slot(base, index, kind, a, b, it):
                k = index % 2
                dve.wait_ge(aux_filled, base + (index + 1))
                if kind in ("cos", "query", "key"):
                    name = ("q_cos", "k_cos")[a] if kind == "cos" else kind
                    rows = HEAD_COLS if kind == "key" else P
                    dve.wait_ge(laid[name], (it + 1) * LAID[name])
                    dve.tensor_copy(parts_t[name][0:rows, :], aux_b[k][0:rows, :]).then_inc(aux_read, 1)
                elif kind == "neg_max":
                    dve.wait_ge(laid[f"neg_max{a}"], (it + 1) * LAID[f"neg_max{a}"])
                    dve.tensor_copy(neg_max_t[:, a, :], aux_b[k][0:2 * 2 * SEQ_TILES, 0:P]).then_inc(aux_read, 1)
                elif kind == "max":
                    t, piece, width, h, heads = b
                    dve.tensor_reduce(neg_piece[:, h:h + heads, t, piece],
                                      aux[k][:, 0:heads * width].rearrange("p (h n) -> p h n", h=heads), AX.X, ALU.max,
                                      negate=True).then_inc(aux_read, 1)

            def normalise(base, index, step, att, tile, g):
                dst = att[:, ds(tile, CT), ds(g * (GROUP * HD), GROUP * HD)].rearrange("p t (h d) -> p t h d", h=GROUP)
                k = index % 2
                o = aux[k].rearrange("p (t h d) -> p t h d", t=CT, h=GROUP)
                dve.wait_ge(aux_filled, base + (index + 1))
                dve.reciprocal(recip[:, k, :, :], o[:, :, :, HD]).then_inc(recips_ready, 1)
                dve.wait_ge(recips_ready, step)
                dve.tensor_tensor(dst, o[:, :, :, 0:HD],
                                  recip[:, k, :, :].unsqueeze(3).to_broadcast([P, CT, GROUP, HD]),
                                  ALU.mult).then_inc(aux_read, 1)

            def zero_masked(it, i):
                j, h, heads = CAUSAL_STEPS[i]
                diagonal = probs[:, j % 2, h:h + heads, j * P:(j + 1) * P]
                dve.wait_ge(probs_ready, it * STEPS + (len(COS_STEPS) + i + 3))
                dve.tensor_tensor(diagonal, diagonal, keep[:, :].unsqueeze(1).to_broadcast([P, heads, P]),
                                  ALU.min).then_inc(masked_probs_zeroed, 1)

            def copy_acc(which, half, it):
                if half == 0:
                    dve.wait_ge(first_half_done, it * 2 + (which + 1))
                else:
                    dve.wait_ge(key_tiles_used, it * (2 * SEQ_TILES) + ((which + 1) * SEQ_TILES + TILE_CREDIT))
                dve.tensor_copy(out_t[:, which, half * BANK:(half + 1) * BANK], acc[:, half, :])\
                   .then_inc(acc_halves_copied, 1)

            stage_xn(0)
            dve.wait_ge(wqkv_landed, 96)
            dve.wait_ge(small_landed, 48)
            dve.tensor_scalar(w_qk[:, 256:384], w_qk[:, 256:384], g1_col[:, :], float(HD) ** -0.5,
                              ALU.mult, ALU.mult).then_inc(weights_scaled, 1)
            dve.tensor_scalar(w_qk[:, 384:416], w_qk[:, 384:416], g1_col[:, :], None, ALU.mult)\
               .then_inc(weights_scaled, 1)
            dve.tensor_scalar(w_v[:, DIM:V_COLS], w_v[:, DIM:V_COLS], g1_col[:, :], None, ALU.mult)\
               .then_inc(weights_scaled, 1)
            dve.tensor_scalar(neg_abs_g[:, :], g_col[:, :], -1.0, None, ALU.mult).then_inc(cos_shift_steps, 1)
            dve.wait_ge(cos_shift_steps, 1)
            dve.tensor_tensor(neg_abs_g[:, :], neg_abs_g[:, :], g_col[:, :], ALU.min).then_inc(cos_shift_steps, 1)
            dve.wait_ge(cos_shift_steps, 2)
            dve.tensor_scalar(cos_shift[:, :], neg_abs_g[:, :].to_broadcast([P, SEQ * GROUP // P]), COS_BOUND, 0.0,
                              ALU.add, ALU.min).then_inc(cos_shift_steps, 1)
            dve.wait_ge(xn_saved, 1)
            dve.wait_ge(xt_in_psum, 1)
            stage_xn(1)
            with dve.Fori(0, CHUNKS // 2) as c:
                project_chunk(c, ahead=True)
            for n, (kind, a, piece) in enumerate(FIRST[:4]):
                if n == 2:
                    project_chunk(CHUNKS - 2, ahead=False)
                empty_slot(0, n, kind, a, piece, 0)
            project_chunk(CHUNKS - 1, ahead=False)
            for n, (kind, a, piece) in list(enumerate(FIRST))[4:]:
                empty_slot(0, n, kind, a, piece, 0)
            with dve.Fori(0, ITERS) as it:
                base = it * JOBS
                b, g = it // GROUPS, it % GROUPS
                last_b, last_g = ((it + (ITERS - 1)) % ITERS) // GROUPS, ((it + (ITERS - 1)) % ITERS) % GROUPS
                for n, (kind, a, piece) in enumerate(COS_JOBS):
                    if kind == "out_causal":
                        normalise(base, FIRST_JOBS + n, it * 4 + 1, att_causal,
                                  last_b * SEQ_TILES + a * CT, last_g)
                    else:
                        empty_slot(base, FIRST_JOBS + n, kind, a, piece, it + 1 if kind in OF_NEXT else it)
                    if kind == "max" and piece == MAXIMA[a][-1]:
                        dve.wait_ge(aux_read, base + (FIRST_JOBS + n + 1 + 2))
                        dve.tensor_tensor(neg_max[:, 2 * a:2 * a + 2, :], neg_piece[:, 2 * a:2 * a + 2, :, 0],
                                          neg_piece[:, 2 * a:2 * a + 2, :, 1], ALU.min).then_inc(neg_max_ready, 1)
                        whole = neg_max[:, 2 * a:2 * a + 2, :].rearrange("p h t -> p (h t)")
                        high, low = neg_max_parts[:, a, 0, :], neg_max_parts[:, a, 1, :]
                        dve.wait_ge(neg_max_ready, it * 6 + (3 * a + 1))
                        dve.tensor_copy(high, whole).then_inc(neg_max_ready, 1)
                        dve.wait_ge(neg_max_ready, it * 6 + (3 * a + 2))
                        dve.tensor_tensor(low, whole, high, ALU.subtract).then_inc(neg_max_ready, 1)
                done = 0
                for i in range(len(CAUSAL_STEPS)):
                    if i in (2, 4):
                        copy_acc(0, i // 2 - 1, it)
                    elif i == 18:
                        copy_acc(1, 0, it)
                    for n in range(done, CAUSAL_ISSUED[i]):
                        kind, a, piece = CAUSAL_JOBS[n]
                        index = FIRST_JOBS + len(COS_JOBS) + n
                        if kind == "out_cos":
                            dve.wait_ge(ffn_in_done["cos_added"], it + 1)
                            normalise(base, index, it * 4 + (a + 2), att_cos, a * CT, 0)
                        elif kind == "out_causal":
                            normalise(base, index, it * 4 + 4, att_causal, b * SEQ_TILES, g)
                        else:
                            empty_slot(base, index, kind, a, piece, it + 1)
                    done = CAUSAL_ISSUED[i]
                    if i < ZEROED_STEPS:
                        zero_masked(it, i)
                copy_acc(1, 1, it)

            def add_attention(c):
                chunk = slice(c * CHUNK, (c + 1) * CHUNK)
                dve.wait_ge(ffn_in_done["projected"], c + 1)
                dve.tensor_tensor(xn[:, chunk], xn[:, chunk], ps[:, 2 + c % 2, :], ALU.add)\
                   .then_inc(ffn_in_done["residual"], 1)

            def sum_squares(c):
                dve.wait_ge(ffn_in_done["squares"], c + 1)
                dve.tensor_reduce(sum_sq[:, c * CT:(c + 1) * CT], f_stage[c % 2].rearrange("p (t d) -> p t d", t=CT),
                                  AX.X, ALU.add).then_inc(ffn_in_done["squares_summed"], 1)

            add_attention(0)
            add_attention(1)
            normalise(ITERS * JOBS, FIRST_JOBS, ITERS * 4 + 1, att_causal, (BATCH - 1) * SEQ_TILES + CT, GROUPS - 1)
            sum_squares(0)
            add_attention(2)
            sum_squares(1)
            add_attention(3)
            sum_squares(2)
            sum_squares(3)
            dve.wait_ge(ffn_in_done["squares_summed"], CHUNKS)
            dve.tensor_scalar(sum_sq[:, :], sum_sq[:, :], 1.0 / DIM, RMS_EPS, ALU.mult, ALU.add)\
               .then_inc(gating_done["mean_squares"], 1)
            dve.wait_ge(gating_done["rms"], 1)
            dve.reciprocal(s_var[:, :], sum_sq[:, :]).then_inc(gating_done["rms_inverse"], 1)
            dve.wait_ge(gating_done["rms_inverse"], 1)

            for c in range(CHUNKS):
                if c >= 2:
                    dve.wait_ge(gating_done["transposed"], c - 1)
                dve.tensor_tensor(f_stage[c % 2].rearrange("p (t d) -> p t d", t=CT),
                                  xn[:, c * CHUNK:(c + 1) * CHUNK].rearrange("p (t d) -> p t d", t=CT),
                                  s_var[:, c * CT:(c + 1) * CT].unsqueeze(2).to_broadcast([P, CT, DIM]), ALU.mult)\
                   .then_inc(gating_done["normalised"], 1)
            dve.wait_ge(gating_done["logits_transposed"], 1)
            logits_ps = ps[:, 6, :].rearrange("p (t c n) -> p c t n", t=CT, c=CHUNKS)[:, :, :, 0:EXPERTS]

            steps2 = [0]

            def link2(ins):
                steps2[0] += 1
                ins.then_inc(gating_done["weight_steps"], 1)
                dve.wait_ge(gating_done["weight_steps"], steps2[0])

            g_max = g_cmp[:, 0, :]
            by_chunk = "p (c t) -> p c t"
            link2(dve.tensor_reduce(g_max.rearrange(by_chunk, c=CHUNKS), logits_ps, AX.X, ALU.max))
            link2(dve.tensor_tensor(logits[:, :, :].rearrange("p (c t) e -> p c t e", c=CHUNKS), logits_ps,
                                    g_max.rearrange(by_chunk, c=CHUNKS).unsqueeze(3)
                                    .to_broadcast([P, CHUNKS, CT, EXPERTS]), ALU.subtract))
            link2(dve.memset(g_rank[:, :, :], 0.0))

            pairs = [(i, j) for i in range(EXPERTS) for j in range(i + 1, EXPERTS)]

            def compare():
                dve.wait_ge(gating_done["logit_exps"], 1)
                for n, (i, j) in enumerate(pairs):
                    ins = dve.tensor_tensor(g_cmp[:, n, :], g_exp[:, :, i], g_exp[:, :, j], ALU.is_ge)
                link2(ins)

            def rank(first, last):
                for n, (i, j) in list(enumerate(pairs))[first:last]:
                    link2(dve.tensor_tensor(g_rank[:, :, j], g_rank[:, :, j], g_cmp[:, n, :], ALU.add))
                    link2(dve.tensor_tensor(g_rank[:, :, i], g_rank[:, :, i], g_cmp[:, n, :], ALU.subtract))

            def weigh():
                for i in range(EXPERTS):
                    ins = dve.tensor_scalar(g_rank[:, :, i], g_rank[:, :, i], float(EXPERTS - 1 - i), 2.0,
                                            ALU.add, ALU.is_lt)
                link2(ins)
                link2(dve.tensor_tensor(g_exp[:, :, :], g_exp[:, :, :], g_rank[:, :, :], ALU.mult))
                link2(dve.tensor_reduce(g_max, g_exp[:, :, :], AX.X, ALU.add))
                link2(dve.reciprocal(g_max, g_max))
                link2(dve.tensor_tensor(comb[:, :].rearrange("p (t e) -> p t e", t=TILES), g_exp[:, :, :],
                                        g_max.unsqueeze(2).to_broadcast([P, TILES, EXPERTS]), ALU.mult))

            def weight_part(k):
                if k == 0:
                    compare()
                elif k <= 3:
                    rank(2 * k - 2, 2 * k)
                elif k == 4:
                    weigh()

            dve.wait_ge(ffn_in_done["all_added"], CHUNKS)

            def chunk_experts(c, first):
                def add_expert(e):
                    dve.wait_ge(experts_done["down_products"], c * EXPERTS + (e + 3))
                    if e:
                        dve.wait_ge(experts_done["outputs_summed"], c * EXPERTS + (e + 2))
                    for t in range(CT):
                        acc_t = x_tok[:, ds(c * CHUNK + t * DIM, DIM)]
                        ins = dve.scalar_tensor_tensor(
                            out=acc_t, in0=ps[:, 4 + e % 2, t * DIM:(t + 1) * DIM],
                            scalar=comb[:, ds(c * (CT * EXPERTS) + (t * EXPERTS + e), 1)], in1=acc_t,
                            op0=ALU.mult, op1=ALU.add)
                    ins.then_inc(experts_done["outputs_summed"], 1)

                for e in range(EXPERTS):
                    for h in range(HT):
                        k = e * HT + h
                        dve.wait_ge(experts_done["silus"], c * (EXPERTS * HT) + (k + 1))
                        if h == 0:
                            dve.wait_ge(experts_done["down_products"], c * EXPERTS + (e + 1))
                        dve.tensor_tensor(hidden[e % 2][:, h, :], gated[k % 2], ps[:, 2 + k % 2, :], ALU.mult)\
                           .then_inc(experts_done["hidden"], 1)
                        if first:
                            weight_part(k)
                    if e:
                        add_expert(e - 1)
                add_expert(EXPERTS - 1)

            chunk_experts(0, first=True)
            with dve.Fori(1, CHUNKS) as c:
                chunk_experts(c, first=False)

        @block.tensor
        def _(pe):
            pe.wait_ge(constants_made, 10)

            def transpose_xn(c):
                pe.wait_ge(xn_staged, CT * c + CT)
                for t in range(CT):
                    ins = pe.transpose(ps[:, 6, t * P:(t + 1) * P], xn_stage[:, t * DIM:(t + 1) * DIM], ident[:, :])
                ins.then_inc(xt_in_psum, 1)

            def project_chunk(c):
                pe.wait_ge(xt_ready, c + 1)
                pe.wait_ge(projections_read, c + 1)
                for t in range(CT):
                    pe.matmul(ps[:, t, 0:QK_COLS + ROPE_COLS], xn_t[:, t * P:(t + 1) * P], w_qk[:, :],
                              start=True, stop=True)
                for t in range(CT):
                    v_out = ps[:, 4 + t // 2, (t % 2) * V_COLS:(t % 2 + 1) * V_COLS]
                    ins = pe.matmul(v_out, xn_t[:, t * P:(t + 1) * P], w_v[:, :], start=True, stop=True)
                ins.then_inc(projected, 1)

            def aux_job(base, index, kind, a, b, batch, group, parity=0):
                k = index % 2
                pe.wait_ge(aux_read, base + (index + 1))
                if kind in ("cos", "query", "key"):
                    if kind == "cos":
                        flat, heads, first, step = parts_cos, QK_HEADS, a * HEADS, GROUP
                    elif kind == "query":
                        flat, heads, first, step = parts_rope, ROPE_HEADS, 0, GROUP
                    else:
                        flat, heads, first, step = parts_rope, ROPE_HEADS, HEADS, 1
                    for t in range(SEQ_TILES):
                        src = flat[:, ds(batch * (SEQ_TILES * heads * HEAD_COLS) + group * (step * HEAD_COLS)
                                         + (t * heads + first) * HEAD_COLS, P)]
                        ins = pe.transpose(aux_b[k][:, t * P:(t + 1) * P], src, ident_b[:, :])
                elif kind == "neg_max":
                    ins = pe.transpose(aux_b[k][0:2 * 2 * SEQ_TILES, 0:P],
                                       neg_max_parts[:, a, :, :].rearrange("p s n -> p (s n)"), ident_b[:, :])
                elif kind == "max":
                    t, piece, width, h, heads = b
                    for i in range(heads):
                        ins = pe.matmul(aux[k][:, i * width:(i + 1) * width],
                                        q_causal_t[parity][0:BIAS_ROW, h + i, t * P:(t + 1) * P],
                                        k_causal_t[parity][0:BIAS_ROW, piece * BANK:piece * BANK + width],
                                        start=i == 0, stop=True, skip_group_check=True)
                        if piece == t // 4:
                            ins = pe.matmul(aux[k][:, (i + 1) * width - P:(i + 1) * width], ident_b[:, :], mask_q[:, :],
                                            start=False, stop=True, skip_group_check=True)
                else:
                    which = int(kind == "out_causal")
                    for t in range(CT):
                        lo = (a * CT + t) * P
                        ins = pe.transpose(aux[k][:, t * P:(t + 1) * P], out_t[:, which, lo:lo + P], ident[:, :])
                ins.then_inc(aux_filled, 1)

            def scores(n, j, h, heads, causal, parity):
                s = slot(n)
                for i in range(heads):
                    if causal:
                        width = SEQ - j * P
                        keys, queries = k_causal_t[parity][:, j * P:(j + 1) * P], q_causal_t[parity][:, h + i, :]
                        place = j * P if heads == 1 else (i * BANK if heads == 2 else i * width)
                    else:
                        width, place = SEQ, 0
                        keys, queries = k_cos_t[:, h, j * P:(j + 1) * P], q_cos_t[:, h, :]
                    done = 0
                    while done < width:
                        at = place + done
                        n_cols = min(width - done, BANK - at % BANK)
                        q0 = SEQ - width + done
                        first = at % BANK == 0 or i == 0 or heads == 2
                        ins = pe.matmul(s[:, at:at + n_cols], keys, queries[:, q0:q0 + n_cols], start=first,
                                        stop=True, skip_group_check=True)
                        if causal and done == 0 and j >= ZEROED_TILES:
                            ins = pe.matmul(s[:, at:at + P], ident_b[:, :], mask_k[:, :], start=False, stop=True,
                                            skip_group_check=True)
                        done += n_cols
                ins.then_inc(scores_ready, 1)

            def values(j, half, causal):
                lo, hi = max(half * BANK, j * P if causal else 0), (half + 1) * BANK
                at = lo - half * BANK
                for h in range(GROUP):
                    v = v_causal_pad[:, j, :] if causal else v_cos_pad[:, j, h, :]
                    ins = pe.matmul(acc[32 * h:32 * h + 32, half, at:at + hi - lo], v, probs[:, j % 2, h, lo:hi],
                                    start=(j == 0 and at == 0), stop=True, skip_group_check=True)
                return ins

            def score_step(n, it_first, exps, cos_laid, parity):
                causal = len(COS_STEPS) <= n < STEPS
                j, h, heads = (COS_STEPS + CAUSAL_STEPS)[n % STEPS]
                if j == h == 0 and not causal:
                    pe.wait_ge(laid["q_cos"], it_first * LAID["q_cos"] + cos_laid * LAID["q_cos"])
                    pe.wait_ge(laid["k_cos"], it_first * LAID["k_cos"] + cos_laid * LAID["k_cos"])
                if j == 0 and causal and h in (0, 2):
                    name = f"neg_max{h // 2}"
                    pe.wait_ge(laid[name], it_first * LAID[name] + 2 * LAID[name])
                pe.wait_ge(probs_ready, exps)
                scores(n, j, h, heads, causal, parity)

            def wait_causal_laid(count):
                for name in ("key", "query"):
                    pe.wait_ge(laid[name], count * LAID[name])

            transpose_xn(0)
            pe.wait_ge(weights_scaled, 3)
            with pe.Fori(0, CHUNKS // 2) as c:
                project_chunk(c)
                transpose_xn(c + 1)
            for c in range(CHUNKS // 2, CHUNKS):
                project_chunk(c)
                if c == CHUNKS // 2:
                    pe.wait_ge(high_parts_again, 2 * c)
                    pe.wait_ge(low_parts, 2 * c + LO_CREDIT)
                    aux_job(0, 0, *FIRST[0], 0, 0)
                    aux_job(0, 1, *FIRST[1], 0, 0)
                    pe.wait_ge(aux_read, 3)
                    transpose_xn(c + 1)
            aux_job(0, 2, *FIRST[2], 0, 0)
            aux_job(0, 3, *FIRST[3], 0, 0)
            pe.wait_ge(buffers_cleared, 11)
            pe.wait_ge(cos_bias_rows_laid, 32)
            pe.wait_ge(high_parts_again, 2 * CHUNKS)
            pe.wait_ge(low_parts, 2 * CHUNKS + LO_CREDIT)
            for n in range(2):
                score_step(n, 0, n + 1, 2, 0)
            wait_causal_laid(2)
            for n, (kind, a, piece) in list(enumerate(FIRST))[4:]:
                aux_job(0, n, kind, a, piece, 0, 0)

            def iteration(it, parity):
                batch, group = it // GROUPS, it % GROUPS
                next_batch, next_group = ((it + 1) % ITERS) // GROUPS, ((it + 1) % ITERS) % GROUPS
                base = it * JOBS

                def next_job(n):
                    kind, a, b = ALL_JOBS[n]
                    if kind == "out_causal":
                        pe.wait_ge(acc_halves_copied, it * 4 + (2 if a else 5))
                    elif kind == "out_cos":
                        pe.wait_ge(acc_halves_copied, it * 4 + (a + 3))
                    elif kind == "max" and b == FIRST_PAIR[0][2]:
                        wait_causal_laid(it + 3)
                    elif kind == "neg_max":
                        pe.wait_ge(neg_max_ready, it * 6 + (3 * a + 3))
                    of_next = kind in OF_NEXT or n >= len(COS_JOBS) and kind == "max"
                    if of_next:
                        aux_job(base, FIRST_JOBS + n, kind, a, b, next_batch, next_group, 1 - parity)
                    else:
                        aux_job(base, FIRST_JOBS + n, kind, a, b, batch, group, parity)

                def value_half(j, half, causal, steps_done):
                    first = half == (j // CT if causal else 0)
                    if first:
                        pe.wait_ge(probs_ready, it * STEPS + (steps_done + 2))
                    if first and j == 0:
                        pe.wait_ge(v_causal_padded if causal else v_cos_padded, it + 1)
                    if first and causal and j < ZEROED_TILES:
                        pe.wait_ge(masked_probs_zeroed, it * ZEROED_STEPS + (steps_done - len(COS_STEPS)))
                    if j == 0:
                        pe.wait_ge(acc_halves_copied, it * 4 + (1 + 2 * causal + half))
                    ins = values(j, half, causal)
                    if half == 1:
                        ins.then_inc(key_tiles_used, 1)
                    if (j, half) == (SEQ_TILES // 2 - 1 if causal else SEQ_TILES - 1, 0):
                        ins.then_inc(first_half_done, 1)

                plan = COS_ISSUED + [len(COS_JOBS) + i for i in CAUSAL_ISSUED] + [JOBS, JOBS]
                tile_of = [step[0] for step in COS_STEPS] + [SEQ_TILES + step[0] for step in CAUSAL_STEPS]
                tile_of += [2 * SEQ_TILES] * 2
                pending, issued = [], 0
                for n in range(2, STEPS + 2):
                    jobs = plan[n] - issued
                    left = tile_of[n:].count(tile_of[n])
                    one_a_step = tile_of.count(tile_of[n]) == len(pending)
                    halves = len(pending) if left == 1 else int(left % 2 == 1 or one_a_step)
                    if jobs >= 2 and not halves:
                        next_job(issued)
                        issued, jobs = issued + 1, jobs - 1
                    score_step(n, it, it * STEPS + (n + 1), 3, parity)
                    for i in range(max(jobs, halves)):
                        if i < jobs:
                            next_job(issued)
                            issued += 1
                        if i < halves:
                            value_half(*pending.pop(0))
                    if left == 1:
                        causal = n >= len(COS_STEPS)
                        j = tile_of[n] % SEQ_TILES
                        pending = [(j, half, causal, n + 1) for half in range(j // CT if causal else 0, 2)]

            def transpose_attention(c):
                if c >= 2:
                    pe.wait_ge(ffn_in_done["copied"], c - 1)
                for t in range(CT):
                    ins = pe.transpose(ps[:, c % 2, t * P:(t + 1) * P], att_causal[:, c * CT + t, :], ident[:, :])
                ins.then_inc(ffn_in_done["transposed"], 1)

            def project_out(c):
                pe.wait_ge(ffn_in_done["copied"], c + 1)
                if c >= 2:
                    pe.wait_ge(ffn_in_done["residual"], c - 1)
                for t in range(CT):
                    ins = pe.matmul(ps[:, 2 + c % 2, t * DIM:(t + 1) * DIM], att_t[c % 2][:, t * P:(t + 1) * P],
                                    w_o[:, :], start=True, stop=True)
                ins.then_inc(ffn_in_done["projected"], 1)

            with pe.Fori(0, ITERS // 2) as pair:
                for parity in range(2):
                    iteration(pair * 2 + parity, parity)

            pe.wait_ge(rest_landed, 80)
            pe.wait_ge(probs_ready, ITERS * STEPS + 2)
            transpose_attention(0)
            transpose_attention(1)
            project_out(0)
            project_out(1)
            pe.wait_ge(aux_read, ITERS * JOBS + (FIRST_JOBS + 2))
            transpose_attention(2)
            pe.wait_ge(acc_halves_copied, ITERS * 4 + 2)
            aux_job(ITERS * JOBS, FIRST_JOBS, "out_causal", 1, 0, 0, 0)
            project_out(2)
            pe.wait_ge(aux_read, ITERS * JOBS + (FIRST_JOBS + 1 + 2))
            transpose_attention(3)
            project_out(3)

            def up(k, count, tokens):
                e, h = divmod(k, HT)
                pe.wait_ge(experts_done["hidden"], count + 1)
                pe.matmul(ps[:, k % 2, :], w_1[:, e, h * P:(h + 1) * P], tokens, start=True, stop=True)
                pe.matmul(ps[:, 2 + k % 2, :], w_3[:, e, h * P:(h + 1) * P], tokens, start=True, stop=True)\
                  .then_inc(experts_done["up_products"], 1)

            def gate(c):
                pe.wait_ge(gating_done["copied"], c + 1)
                pe.matmul(ps[32 * c:32 * c + 32, 7, :], w_gate[:, :], xf_t[:, c * CHUNK:(c + 1) * CHUNK],
                          start=True, stop=True, skip_group_check=True).then_inc(gating_done["products"], 1)

            pe.wait_ge(ffn_in_done["residual"], CHUNKS)
            for c in range(CHUNKS):
                pe.wait_ge(gating_done["normalised"], c + 1)
                if c >= 2:
                    pe.wait_ge(gating_done["copied"], c - 1)
                for t in range(CT):
                    ins = pe.transpose(ps[:, 4 + c % 2, t * P:(t + 1) * P], f_stage[c % 2][:, t * DIM:(t + 1) * DIM],
                                       ident[:, :])
                ins.then_inc(gating_done["transposed"], 1)
                if c:
                    gate(c - 1)
            gate(CHUNKS - 1)
            up(0, 0, xf_t[:, 0:CHUNK])
            pe.wait_ge(gating_done["logits_copied"], 1)
            for t in range(CT):
                ins = pe.transpose(ps[:, 6, t * P:(t + 1) * P], att_t[0][:, t * P:(t + 1) * P], ident[:, :])
            ins.then_inc(gating_done["logits_transposed"], 1)

            with pe.Fori(0, CHUNKS) as c:
                def down(e):
                    pe.wait_ge(experts_done["hidden"], c * (EXPERTS * HT) + ((e + 1) * HT + 2))
                    pe.wait_ge(experts_done["outputs_summed"], c * EXPERTS + (e + 1))
                    for t in range(CT):
                        for h in range(HT):
                            ins = pe.matmul(ps[:, 4 + e % 2, t * DIM:(t + 1) * DIM],
                                            hidden[e % 2][:, h, t * P:(t + 1) * P], w_2[:, e * HT + h, :],
                                            start=h == 0, stop=h == HT - 1)
                    ins.then_inc(experts_done["down_products"], 1)

                tokens = xf_t[:, ds(c * CHUNK, CHUNK)]
                for k in range(1, EXPERTS * HT):
                    up(k, c * (EXPERTS * HT) + k, tokens)
                    if k % HT == 0:
                        down(k // HT - 1)
                up(0, c * (EXPERTS * HT) + EXPERTS * HT, xf_t[:, ds(((c + 1) % CHUNKS) * CHUNK, CHUNK)])
                down(EXPERTS - 1)


def kernel(**inputs):
    import numpy as _np
    import concourse.bacc as _bacc
    from concourse import mybir as _mybir
    from concourse.bass_utils import run_bass_kernel_spmd as _run

    inv_freq = _np.float32(1.0) / _np.float32(10000.0) ** (_np.arange(0, HD, 2, dtype=_np.float32) / _np.float32(HD))
    freqs = _np.arange(SEQ, dtype=_np.float32)[:, None] * inv_freq.astype(_np.float32)[None, :]
    angles = _np.concatenate([freqs, freqs], axis=-1)
    sign = _np.where(_np.arange(HD) < HD // 2, -1.0, 1.0)

    def tiled(table):
        table = table.astype(_np.float32).reshape(SEQ_TILES, P, HD)
        return _np.ascontiguousarray(table.transpose(1, 0, 2).reshape(P, SEQ_TILES * HD))

    given = {name.replace("L0_", ""): _np.asarray(a) for name, a in inputs.items()}
    arrays = {
        "x": given["attn_x"], "wq_cos": given["attn_Wq"].T, "wk_cos": given["attn_Wk"].T, "wv_cos": given["attn_Wv"].T,
        "g_scale": _np.broadcast_to(given["attn_g_scale"].reshape(1, 1), (P, 1)),
        "g1": given["ffn_g1"].reshape(P, 1), "g2": given["ffn_g2"].reshape(P, 1),
        "wq": given["ffn_wq"], "wk": given["ffn_wk"], "wv": given["ffn_wv"], "wo": given["ffn_wo"],
        "gate": given["ffn_gate"], "w1": given["ffn_w1"], "w2": given["ffn_w2"], "w3": given["ffn_w3"],
        "cos_table": tiled(_np.cos(angles)), "sin_table": tiled(_np.sin(angles) * sign),
    }
    nc = _bacc.Bacc("TRN2", target_bir_lowering=False, num_devices=1)
    feeds, aps = {}, {}
    for name, a in arrays.items():
        feeds[f"in_{name}"] = _np.ascontiguousarray(a)
        aps[name] = nc.dram_tensor(f"in_{name}", a.shape, _mybir.dt.float32, kind="ExternalInput").ap()
    result = nc.dram_tensor("out_dram", (BATCH, SEQ, DIM), _mybir.dt.float32, kind="ExternalOutput").ap()
    build(nc, out=result, **aps)
    return _run(nc, [feeds], core_ids=[0]).results[0]["out_dram"]
```
